# Optimizing a Trainium2 kernel written in Bass

```python
import numpy as np
import jax
import jax.numpy as jnp

def _softmax(x, axis=-1):
    return jax.nn.softmax(x, axis=axis)

def _gelu(x):
    return jax.nn.gelu(x, approximate=True)

def _silu(x):
    return jax.nn.silu(x)

def _sigmoid(x):
    return jax.nn.sigmoid(x)

def _layernorm(x, axis=-1, eps=1e-05):
    m = jnp.mean(x, axis=axis, keepdims=True)
    v = jnp.var(x, axis=axis, keepdims=True)
    return (x - m) / jnp.sqrt(v + eps)

def _scatter_add(tgt, idx, src, axis=0):
    return tgt.at[idx].add(src)

def _segment_sum(src, seg, n):
    return jax.ops.segment_sum(src, seg, n)
kernel_name = 'mk_conv_attn_hybrid_d2_conv_nhwc128_r4_942bb1'

def setup_inputs(seed: int=0):
    np.random.seed(seed)
    _w = jnp.asarray

    def _rec_inputs():
        import jax
        import jax.numpy as jnp
        _gk = jax.random.key(seed)
        x = -0.0002091 + 1 * jax.random.normal(jax.random.fold_in(_gk, 1), (16, 56, 56, 32), jnp.float32)
        return x
    x = _rec_inputs()

    def _L0_conv_setup():
        import jax, jax.numpy as jnp
        import numpy as np
        WS = 7
        SHIFT = 3
        NH = 4

        def _rel_index(ws: int) -> np.ndarray:
            coords = np.stack(np.meshgrid(np.arange(ws), np.arange(ws), indexing='ij'), -1).reshape(-1, 2)
            d = coords[:, None, :] - coords[None, :, :]
            idx = (d[..., 0] + ws - 1) * (2 * ws - 1) + d[..., 1] + ws - 1
            return idx.reshape(-1).astype(np.int32)

        def _ln(x, g, b, eps=1e-05):
            m = x.mean(-1, keepdims=True)
            v = ((x - m) ** 2).mean(-1, keepdims=True)
            return (x - m) / jnp.sqrt(v + eps) * g + b
        key = jax.random.key(seed)
        ks = jax.random.split(key, 14)
        B, H, W, C = (16, 56, 56, 32)
        hidden = int(C * 4.0)
        s = 0.02
        return {'x': jax.random.normal(ks[0], (B, H, W, C), jnp.float32), 'norm1_g': jnp.ones((C,), jnp.float32), 'norm1_b': jnp.zeros((C,), jnp.float32), 'qkv_w': jax.random.normal(ks[1], (3 * C, C), jnp.float32) * s, 'qkv_b': jnp.zeros((3 * C,), jnp.float32), 'out_w': jax.random.normal(ks[2], (C, C), jnp.float32) * s, 'out_b': jnp.zeros((C,), jnp.float32), 'pe_table': jax.random.normal(ks[3], (NH, (2 * WS - 1) ** 2), jnp.float32) * s, 'norm2_g': jnp.ones((C,), jnp.float32), 'norm2_b': jnp.zeros((C,), jnp.float32), 'mlp_w1': jax.random.normal(ks[4], (hidden, C), jnp.float32) * s, 'mlp_b1': jnp.zeros((hidden,), jnp.float32), 'mlp_w2': jax.random.normal(ks[5], (C, hidden), jnp.float32) * s, 'mlp_b2': jnp.zeros((C,), jnp.float32)}
    _L0_conv_all = _L0_conv_setup()
    _L0_conv_in = {k: v for k, v in _L0_conv_all.items() if k in ('norm1_g', 'norm1_b', 'qkv_w', 'qkv_b', 'out_w', 'out_b', 'pe_table', 'norm2_g', 'norm2_b', 'mlp_w1', 'mlp_b1', 'mlp_w2', 'mlp_b2')}
    del _L0_conv_all

    def _L1_attn_setup():
        import jax, jax.numpy as jnp
        import numpy as np
        B, S, D = (4, 1024, 32)
        key = jax.random.key(seed)
        ks = jax.random.split(key, 4)
        scale = 1.0 / np.sqrt(D)
        return {'x': jax.random.normal(ks[0], (B, S, D), dtype=jnp.float32), 'Wq': jax.random.normal(ks[1], (D, D), dtype=jnp.float32) * scale, 'bq': jnp.zeros((D,), dtype=jnp.float32), 'Wk': jax.random.normal(ks[2], (D, D), dtype=jnp.float32) * scale, 'bk': jnp.zeros((D,), dtype=jnp.float32), 'Wv': jax.random.normal(ks[3], (D, D), dtype=jnp.float32) * scale, 'bv': jnp.zeros((D,), dtype=jnp.float32)}
    _L1_attn_all = _L1_attn_setup()
    _L1_attn_in = {k: v for k, v in _L1_attn_all.items() if k in ('Wq', 'bq', 'Wk', 'bk', 'Wv', 'bv')}
    del _L1_attn_all

    def _L1_ffn_setup():
        import jax, jax.numpy as jnp
        import numpy as np
        B, S, D, E, H, O, K = (128, 512, 32, 16, 128, 32, 8)
        key = jax.random.key(seed)
        k0, k1, k2, k3 = jax.random.split(key, 4)
        x = jax.random.normal(k0, (B, S, D), dtype=jnp.float32)
        gate_w = jax.random.normal(k1, (E, D), dtype=jnp.float32) * (1.0 / np.sqrt(D))
        gate_b = jnp.zeros((E,), dtype=jnp.float32)
        weight1 = jax.random.uniform(k2, (E, D + 1, H), dtype=jnp.float32, minval=-1.0, maxval=1.0) * (1.0 / np.sqrt(D + 1))
        weight2 = jax.random.uniform(k3, (E, H + 1, O), dtype=jnp.float32, minval=-1.0, maxval=1.0) * (1.0 / np.sqrt(H + 1))
        return {'x': x, 'gate_w': gate_w, 'gate_b': gate_b, 'weight1': weight1, 'weight2': weight2}
    _L1_ffn_all = _L1_ffn_setup()
    _L1_ffn_in = {k: v for k, v in _L1_ffn_all.items() if k in ('gate_w', 'gate_b', 'weight1', 'weight2')}
    del _L1_ffn_all
    return {'x': x, 'L0_conv_norm1_g': _L0_conv_in['norm1_g'], 'L0_conv_norm1_b': _L0_conv_in['norm1_b'], 'L0_conv_qkv_w': _L0_conv_in['qkv_w'], 'L0_conv_qkv_b': _L0_conv_in['qkv_b'], 'L0_conv_out_w': _L0_conv_in['out_w'], 'L0_conv_out_b': _L0_conv_in['out_b'], 'L0_conv_pe_table': _L0_conv_in['pe_table'], 'L0_conv_norm2_g': _L0_conv_in['norm2_g'], 'L0_conv_norm2_b': _L0_conv_in['norm2_b'], 'L0_conv_mlp_w1': _L0_conv_in['mlp_w1'], 'L0_conv_mlp_b1': _L0_conv_in['mlp_b1'], 'L0_conv_mlp_w2': _L0_conv_in['mlp_w2'], 'L0_conv_mlp_b2': _L0_conv_in['mlp_b2'], 'L1_attn_Wq': _L1_attn_in['Wq'], 'L1_attn_bq': _L1_attn_in['bq'], 'L1_attn_Wk': _L1_attn_in['Wk'], 'L1_attn_bk': _L1_attn_in['bk'], 'L1_attn_Wv': _L1_attn_in['Wv'], 'L1_attn_bv': _L1_attn_in['bv'], 'L1_ffn_gate_w': _L1_ffn_in['gate_w'], 'L1_ffn_gate_b': _L1_ffn_in['gate_b'], 'L1_ffn_weight1': _L1_ffn_in['weight1'], 'L1_ffn_weight2': _L1_ffn_in['weight2']}

def reference(x, L0_conv_norm1_g, L0_conv_norm1_b, L0_conv_qkv_w, L0_conv_qkv_b, L0_conv_out_w, L0_conv_out_b, L0_conv_pe_table, L0_conv_norm2_g, L0_conv_norm2_b, L0_conv_mlp_w1, L0_conv_mlp_b1, L0_conv_mlp_w2, L0_conv_mlp_b2, L1_attn_Wq, L1_attn_bq, L1_attn_Wk, L1_attn_bk, L1_attn_Wv, L1_attn_bv, L1_ffn_gate_w, L1_ffn_gate_b, L1_ffn_weight1, L1_ffn_weight2):
    import jax
    import jax.numpy as jnp

    def _L0_conv_ref(x, norm1_g, norm1_b, qkv_w, qkv_b, out_w, out_b, pe_table, norm2_g, norm2_b, mlp_w1, mlp_b1, mlp_w2, mlp_b2):
        import jax, jax.numpy as jnp
        import numpy as np
        WS = 7
        SHIFT = 3
        NH = 4

        def _rel_index(ws: int) -> np.ndarray:
            coords = np.stack(np.meshgrid(np.arange(ws), np.arange(ws), indexing='ij'), -1).reshape(-1, 2)
            d = coords[:, None, :] - coords[None, :, :]
            idx = (d[..., 0] + ws - 1) * (2 * ws - 1) + d[..., 1] + ws - 1
            return idx.reshape(-1).astype(np.int32)

        def _ln(x, g, b, eps=1e-05):
            m = x.mean(-1, keepdims=True)
            v = ((x - m) ** 2).mean(-1, keepdims=True)
            return (x - m) / jnp.sqrt(v + eps) * g + b
        B, H, W, C = x.shape
        nH, nW = (H // WS, W // WS)
        L = WS * WS
        hd = C // NH
        h = _ln(x, norm1_g, norm1_b)
        h = jnp.roll(h, (SHIFT, SHIFT), (1, 2))
        h = h.reshape(B, nH, WS, nW, WS, C).transpose(0, 1, 3, 2, 4, 5).reshape(B * nH * nW, L, C)
        qkv = h @ qkv_w.T + qkv_b
        q, k, v = jnp.split(qkv, 3, axis=-1)
        to_heads = lambda t: t.reshape(-1, L, NH, hd).transpose(0, 2, 1, 3)
        q, k, v = (to_heads(q), to_heads(k), to_heads(v))
        idx = jnp.asarray(_rel_index(WS))
        bias = pe_table[:, idx].reshape(NH, L, L)
        scores = jnp.einsum('nhqd,nhkd->nhqk', q, k) / jnp.sqrt(jnp.float32(hd)) + bias[None]
        attn = jax.nn.softmax(scores, axis=-1)
        o = jnp.einsum('nhqk,nhkd->nhqd', attn, v).transpose(0, 2, 1, 3).reshape(-1, L, C)
        o = o @ out_w.T + out_b
        o = o.reshape(B, nH, nW, WS, WS, C).transpose(0, 1, 3, 2, 4, 5).reshape(B, H, W, C)
        h2 = _ln(o, norm2_g, norm2_b)
        y = jax.nn.gelu(h2 @ mlp_w1.T + mlp_b1, approximate=False) @ mlp_w2.T + mlp_b2
        return y

    def _L1_attn_ref(x, Wq, bq, Wk, bk, Wv, bv):
        import jax, jax.numpy as jnp
        import numpy as np
        B, S, D = (4, 1024, 32)
        q = jnp.einsum('bsd,de->bse', x, Wq) + bq
        k = jnp.einsum('bsd,de->bse', x, Wk) + bk
        v = jnp.einsum('bsd,de->bse', x, Wv) + bv
        d = x.shape[-1]
        scores = jnp.einsum('bqd,bkd->bqk', q, k) / jnp.sqrt(jnp.asarray(d, x.dtype))
        attn = jax.nn.softmax(scores, axis=-1)
        out = jnp.einsum('bqk,bkd->bqd', attn, v)
        return out + x

    def _L1_ffn_ref(x, gate_w, gate_b, weight1, weight2):
        import jax, jax.numpy as jnp
        import numpy as np
        B, S, D, E, H, O, K = (128, 512, 32, 16, 128, 32, 8)
        Bn, Sn, Dn = x.shape
        logits = jnp.einsum('bsd,ed->bse', x, gate_w) + gate_b
        probs = jax.nn.softmax(logits, axis=1)
        vals, idx = jax.lax.top_k(probs.transpose(0, 2, 1), K)
        topv = vals.transpose(0, 2, 1)
        topi = idx.transpose(0, 2, 1)
        flat_idx = topi.reshape(Bn, K * E)
        gathered = jnp.take_along_axis(x, flat_idx[:, :, None], axis=1)
        gathered = gathered.reshape(Bn, K, E, Dn)
        pooled = jnp.einsum('bked,bke->bed', gathered, topv)
        ones = jnp.ones((E, Bn, 1), dtype=x.dtype)
        h = jnp.concatenate([pooled.transpose(1, 0, 2), ones], axis=-1)
        h = jax.nn.gelu(jnp.einsum('ebd,edh->ebh', h, weight1), approximate=False)
        h = jnp.concatenate([h, ones], axis=-1)
        out = jnp.einsum('ebh,eho->ebo', h, weight2)
        out = out.transpose(1, 0, 2)
        weighted = jnp.einsum('beo,bke->bkeo', out, topv).reshape(Bn, K * E, O)
        outputs = jnp.zeros((Bn, Sn, O), dtype=x.dtype)
        outputs = outputs.at[jnp.arange(Bn)[:, None], flat_idx].add(weighted)
        return outputs

    def _gn(v, G=32, eps=1e-05):
        B_, H_, W_, C_ = v.shape
        g = v.reshape(B_, H_, W_, G, C_ // G)
        m = jnp.mean(g, axis=(1, 2, 4), keepdims=True)
        s = jnp.var(g, axis=(1, 2, 4), keepdims=True)
        return ((g - m) / jnp.sqrt(s + eps)).reshape(v.shape)

    def _ln_c(v, eps=1e-06):
        m = jnp.mean(v, axis=-1, keepdims=True)
        s = jnp.var(v, axis=-1, keepdims=True)
        return (v - m) / jnp.sqrt(s + eps)

    def _ln_t(v, eps=1e-05):
        m = jnp.mean(v, axis=-1, keepdims=True)
        s = jnp.var(v, axis=-1, keepdims=True)
        return (v - m) / jnp.sqrt(s + eps)

    def _to_tokens(v):
        B_, H_, W_, C_ = v.shape
        return v.reshape(B_, H_ * W_, C_)

    def _from_tokens(t, like):
        return t.reshape(like.shape)
    x = x + _L0_conv_ref(_gn(x), L0_conv_norm1_g, L0_conv_norm1_b, L0_conv_qkv_w, L0_conv_qkv_b, L0_conv_out_w, L0_conv_out_b, L0_conv_pe_table, L0_conv_norm2_g, L0_conv_norm2_b, L0_conv_mlp_w1, L0_conv_mlp_b1, L0_conv_mlp_w2, L0_conv_mlp_b2)
    t = _to_tokens(x)
    t = t + _L1_attn_ref(_ln_t(t), L1_attn_Wq, L1_attn_bq, L1_attn_Wk, L1_attn_bk, L1_attn_Wv, L1_attn_bv)
    t = t + _L1_ffn_ref(_ln_t(t), L1_ffn_gate_w, L1_ffn_gate_b, L1_ffn_weight1, L1_ffn_weight2)
    x = _from_tokens(t, x)
    return x

_drawn_inputs = setup_inputs


def setup_inputs(seed=0):
    import zlib

    import numpy as np

    out = dict(_drawn_inputs(seed))
    spreads = {'L0_conv_norm1_g': (1.0, 0.6),
     'L0_conv_norm1_b': (0.0, 0.8),
     'L0_conv_qkv_b': (0.0, 0.8),
     'L0_conv_out_b': (0.0, 0.457),
     'L0_conv_norm2_g': (1.0, 0.6),
     'L0_conv_norm2_b': (0.0, 0.8),
     'L0_conv_mlp_b1': (0.0, 0.486),
     'L0_conv_mlp_b2': (0.0, 0.1),
     'L1_attn_bq': (0.0, 0.8),
     'L1_attn_bk': (0.0, 2.0),
     'L1_attn_bv': (0.0, 0.1),
     'L1_ffn_gate_b': (0.0, 0.8)}
    factors = {'L0_conv_qkv_w': 8.0,
     'L0_conv_out_w': 8.0,
     'L0_conv_pe_table': 50.267,
     'L0_conv_mlp_w1': 4.148,
     'L0_conv_mlp_w2': 2.818,
     'L1_ffn_gate_w': 8.0,
     'L1_ffn_weight1': 8.0,
     'L1_ffn_weight2': 8.0}
    for name, (base, spread) in spreads.items():
        noise = np.random.default_rng([zlib.crc32(name.encode()), seed]).standard_normal(out[name].shape)
        drawn = base * np.exp(spread * noise) if base else spread * noise
        out[name] = jnp.asarray(drawn.astype(out[name].dtype))
    for name, factor in factors.items():
        out[name] = (out[name] * factor).astype(out[name].dtype)
    return out
```

```python
from contextlib import ExitStack

import numpy as np

import concourse.bass as bass
from concourse import mybir

F32 = mybir.dt.float32
F16 = mybir.dt.float16
BF16 = mybir.dt.bfloat16
ALU = mybir.AluOpType
ACT = mybir.ActivationFunctionType
AX_X = mybir.AxisListType.X

B, H, W, C = 16, 56, 56, 32
S = H * W
WS, SHIFT, NH = 7, 3, 4
HD = C // NH
HIDDEN = 4 * C
L = WS * WS
GB = 4
G = B // GB
NC = H // WS
CT = WS * W
NU = W // WS // 2
HALO = H + SHIFT
SP = W // 2
PI = S // SP
T = 128
NT = -(-S // T)
TL = S - (NT - 1) * T
KN = 448
NK = S // KN
QC = 4 * T
NQ = -(-S // QC)
E, TOP, EH = 16, 8, 128
PB = 8
NEG = -3.0e38
VS_REP, VS_FOLD, VS_BV = 1, 5, 6
VS_GN = VS_BV + 2 + 2 * G
VS_STAGE0 = VS_GN + 2

CONST = {}
_at = 0
for _n, _w in (("ident", 128), ("negident", 128), ("center", 128), ("mean", 128), ("vmask", 128), ("blk4", GB),
               ("head4", NH), ("blk8", PB), ("lo_q", 1), ("lo_k", 1), ("one", 8), ("eps", 1)):
    CONST[_n] = (_at, _w)
    _at += _w
NCONST = _at


def shape_constants():
    p = np.arange(128)
    c = np.zeros((128, NCONST), np.float32)

    def put(name, value):
        at, w = CONST[name]
        c[:, at:at + w] = value

    same = (p[:, None] // C == p[None, :] // C).astype(np.float32)
    put("ident", np.eye(128))
    put("negident", -np.eye(128))
    put("mean", same / C)
    put("center", np.eye(128) - same / C)
    h, pair, ch = np.meshgrid(np.arange(2), np.arange(2), np.arange(C), indexing="ij")
    put("vmask", ((ch // HD) == 2 * pair + h).reshape(1, 128))
    put("blk4", p[:, None] // C == np.arange(GB)[None, :])
    put("head4", (p[:, None] % C) // HD == np.arange(NH)[None, :])
    put("blk8", p[:, None] // E == np.arange(PB)[None, :])
    put("lo_q", -(p[:, None] // C == 1).astype(np.float32))
    put("lo_k", -(p[:, None] // C == 2).astype(np.float32))
    put("one", 1.0)
    put("eps", 1e-5)
    return c


def conv_attention_moe(nc, a, cst_d, out):
    ctx = ExitStack()
    with ctx:
        ctx.enter_context(nc.allow_non_contiguous_dma("small weights, token rows"))

        def sb(name, shape, dt=F32):
            return ctx.enter_context(nc.sbuf_tensor(name, shape, dt))

        def sem(name):
            return ctx.enter_context(nc.semaphore(name))

        xa_d = nc.dram_tensor("xa_scratch", (B * C, S), F32, kind="Internal").ap()
        res_d = nc.dram_tensor("res_scratch", (B * C, S), F32, kind="Internal").ap()

        cst = sb("cst", [128, NCONST])
        wp = sb("wp", [128, 3 * 128])
        wvm = sb("wvm", [128, 4, C])
        wv = sb("wv", [128, 2, GB, 64])
        w1t = sb("w1t", [128, HIDDEN])
        w1f = sb("w1f", [128, GB, HIDDEN])
        w2t = sb("w2t", [128, C])
        wsmall = sb("wsmall", [128, 5, GB, C])
        w1raw = sb("w1raw", [128, GB, C])
        w2raw = sb("w2raw", [C, HIDDEN])
        wrep = sb("wrep", [128, 5, C])
        wbd = sb("wbd", [128, 3, 128])
        wgate = sb("wgate", [128, GB, E])
        pv = sb("pv", [128, 16])
        bv = sb("bv", [128, 17])
        wqr = sb("wqr", [96, 3, C])
        wkr = sb("wkr", [96, 3, C])
        wva = sb("wva", [96, 65])
        gateb = sb("gateb", [128, 1])
        relb = sb("relb", [128, NH, L])
        relr = sb("relr", [128, NH, L])
        gn = sb("gn", [128, G, 4])
        bns = sb("bns", [128, NC, 6])
        mb = sb("mb", [128, 16])
        tok = sb("tok", [128, B, NT, C])
        ximg = sb("ximg", [128, G * HALO, W])
        xf = ximg[:, :, :].rearrange("p r c -> p (r c)")[:, 0:B * NT * C].rearrange(
            "p (t b c) -> p t b c", b=B, t=NT)
        ARENA = 19400
        arena = sb("arena", [128, ARENA])
        at = [0]

        def carve(n, parts=128):
            v = arena[0:parts, at[0]:at[0] + n]
            at[0] += n
            assert at[0] <= ARENA
            return v

        xin = carve(GB * SP * C, PI).rearrange("p (b n c) -> p b n c", b=GB, c=C)
        xin2 = carve(2 * GB * SP * C, PI).rearrange("p (i n b c) -> p i n b c", i=2, b=GB, c=C)
        at[0] = 0
        xg = carve(CT)
        sq = carve(CT)
        sd = carve(CT)
        rs = carve(CT)
        xn = carve(CT)
        qz = carve(GB * CT).rearrange("p (j n) -> p j n", j=GB)
        kz = carve(NH * CT).rearrange("p (h n) -> p h n", h=NH)
        sc = carve(2 * GB * NH * L).rearrange("p (i n) -> p i n", i=2)
        ex = carve(2 * GB * NH * L).rearrange("p (i n) -> p i n", i=2)
        pr = carve(2 * GB * NH * 64).rearrange("p (i n) -> p i n", i=2)
        mx = carve(4 * GB * NH).rearrange("p (i n) -> p i n", i=4)
        pt = carve(2 * 8 * 113).rearrange("p (i n) -> p i n", i=2)
        vs = carve(2 * GB * 128).rearrange("p (i n) -> p i n", i=2)
        oc = carve(CT)
        o2 = carve(CT)
        gh = carve(GB * CT).rearrange("p (j n) -> p j n", j=GB)
        t1 = carve(CT)
        xa = carve(CT)
        rt = carve(CT)
        at[0] = 0
        xr = carve(S, 96)
        q2 = carve(S // 2)[:, :].bitcast(F16)
        k2 = carve(S // 2)[:, :].bitcast(F16)
        hi = carve(KN // 2 * 2)[:, :].bitcast(F16).rearrange("p (i n) -> p i n", i=2)
        pk = carve(2 * 2 * QC).rearrange("p (i n) -> p i n", i=2)
        pl = carve(2 * QC).bitcast(F16).rearrange("p (i n) -> p i n", i=2)
        vh = carve(NT * 33).bitcast(F16).rearrange("p (t n) -> p t n", t=NT)
        res = carve(NT * C).rearrange("p (t c) -> p t c", t=NT)
        mxp = carve(4 * 8).rearrange("p (t n) -> p t n", t=4)
        mq = carve(8)
        rden = carve(8)
        lnx = carve(NT * C).rearrange("p (t c) -> p t c", t=NT)
        lns = carve(NT * C).rearrange("p (t c) -> p t c", t=NT)
        lnv = carve(5 * NT).rearrange("p (i t) -> p i t", i=5)
        half = sb("half", [128, NT])
        at[0] = 0
        xft = carve(S)
        lg = carve(S)
        pe_ = carve(S)
        mk = carve(S)
        mt = carve(NT * 128).rearrange("p (t n) -> p t n", t=NT)
        bdo = carve(PB * C)
        m8 = carve(8)
        st = carve(8)
        pooled = carve(E * PB, C + 1).rearrange("p (e b) -> p e b", e=E)
        eh = carve(E * PB)
        eo = carve(E * PB, C)
        w1e = sb("w1e", [C + 1, E, EH])
        w2e = sb("w2e", [EH, E, C])
        w2b = sb("w2b", [1, E, C])

        ps = ctx.enter_context(nc.psum_tensor("ps", [128, 8, 512], F32))

        def cv(name, parts=128, at_=0):
            o, w = CONST[name]
            return cst[at_:at_ + parts, o:o + w]

        G1, B1N, QB, KB, VB, OB, G2, B2N, M2B, M1B = range(10)
        BK, BV, BO, B1, BKH, BQM, SQM = 0, 1, 2, 3, 4, 8, 12

        s_cst = sem("constants_loaded")
        s_w = sem("weights_loaded")
        s_bias = sem("relative_bias_loaded")
        s_clear = sem("cleared")
        s_vec = sem("setup_vector_steps")
        s_wt = sem("weights_transposed")
        s_wb = sem("bias_products")
        s_xin = sem("input_loaded")
        s_xt = sem("input_transposed")
        s_xorder = sem("input_ordered")
        s_xe = sem("input_evacuated")
        s_gsd = sem("groupnorm_std")
        s_clear2 = sem("attention_cleared")
        s_pow = sem("pow_steps")
        conv = {n: sem("conv_" + n) for n in (
            "xg", "center", "square", "var", "std", "rstd", "norm", "qk", "kz", "score", "vprod", "bias", "max", "sub",
            "exp", "sum", "rsum", "prob", "ptrans", "pcopy_a", "pcopy_b", "vcopy", "av", "oc", "oproj", "o2", "hid",
            "gelu", "y", "t1", "rt", "stored")}
        att = {n: sem("attn_" + n) for n in (
            "load", "prod", "hi", "lo", "vprod", "vcopy", "score1", "max1", "maxall", "mrow", "mcopy", "score2", "exp",
            "av", "rden", "o", "tok", "ln", "ss", "xf", "rest", "vrest", "sum")}
        moe = {n: sem("moe_" + n) for n in (
            "xft", "xftc_v", "xftc_a", "logit", "logitc", "top", "exp", "mk", "mt", "mtc_v", "mtc_a", "pool", "poolc",
            "hid", "gelu", "out", "outc", "outt", "bdo", "scat", "add", "stored")}
        block = ctx.enter_context(nc.Block())

        x_d = a["x"].rearrange("b h w c -> b (h w) c")
        out_d = out.rearrange("b h w c -> b (h w) c")

        def col(v):
            return v.rearrange("(n o) -> n o", o=1)


        def image(g, row, rows):
            return ximg[:, bass.ds(g * HALO + row, rows), :]

        def tile_rows(t):
            return T if t < NT - 1 else TL

        def chunk_tiles(c):
            return range(4 * c, min(4 * c + 4, NT))

        def chunk_cols(c):
            return min(QC, S - QC * c)

        NG = (NT + 1) // 2
        NP1 = NT * NK
        NX = -(-NT // 4)
        weights = 5 + 2 + 9 * GB + 1 + 12 + 2 + PB + 3

        @block.sync
        def _(sp):
            sp.dma_start(cst[:, :], cst_d).then_inc(s_cst, 16)
            count = [0]

            def load(dst, src):
                sp.dma_start(dst, src).then_inc(s_w, 16)
                count[0] += 1

            def load_input(g):
                if g:
                    sp.wait_ge(s_xorder, g)
                sp.dma_start(xin.rearrange("p b n c -> p b (n c)"), x_d[GB * g:GB * (g + 1)].rearrange("b (p n) c -> p b (n c)", p=PI))\
                  .then_inc(s_xin, 16)

            load_input(0)
            for i in range(3):
                load(wsmall[0:C, i, 0, :], a["L0_conv_qkv_w"][C * i:C * (i + 1), :])
            load(wsmall[0:C, 3, 0, :], a["L0_conv_out_w"])
            load(wsmall[0:E, 4, 0, :], a["L1_ffn_gate_w"])
            load(w1raw[:, 0, :], a["L0_conv_mlp_w1"])
            load(w2raw[:, :], a["L0_conv_mlp_w2"])
            qkvb = a["L0_conv_qkv_b"]
            for k, v in ((G1, a["L0_conv_norm1_g"]), (B1N, a["L0_conv_norm1_b"]), (QB, qkvb[0:C]), (KB, qkvb[C:2 * C]),
                         (VB, qkvb[2 * C:3 * C]), (OB, a["L0_conv_out_b"]), (G2, a["L0_conv_norm2_g"]),
                         (B2N, a["L0_conv_norm2_b"]), (M2B, a["L0_conv_mlp_b2"])):
                for j in range(GB):
                    load(pv[C * j:C * (j + 1), k:k + 1], col(v))
            load(pv[:, M1B:M1B + 1], col(a["L0_conv_mlp_b1"]))
            sp.wait_ge(s_clear, 2)
            for r in range(3):
                load(wqr[0:C, r, :], a["L1_attn_Wq"])
                load(wqr[C:C + 1, r, :], a["L1_attn_bq"].rearrange("(o n) -> o n", o=1))
                load(wkr[0:C, r, :], a["L1_attn_Wk"])
                load(wkr[C:C + 1, r, :], a["L1_attn_bk"].rearrange("(o n) -> o n", o=1))
            load(wva[0:C, 0:C], a["L1_attn_Wv"])
            load(wva[C:C + 1, 0:C], a["L1_attn_bv"].rearrange("(o n) -> o n", o=1))
            for b in range(PB):
                load(gateb[E * b:E * (b + 1), :], col(a["L1_ffn_gate_b"]))
            load(w1e[:, :, :], a["L1_ffn_weight1"].rearrange("e d h -> d e h"))
            load(w2e[:, :, :], a["L1_ffn_weight2"][:, 0:EH, :].rearrange("e h o -> h e o"))
            load(w2b[:, :, :], a["L1_ffn_weight2"][:, EH:EH + 1, :].rearrange("e h o -> h e o"))
            assert count[0] == weights
            for g in range(1, G):
                load_input(g)
            xa_g = xa_d.rearrange("(g p) n -> g p n", g=G)
            res_g = res_d.rearrange("(g p) n -> g p n", g=G)
            with sp.Fori(0, G) as g:
                with sp.Fori(0, NC) as c:
                    it = g * NC + c
                    sp.wait_ge(conv["rt"], it + 1)
                    sp.dma_start(xa_g[bass.ds(g, 1), :, bass.ds(c * CT, CT)].rearrange("o p n -> (o p) n"), xa[:, :])\
                      .then_inc(conv["stored"], 16)
                    sp.dma_start(res_g[bass.ds(g, 1), :, bass.ds(c * CT, CT)].rearrange("o p n -> (o p) n"), rt[:, :])\
                      .then_inc(conv["stored"], 16)
            sp.wait_ge(conv["stored"], 32 * G * NC)
            xa_b = xa_d.rearrange("(b p) n -> b p n", b=B)
            res_b = res_d.rearrange("(b p) n -> b p n", b=B)
            sp.wait_ge(s_clear2, 1)
            with sp.Fori(0, B) as b:
                sp.wait_ge(att["vprod"], b * NT)
                sp.dma_start(xr[0:C, :], xa_b[bass.ds(b, 1)].rearrange("o p n -> (o p) n")).then_inc(att["load"], 16)
                sp.dma_start(xr[2 * C:3 * C, :], res_b[bass.ds(b, 1)].rearrange("o p n -> (o p) n"))\
                  .then_inc(att["load"], 16)
            for h in range(B // PB):
                sp.wait_ge(moe["add"], NT * (h + 1))
                for b in range(PB * h, PB * (h + 1)):
                    sp.dma_start(out_d[b, 0:(NT - 1) * T, :].rearrange("(t p) c -> p t c", p=T), tok[:, b, 0:NT - 1, :])\
                      .then_inc(moe["stored"], 16)
                    sp.dma_start(out_d[b, (NT - 1) * T:S, :], tok[0:TL, b, NT - 1, :]).then_inc(moe["stored"], 16)
            sp.wait_ge(moe["stored"], 32 * B)

        @block.gpsimd
        def _(pool):
            pool.memset(relr[:, :, :], 0.0).then_inc(s_clear, 1)
            pool.memset(wva[:, :], 0.0)
            pool.memset(wqr[:, :, :], 0.0)
            pool.memset(wkr[:, :, :], 0.0).then_inc(s_clear, 1)
            pool.memset(half[:, :], -0.5).then_inc(s_clear, 1)
            pool.memset(tok[:, :, NT - 1, :], 0.0).then_inc(s_clear, 1)
            pool.wait_ge(s_clear, 4)
            with pool.Fori(0, G * NC) as it:
                for u in range(NU + 1):
                    if u < NU:
                        i = u % 2
                        pool.wait_ge(conv["max"], it * NU + u + 1)
                        s3 = sc[0:113, i, :].rearrange("p (m k) -> p m k", k=L)
                        pool.tensor_tensor(s3, s3, mx[0:113, i, :].rearrange("p (m o) -> p m o", o=1)
                                           .broadcast_to([113, GB * NH, L]), ALU.subtract).then_inc(conv["sub"], 1)
                    if u >= 1:
                        i = (u - 1) % 2
                        pool.wait_ge(conv["rsum"], it * NU + u)
                        if u >= 3:
                            pool.wait_ge(conv["ptrans"], it * (2 * NU) + 2 * (u - 2))
                        pool.tensor_tensor(pr[0:113, i, :].rearrange("p (m k) -> p m k", k=64)[:, :, 0:L],
                                           ex[0:113, i, :].rearrange("p (m k) -> p m k", k=L),
                                           mx[0:113, 2 + i, :].rearrange("p (m o) -> p m o", o=1)
                                           .broadcast_to([113, GB * NH, L]), ALU.mult).then_inc(conv["prob"], 1)
            with pool.Fori(0, B) as b:
                for c in range(NQ):
                    tiles = chunk_tiles(c)
                    k, t0, rows = len(tiles), 4 * c, tile_rows(4 * c)
                    pool.wait_ge(att["o"], b * NQ + c + 1)
                    pool.tensor_tensor(lnx[0:rows, t0:t0 + k, :], lnx[0:rows, t0:t0 + k, :], lns[0:rows, t0:t0 + k, :],
                                       ALU.add).then_inc(att["sum"], 1)
                    pool.wait_ge(att["sum"], b * NQ + c + 1)
                    pool.tensor_tensor(tok[0:rows, bass.ds(b, 1), t0:t0 + k, :].rearrange("p o t c -> p (o t) c"),
                                       lnx[0:rows, t0:t0 + k, :], res[0:rows, t0:t0 + k, :], ALU.add)\
                        .then_inc(att["tok"], 1)
                pool.wait_ge(att["ln"], b * 5 + 5)
                pool.tensor_tensor(lnv[:, 4, :], lnv[:, 3, :], half[:, :], ALU.pow).then_inc(s_pow, 1)
                pool.wait_ge(s_pow, b + 1)
                pool.tensor_tensor(xf[:, :, bass.ds(b, 1), :].rearrange("p t o c -> p (t o) c"), lnx[:, :, :],
                                   lnv[:, 4, :].rearrange("p (t o) -> p t o", o=1).broadcast_to([128, NT, C]),
                                   ALU.mult).then_inc(att["xf"], 1)

        @block.scalar
        def _(act):
            tab = a["L0_conv_pe_table"].rearrange("h (y x) -> h y x", x=2 * WS - 1)
            act.wait_ge(s_clear, 2)
            for hf in range(2):
                for qy in range(WS):
                    for qx in range(WS):
                        p = 64 * hf + WS * qy + qx
                        act.dma_start(relr[p:p + 1, :, :].rearrange("p h (y x) -> p h y x", x=WS),
                                      tab[:, qy:qy + WS, qx:qx + WS].rearrange("h y (o x) -> o h y x", o=1))\
                           .then_inc(s_bias, 16)
            for g in range(G):
                act.wait_ge(s_xin, 16 * (g + 1))
                if g >= 2:
                    act.wait_ge(s_xt, NK * (g - 1))
                act.activation(xin2[:, g % 2], xin.rearrange("p b n c -> p n b c"), ACT.Copy).then_inc(s_xorder, 1)
            act.wait_ge(s_vec, VS_GN)
            act.activation(gn[:, :, 2], gn[:, :, 1], ACT.Sqrt, bias=cv("eps")[:, 0:1]).then_inc(s_gsd, 1)

            def layer_norm(it, k):
                act.wait_ge(conv["center"], it * 3 + k)
                act.activation(sq[:, :], ps[:, 7, 0:CT], ACT.Square).then_inc(conv["square"], 1)
                act.wait_ge(conv["var"], it * 3 + k)
                act.activation(sd[:, :], ps[:, 5, 0:CT], ACT.Sqrt, bias=cv("eps")[:, 0:1]).then_inc(conv["std"], 1)

            def values_and_exp(it, u):
                i = u % 2
                act.wait_ge(conv["vprod"], it * NU + u + 1)
                if u >= 2:
                    act.wait_ge(conv["av"], it * NU + u - 1)
                act.activation(vs[0:113, i, :], ps[0:113, 7, :], ACT.Copy)\
                   .then_inc(conv["vcopy"], 1)
                act.wait_ge(conv["sub"], it * NU + u + 1)
                if u >= 2:
                    act.wait_ge(conv["prob"], it * NU + u - 1)
                act.activation(ex[0:113, i, :], sc[0:113, i, :], ACT.Exp).then_inc(conv["exp"], 1)

            def probs_a(it, u):
                i = u % 2
                act.wait_ge(conv["ptrans"], it * (2 * NU) + 2 * u + 1)
                if u >= 2:
                    act.wait_ge(conv["av"], it * NU + u - 1)
                act.activation(pt[:, i, 0:4 * 113].rearrange("p (n q) -> p n q", q=113),
                               ps[:, 4, :].rearrange("p (n q) -> p n q", q=128)[:, :, 0:113], ACT.Copy)\
                   .then_inc(conv["pcopy_a"], 1)

            with act.Fori(0, G * NC) as it:
                layer_norm(it, 1)
                act.wait_ge(conv["qk"], it * 2 + 1)
                for j in range(GB):
                    act.activation(qz[:, j, :], ps[:, 4, 0:CT], ACT.Identity, bias=bv[:, BQM + j:BQM + j + 1],
                                   scale=bv[:, SQM + j:SQM + j + 1])
                act.wait_ge(conv["qk"], it * 2 + 2)
                for h in range(NH):
                    last = act.activation(kz[:, h, :], ps[:, 5, 0:CT], ACT.Identity, bias=bv[:, BKH + h:BKH + h + 1],
                                          scale=cv("head4")[:, h:h + 1])
                last.then_inc(conv["kz"], 1)
                values_and_exp(it, 0)
                for u in range(1, NU):
                    values_and_exp(it, u)
                    probs_a(it, u - 1)
                probs_a(it, NU - 1)
                act.wait_ge(conv["av"], it * NU + NU)
                act.activation(oc[:, :].rearrange("p (r w c) -> p w r c", r=WS, c=WS),
                               ps[:, 6, 0:CT].rearrange("p (w r c) -> p w r c", r=WS, c=WS), ACT.Copy)\
                   .then_inc(conv["oc"], 1)
                act.wait_ge(conv["oproj"], it + 1)
                act.activation(o2[:, :], ps[:, 4, 0:CT], ACT.Identity, bias=bv[:, BO:BO + 1]).then_inc(conv["o2"], 1)
                layer_norm(it, 2)
                act.wait_ge(conv["hid"], it + 1)
                act.activation(gh[:, :, :], ps[:, 0:GB, 0:CT], ACT.Gelu, bias=bv[:, B1:B1 + 1]).then_inc(conv["gelu"], 1)
                layer_norm(it, 3)

            with act.Fori(0, B) as b:
                for n in range(2 * NK):
                    act.wait_ge(att["prod"], b * (2 * NK) + n + 1)
                    if n >= 2:
                        act.wait_ge(att["lo"], b * (2 * NK) + n - 1)
                    act.activation(hi[0:96, n % 2, :], ps[0:96, 4 + n % 2, 0:KN], ACT.Copy).then_inc(att["hi"], 1)
                act.wait_ge(att["vprod"], b * NT + NT)
                for src, dst in ((slice(0, C + 1), vh[:, :, 0:C + 1]), (slice(C + 1, 65), res[:, :, :])):
                    for k in range(4):
                        n = min(7, NT - 7 * k)
                        rows = T
                        if k == 3:
                            act.activation(dst[0:TL, NT - 1, :], ps[0:TL, 3, 65 * (n - 1):65 * n][:, src], ACT.Copy)
                            n -= 1
                        last = act.activation(dst[:, 7 * k:7 * k + n, :],
                                              ps[:, k, 0:65 * n].rearrange("p (t n) -> p t n", n=65)[:, :, src], ACT.Copy)
                    last.then_inc(att["vcopy"], 1)

                def max_row(c):
                    n = chunk_cols(c)
                    act.wait_ge(att["mrow"], b * NQ + c + 1)
                    act.activation(q2[96:97, QC * c:QC * c + n], ps[96:97, 7, 0:n], ACT.Copy).then_inc(att["mcopy"], 1)

                max_row(0)
                for c in range(NQ):
                    n = chunk_cols(c)
                    for r in range(NG):
                        at_ = NG * c + r
                        act.wait_ge(att["score2"], b * (NG * NQ) + at_ + 1)
                        if at_ >= 2:
                            act.wait_ge(att["av"], b * (NG * NQ) + at_ - 1)
                        par = at_ % 2
                        if 2 * r + 1 < NT:
                            k = 2
                            rows = T
                        else:
                            k, rows = 1, TL
                        act.activation(pk[0:rows, par, :].rearrange("p (k n) -> p k n", k=2)[:, 0:k, 0:n],
                                       ps[0:rows, 2 * par:2 * par + k, 0:n], ACT.Exp, scale=float(C) ** -0.5)\
                           .then_inc(att["exp"], 1)
                    if c + 1 < NQ:
                        max_row(c + 1)

            for h in range(B // PB):
                for gg in range(2):
                    for n in range(1, NX, 2):
                        act.wait_ge(moe["xft"], NX * (2 * h + gg) + n + 1)
                        act.activation(xft[:, QC * n:QC * n + chunk_cols(n)], ps[:, n, 0:chunk_cols(n)], ACT.Copy)\
                           .then_inc(moe["xftc_a"], 1)
                    for n in range(NK):
                        act.wait_ge(moe["logit"], NK * (2 * h + gg) + n + 1)
                        act.activation(lg[64 * gg:64 * gg + 64, KN * n:KN * n + KN], ps[64 * gg:64 * gg + 64, 7, 0:KN],
                                       ACT.Identity, bias=gateb[64 * gg:64 * gg + 64, 0:1]).then_inc(moe["logitc"], 1)
                act.wait_ge(moe["top"], 2 * h + 2)
                act.activation(pe_[:, :], lg[:, :], ACT.Exp, bias=st[:, 0:1], accum_out=st[:, 1:2]).then_inc(moe["exp"], 1)
                for n in range(1, NX, 2):
                    act.wait_ge(moe["mt"], NX * h + n + 1)
                    k = len(chunk_tiles(n))
                    act.activation(mt[:, 4 * n:4 * n + k, :].rearrange("p t n -> p (t n)"), ps[:, n, 0:128 * k], ACT.Copy)\
                       .then_inc(moe["mtc_a"], 1)
                act.wait_ge(moe["hid"], h + 1)
                act.activation(eh[:, :], ps[:, 0, 0:E * PB], ACT.Gelu).then_inc(moe["gelu"], 1)

        @block.vector
        def _(dve):
            steps = [0]

            def step(ins, wait=True):
                steps[0] += 1
                ins.then_inc(s_vec, 1)
                if wait:
                    dve.wait_ge(s_vec, steps[0])

            def bcast(v, n):
                return v.rearrange("p (o c) -> p o c", o=1).broadcast_to([v.shape[0], n, v.shape[1]])

            dve.wait_ge(s_cst, 16)
            dve.wait_ge(s_w, 16 * weights)
            dve.memset(ps[:, 0:4, :], 0.0)
            for i in range(4):
                dve.tensor_copy(wsmall[0:C, i, 1:GB, :], bcast(wsmall[0:C, i, 0, :], GB - 1))
            dve.tensor_copy(wsmall[0:E, 4, 1:GB, :], bcast(wsmall[0:E, 4, 0, :], GB - 1))
            step(dve.tensor_copy(w1raw[:, 1:GB, :], bcast(w1raw[:, 0, :], GB - 1)))
            assert steps[0] == VS_REP
            dve.wait_ge(s_wt, 1)
            dve.tensor_copy(wrep[:, 0:4, :], ps[:, 4, 0:128].rearrange("p (i c) -> p i c", i=4))
            dve.tensor_copy(wrep[:, 4, 0:E], ps[:, 4, 128:128 + E])
            dve.tensor_copy(w1t[:, :], ps[:, 5, 0:128])
            step(dve.tensor_copy(w2t[:, :], ps[:, 6, 0:C]))

            def mask(name, n):
                return cv(name).rearrange("p (j o) -> p j o", o=1).broadcast_to([128, GB, n])

            for i in range(3):
                dve.tensor_tensor(wbd[:, i, :].rearrange("p (j c) -> p j c", j=GB), bcast(wrep[:, i, :], GB), mask("blk4", C),
                                  ALU.mult)
            dve.tensor_tensor(wp[:, 256:384].rearrange("p (j c) -> p j c", j=GB), bcast(wrep[:, 3, :], GB), mask("blk4", C),
                              ALU.mult)
            dve.tensor_tensor(wgate[:, :, :], bcast(wrep[:, 4, 0:E], GB), mask("blk4", E), ALU.mult)
            dve.scalar_tensor_tensor(wvm[:, :, :],
                                     cv("vmask").rearrange("p (n c) -> p n c", c=C), pv[:, G1:G1 + 1],
                                     bcast(wrep[:, 2, :], 4), ALU.mult, ALU.mult)
            for j in range(GB):
                dve.tensor_scalar(w1f[:, j, :], w1t[:, :], pv[:, G2:G2 + 1], cv("blk4")[:, j:j + 1], ALU.mult, ALU.mult)
            step(dve.tensor_copy(wva[64:96, C + 1:65], cv("ident", 32, 64)[:, 64:96]))
            for j in range(GB):
                dve.tensor_scalar(wv[:, :, j, :], wvm[:, :, :].rearrange("p (h a) c -> p h (a c)", h=2),
                                  cv("blk4")[:, j:j + 1], None, ALU.mult)
            step(dve.memset(wva[C:C + 1, C:C + 1], 1.0))
            step(dve.tensor_scalar(wp[:, 0:256], wbd[:, 0:2, :].rearrange("p i c -> p (i c)"), pv[:, G1:G1 + 1], None,
                                   ALU.mult))
            assert steps[0] == VS_FOLD
            dve.wait_ge(s_wb, 1)
            dve.tensor_scalar(bv[:, 16:17], ps[:, 4, 0:1], pv[:, QB:QB + 1], float(HD) ** -0.5, ALU.add, ALU.mult)
            dve.tensor_scalar(bv[:, SQM:SQM + GB], cv("blk4"), float(HD) ** -0.5, None, ALU.mult)
            dve.tensor_scalar(bv[:, BK:BK + 1], ps[:, 4, 1:2], pv[:, KB:KB + 1], None, ALU.add)
            dve.tensor_scalar(bv[:, B1:B1 + 1], ps[:, 5, 0:1], pv[:, M1B:M1B + 1], None, ALU.add)
            step(dve.tensor_scalar(bv[:, BV:BV + 1], ps[:, 4, 2:3], pv[:, VB:VB + 1], None, ALU.add))
            assert steps[0] == VS_BV
            dve.tensor_scalar(bv[:, BQM:BQM + GB], cv("blk4"), bv[:, 16:17], None, ALU.mult)
            dve.tensor_scalar(bv[:, BKH:BKH + NH], cv("head4"), bv[:, BK:BK + 1], None, ALU.mult)
            dve.wait_ge(s_wb, 2)
            step(dve.tensor_scalar(bv[:, BO:BO + 1], ps[:, 4, 3:4], pv[:, OB:OB + 1], None, ALU.add))
            dve.wait_ge(s_bias, 16 * 2 * L)
            step(dve.tensor_copy(relb[:, :, :], relr[:, :, ::-1]))

            for g in range(G):
                img = ximg[:, g * HALO:(g + 1) * HALO, :].rearrange("p r c -> p (r c)")
                for n in range(NK):
                    dve.wait_ge(s_xt, NK * g + n + 1)
                    dve.tensor_copy(img[:, SHIFT * W:].rearrange("p (q j) -> p j q", j=SP)[:, 4 * n:4 * n + 4, :],
                                    ps[:, n, 0:KN].rearrange("p (j q) -> p j q", j=4)).then_inc(s_xe, 1)
                dve.wait_ge(s_xe, NK * (g + 1))
                dve.tensor_copy(img[:, 0:SHIFT * W], img[:, H * W:HALO * W])
                for c in range(NC):
                    last = dve.bn_stats(bns[:, c, :], img[:, SHIFT * W + CT * c:SHIFT * W + CT * (c + 1)])
                step(last)
                step(dve.bn_aggr(gn[:, g, 0:2], bns[:, :, :].rearrange("p c s -> p (c s)")))
            assert steps[0] == VS_GN
            dve.wait_ge(s_gsd, 1)
            step(dve.reciprocal(gn[:, :, 3], gn[:, :, 2]))
            dve.memset(pr[:, :, :], 0.0)
            dve.memset(ps[:, 7, :], 0.0)
            step(dve.memset(ps[:, 0:4, :], 0.0))
            assert steps[0] == VS_STAGE0

            def bias_and_max(it, u):
                i = u % 2
                dve.wait_ge(conv["score"], it * NU + u + 1)
                if u >= 2:
                    dve.wait_ge(conv["exp"], it * NU + u - 1)
                s4 = sc[0:113, i, :].rearrange("p (j n) -> p j n", j=GB)
                dve.tensor_tensor(s4, ps[0:113, 0:GB, 0:NH * L],
                                  bcast(relb[0:113, :, :].rearrange("p h k -> p (h k)"), GB), ALU.add)\
                   .then_inc(conv["bias"], 1)
                dve.wait_ge(conv["bias"], it * NU + u + 1)
                dve.tensor_reduce(mx[0:113, i, :], sc[0:113, i, :].rearrange("p (m k) -> p m k", k=L), AX_X, ALU.max)\
                   .then_inc(conv["max"], 1)

            def sums(it, u):
                i = u % 2
                dve.wait_ge(conv["exp"], it * NU + u + 1)
                dve.tensor_reduce(mx[0:113, 2 + i, :], ex[0:113, i, :].rearrange("p (m k) -> p m k", k=L), AX_X, ALU.add)\
                   .then_inc(conv["sum"], 1)
                dve.wait_ge(conv["sum"], it * NU + u + 1)
                dve.reciprocal(mx[0:113, 2 + i, :], mx[0:113, 2 + i, :]).then_inc(conv["rsum"], 1)

            def probs_b(it, u):
                i = u % 2
                dve.wait_ge(conv["ptrans"], it * (2 * NU) + 2 * u + 2)
                if u >= 2:
                    dve.wait_ge(conv["av"], it * NU + u - 1)
                dve.tensor_copy(pt[:, i, 4 * 113:8 * 113].rearrange("p (n q) -> p n q", q=113),
                                ps[:, 5, :].rearrange("p (n q) -> p n q", q=128)[:, :, 0:113]).then_inc(conv["pcopy_b"], 1)

            def normalize(it, k, dst):
                dve.wait_ge(conv["std"], it * 3 + k)
                dve.reciprocal(rs[:, :], sd[:, :]).then_inc(conv["rstd"], 1)
                dve.wait_ge(conv["rstd"], it * 3 + k)
                if k == 1:
                    def rows(v):
                        return v.rearrange("p (r w c) -> p r w c", r=WS, c=WS)
                    dve.tensor_tensor(dst[:, :].rearrange("p (w r c) -> p r w c", r=WS, c=WS), rows(ps[:, 7, 0:CT]),
                                      rows(rs[:, :]), ALU.mult).then_inc(conv["norm"], 1)
                else:
                    dve.tensor_tensor(dst[:, :], ps[:, 7, 0:CT], rs[:, :], ALU.mult).then_inc(conv["norm"], 1)

            with dve.Fori(0, G) as g:
                with dve.Fori(0, NC) as c:
                    it = g * NC + c
                    mean = gn[:, bass.ds(g, 1), 0]
                    rstd = gn[:, bass.ds(g, 1), 3]
                    xg3 = xg[:, :].rearrange("p (r c) -> p r c", c=W)
                    src = image(g, c * WS, WS)
                    dve.tensor_scalar(xg3[:, :, SHIFT:W], src[:, :, 0:W - SHIFT], mean, rstd, ALU.subtract, ALU.mult)
                    dve.tensor_scalar(xg3[:, :, 0:SHIFT], src[:, :, W - SHIFT:W], mean, rstd, ALU.subtract, ALU.mult)\
                       .then_inc(conv["xg"], 1)
                    normalize(it, 1, xn)
                    bias_and_max(it, 0)
                    for u in range(NU):
                        if u + 1 < NU:
                            bias_and_max(it, u + 1)
                        sums(it, u)
                        probs_b(it, u)
                    normalize(it, 2, xn)
                    dve.wait_ge(conv["y"], it + 1)
                    dve.scalar_tensor_tensor(t1[:, :], ps[:, 6, 0:CT], pv[:, M2B:M2B + 1],
                                             image(g, c * WS + SHIFT, WS).rearrange("p r c -> p (r c)"), ALU.add, ALU.add)\
                       .then_inc(conv["t1"], 1)
                    dve.wait_ge(conv["stored"], it * 32)
                    normalize(it, 3, xa)
                    dve.wait_ge(conv["norm"], it * 3 + 3)
                    dve.tensor_tensor(rt[:, :], t1[:, :], xa[:, :], ALU.add).then_inc(conv["rt"], 1)

            dve.wait_ge(conv["stored"], 32 * G * NC)
            dve.memset(xr[32:64, :], 0.0).then_inc(s_vec, 1)
            dve.wait_ge(s_vec, VS_STAGE0 + 1)
            dve.memset(xr[32:33, :], 1.0)
            dve.memset(vh[:, NT - 1, :], 0.0)
            dve.memset(k2[96:97, :], 1.0).then_inc(s_clear2, 1)
            with dve.Fori(0, B) as b:
                for n in range(2 * NK):
                    dst, m = (q2, "lo_q") if n < NK else (k2, "lo_k")
                    cols = slice(KN * (n % NK), KN * (n % NK) + KN)
                    dve.wait_ge(att["hi"], b * (2 * NK) + n + 1)
                    dve.scalar_tensor_tensor(dst[0:96, cols], hi[0:96, n % 2, :], cv(m, 96), ps[0:96, 4 + n % 2, 0:KN],
                                             ALU.mult, ALU.add).then_inc(att["lo"], 1)

                def row_max_part(c, k):
                    t, n = k // NK, k % NK
                    rows, i = tile_rows(t), t % 4
                    dve.wait_ge(att["score1"], b * NP1 + k + 1)
                    dve.tensor_reduce(mxp[0:rows, i, n:n + 1], ps[0:rows, 4 + k % 2, 0:KN], AX_X, ALU.max)\
                       .then_inc(att["max1"], 1)
                    if n == NK - 1:
                        dve.wait_ge(att["max1"], b * NP1 + k + 1)
                        dve.tensor_reduce(mq[0:rows, 4 * (c % 2) + i:4 * (c % 2) + i + 1], mxp[0:rows, i, 0:NK], AX_X, ALU.max)\
                           .then_inc(att["maxall"], 1)

                def row_max(c):
                    for k in range(NK * len(chunk_tiles(c))):
                        row_max_part(c, k)

                def rest(c, r):
                    at_, n = NG * c + r, chunk_cols(c)
                    dve.wait_ge(att["exp"], b * (NG * NQ) + at_ + 1)
                    k, rows = (2, T) if 2 * r + 1 < NT else (1, TL)
                    full = pk[0:rows, at_ % 2, :]
                    dve.tensor_tensor(pl[0:rows, at_ % 2, :].rearrange("p (k n) -> p k n", k=2)[:, 0:k, 0:n],
                                      full.rearrange("p (k n) -> p k n", k=2)[:, 0:k, 0:n],
                                      full.bitcast(BF16).rearrange("p (k n s) -> p k n s", k=2, s=2)[:, 0:k, 0:n, 1],
                                      ALU.subtract).then_inc(att["rest"], 1)

                dve.wait_ge(att["vcopy"], b * 2 + 2)
                for k in range(4):
                    n = min(7, NT - 7 * k)
                    if k == 3:
                        dve.tensor_tensor(vh[0:TL, NT - 1, 33:65], ps[0:TL, 3, 65 * (n - 1):65 * (n - 1) + C],
                                          vh[0:TL, NT - 1, 0:C], ALU.subtract)
                        n -= 1
                    last = dve.tensor_tensor(vh[:, 7 * k:7 * k + n, 33:65],
                                             ps[:, k, 0:65 * n].rearrange("p (t n) -> p t n", n=65)[:, :, 0:C],
                                             vh[:, 7 * k:7 * k + n, 0:C], ALU.subtract)
                last.then_inc(att["vrest"], 1)
                row_max(0)
                for c in range(NQ):
                    todo = [NK * t + n for t in (chunk_tiles(c + 1) if c + 1 < NQ else ()) for n in range(NK)]
                    done = 0
                    for r in range(NG):
                        upto = len(todo) * (r + 1) // NG
                        for k in todo[done:upto]:
                            row_max_part(c + 1, k)
                        done = upto
                        rest(c, r)
                    tiles = chunk_tiles(c)
                    k, t0, rows = len(tiles), 4 * c, tile_rows(4 * c)
                    o4 = ps[0:rows, 6, 0:65 * k].rearrange("p (t n) -> p t n", n=65)
                    dve.wait_ge(att["av"], b * (NG * NQ) + NG * (c + 1))
                    if c == 0:
                        dve.wait_ge(att["xf"], b)
                    dve.reciprocal(rden[0:rows, 0:k], o4[:, :, C]).then_inc(att["rden"], 1)
                    dve.wait_ge(att["rden"], b * NQ + c + 1)
                    rd = rden[0:rows, 0:k].rearrange("p (t o) -> p t o", o=1).broadcast_to([rows, k, C])
                    dve.tensor_tensor(lnx[0:rows, t0:t0 + k, :], o4[:, :, 0:C], rd, ALU.mult)
                    dve.tensor_tensor(lns[0:rows, t0:t0 + k, :], o4[:, :, 33:65], rd, ALU.mult).then_inc(att["o"], 1)
                tb = tok[:, bass.ds(b, 1), :, :].rearrange("p o t c -> p (o t) c")
                dve.wait_ge(att["tok"], b * NQ + NQ)
                dve.tensor_reduce(lnv[:, 0, :], tb, AX_X, ALU.add).then_inc(att["ln"], 1)
                dve.wait_ge(att["ln"], b * 5 + 1)
                dve.tensor_scalar(lnv[:, 1, :], lnv[:, 0, :], 1.0 / C, None, ALU.mult).then_inc(att["ln"], 1)
                dve.wait_ge(att["ln"], b * 5 + 2)
                dve.tensor_tensor(lnx[:, :, :], tb,
                                  lnv[:, 1, :].rearrange("p (t o) -> p t o", o=1).broadcast_to([128, NT, C]), ALU.subtract)\
                   .then_inc(att["ln"], 1)
                dve.wait_ge(att["ln"], b * 5 + 3)
                dve.tensor_tensor(lns[:, :, :], lnx[:, :, :], lnx[:, :, :], ALU.mult).then_inc(att["ln"], 1)
                dve.wait_ge(att["ln"], b * 5 + 4)
                dve.tensor_reduce(lnv[:, 2, :], lns[:, :, :], AX_X, ALU.add).then_inc(att["ss"], 1)
                dve.wait_ge(att["ss"], b + 1)
                dve.tensor_scalar(lnv[:, 3, :], lnv[:, 2, :], 1.0 / C, 1e-5, ALU.mult, ALU.add).then_inc(att["ln"], 1)

            dve.wait_ge(att["xf"], B)
            dve.memset(pooled[C:C + 1, :, :], 1.0)
            mstep = [0]

            def mwait(ins):
                mstep[0] += 1
                ins.then_inc(moe["mk"], 1)
                dve.wait_ge(moe["mk"], mstep[0])

            for h in range(B // PB):
                for gg in range(2):
                    for n in range(0, NX, 2):
                        dve.wait_ge(moe["xft"], NX * (2 * h + gg) + n + 1)
                        dve.tensor_copy(xft[:, QC * n:QC * n + chunk_cols(n)], ps[:, n, 0:chunk_cols(n)])\
                           .then_inc(moe["xftc_v"], 1)
                dve.wait_ge(moe["logitc"], 2 * NK * (h + 1))
                dve.max(m8[:, :], lg[:, :]).then_inc(moe["top"], 1)
                dve.wait_ge(moe["top"], 2 * h + 1)
                dve.tensor_scalar(st[:, 0:1], m8[:, 0:1], -1.0, None, ALU.mult).then_inc(moe["top"], 1)
                mwait(dve.match_replace(mk[:, :], m8[:, :], lg[:, :], NEG))
                mwait(dve.tensor_tensor(mk[:, :], lg[:, :], mk[:, :], ALU.not_equal))
                dve.wait_ge(moe["exp"], h + 1)
                mwait(dve.reciprocal(st[:, 2:3], st[:, 1:2]))
                mwait(dve.scalar_tensor_tensor(mk[:, :], pe_[:, :], st[:, 2:3], mk[:, :], ALU.mult, ALU.mult))
                for n in range(0, NX, 2):
                    dve.wait_ge(moe["mt"], NX * h + n + 1)
                    k = len(chunk_tiles(n))
                    rows = tile_rows(4 * n)
                    dve.tensor_copy(mt[0:rows, 4 * n:4 * n + k, :].rearrange("p t n -> p (t n)"), ps[0:rows, n, 0:128 * k])\
                       .then_inc(moe["mtc_v"], 1)
                dve.wait_ge(moe["pool"], h + 1)
                for b in range(PB):
                    j, gg = b % GB, b // GB
                    last = dve.tensor_copy(pooled[0:C, :, b], ps[C * j:C * j + C, 7, 64 * gg + E * j:64 * gg + E * j + E])
                last.then_inc(moe["poolc"], 1)
                dve.wait_ge(moe["out"], h + 1)
                dve.tensor_copy(eo[:, :].rearrange("p (b e) -> p e b", b=PB),
                                ps[0:C, 1, 0:E * PB].rearrange("p (e b) -> p e b", e=E)).then_inc(moe["outc"], 1)
                dve.wait_ge(moe["outt"], h + 1)
                dve.tensor_tensor(bdo[:, :].rearrange("p (b c) -> p b c", b=PB), bcast(ps[:, 2, 0:C], PB),
                                  cv("blk8").rearrange("p (b o) -> p b o", o=1).broadcast_to([128, PB, C]), ALU.mult)\
                   .then_inc(moe["bdo"], 1)
                for t in range(NT):
                    rows = tile_rows(t)
                    dve.wait_ge(moe["scat"], NT * h + t + 1)
                    v = tok[0:rows, PB * h:PB * (h + 1), t, :]
                    dve.tensor_tensor(v, v, ps[0:rows, 3 + t % 4, 0:PB * C].rearrange("p (b c) -> p b c", b=PB), ALU.add)\
                       .then_inc(moe["add"], 1)

        @block.tensor
        def _(pe):
            def ident(n):
                return cv("ident", n)[:, 0:n]

            pe.wait_ge(s_cst, 16)
            pe.wait_ge(s_vec, VS_REP)
            for i in range(4):
                pe.transpose(ps[:, 4, C * i:C * (i + 1)], wsmall[0:C, i, :, :].rearrange("p j c -> p (j c)"), ident(C))
            pe.transpose(ps[:, 4, 128:128 + E], wsmall[0:E, 4, :, :].rearrange("p j c -> p (j c)"), ident(E))
            pe.transpose(ps[:, 5, 0:128], w1raw[:, :, :].rearrange("p j c -> p (j c)"), ident(128))
            pe.transpose(ps[:, 6, 0:C], w2raw[:, :], ident(C)).then_inc(s_wt, 1)
            pe.wait_ge(s_vec, VS_FOLD)
            for i in range(3):
                pe.matmul(ps[:, 4, i:i + 1], wbd[:, i, :], pv[:, B1N:B1N + 1], start=True, stop=True)
            pe.matmul(ps[:, 5, 0:1], w1t[0:C, :], pv[0:C, B2N:B2N + 1], start=True, stop=True).then_inc(s_wb, 1)
            pe.wait_ge(s_vec, VS_BV)
            pe.matmul(ps[:, 4, 3:4], wp[:, 256:384], bv[:, BV:BV + 1], start=True, stop=True).then_inc(s_wb, 1)
            pe.wait_ge(s_vec, VS_BV + 1)

            for g in range(G):
                pe.wait_ge(s_xorder, g + 1)
                for n in range(NK):
                    if g:
                        pe.wait_ge(s_xe, NK * (g - 1) + n + 1)
                    for j in range(4):
                        k = 4 * n + j
                        last = pe.transpose(ps[:, n, PI * j:PI * (j + 1)], xin2[:, g % 2, k].rearrange("p b c -> p (b c)"), ident(PI))
                    last.then_inc(s_xt, 1)

            pe.wait_ge(s_vec, VS_STAGE0)
            pe.wait_ge(s_clear, 4)

            def layer_norm(it, k, src):
                pe.matmul(ps[:, 7, 0:CT], cv("center"), src[:, :], start=True, stop=True).then_inc(conv["center"], 1)
                pe.wait_ge(conv["square"], it * 3 + k)
                pe.matmul(ps[:, 5, 0:CT], cv("mean"), sq[:, :], start=True, stop=True).then_inc(conv["var"], 1)

            def scores(it, u):
                if u:
                    pe.wait_ge(conv["bias"], it * NU + u)
                for hf in range(2):
                    w = slice(L * (2 * u + hf), L * (2 * u + hf + 1))
                    for j in range(GB):
                        last = pe.matmul(ps[64 * hf:64 * hf + L, j, 0:NH * L], qz[:, j, w], kz[:, :, w], start=True,
                                         stop=True)
                last.then_inc(conv["score"], 1)
                if u:
                    pe.wait_ge(conv["vcopy"], it * NU + u)
                for hf in range(2):
                    w = slice(L * (2 * u + hf), L * (2 * u + hf + 1))
                    for hh in range(2):
                        last = pe.matmul(ps[64 * hh:64 * hh + L, 7, 256 * hf:256 * hf + 256], xn[:, w],
                                         wv[:, hh, :, :].rearrange("p j n -> p (j n)"), start=True, stop=True)
                last.then_inc(conv["vprod"], 1)

            def transposes(it, u):
                i = u % 2
                pe.wait_ge(conv["prob"], it * NU + u + 1)
                for k in range(2):
                    pe.wait_ge(conv[("pcopy_a", "pcopy_b")[k]], it * NU + u)
                    for n in range(4):
                        m = 4 * k + n
                        last = pe.transpose(ps[:, 4 + k, 128 * n:128 * n + 113], pr[0:113, i, 128 * m:128 * m + 128],
                                            ident(113))
                    last.then_inc(conv["ptrans"], 1)

            def weighted_values(it, u):
                i = u % 2
                pe.wait_ge(conv["pcopy_a"], it * NU + u + 1)
                pe.wait_ge(conv["pcopy_b"], it * NU + u + 1)
                pe.wait_ge(conv["vcopy"], it * NU + u + 1)
                for hf in range(2):
                    for pair in range(2):
                        for j in range(GB):
                            w = 2 * u + hf
                            v = 256 * hf + 64 * j + C * pair
                            q = 113 * (2 * j + pair) + 64 * hf
                            last = pe.matmul(ps[C * j:C * (j + 1), 6, L * w:L * (w + 1)], vs[0:113, i, v:v + C],
                                             pt[0:113, i, q:q + L], start=(pair == 0), stop=(pair == 1),
                                             skip_group_check=True)
                last.then_inc(conv["av"], 1)

            with pe.Fori(0, G * NC) as it:
                pe.wait_ge(conv["xg"], it + 1)
                pe.wait_ge(conv["norm"], it * 3)
                layer_norm(it, 1, xg)
                pe.wait_ge(conv["norm"], it * 3 + 1)
                pe.matmul(ps[:, 4, 0:CT], wp[:, 0:128], xn[:, :], start=True, stop=True).then_inc(conv["qk"], 1)
                pe.matmul(ps[:, 5, 0:CT], wp[:, 128:256], xn[:, :], start=True, stop=True).then_inc(conv["qk"], 1)
                pe.wait_ge(conv["kz"], it + 1)
                scores(it, 0)
                for u in range(NU):
                    if u + 1 < NU:
                        scores(it, u + 1)
                    transposes(it, u)
                    weighted_values(it, u)
                pe.wait_ge(conv["oc"], it + 1)
                pe.matmul(ps[:, 4, 0:CT], wp[:, 256:384], oc[:, :], start=True, stop=True).then_inc(conv["oproj"], 1)
                pe.wait_ge(conv["o2"], it + 1)
                layer_norm(it, 2, o2)
                pe.wait_ge(conv["norm"], it * 3 + 2)
                for j in range(GB):
                    last = pe.matmul(ps[:, j, 0:CT], w1f[:, j, :], xn[:, :], start=True, stop=True)
                last.then_inc(conv["hid"], 1)
                pe.wait_ge(conv["gelu"], it + 1)
                for j in range(GB):
                    last = pe.matmul(ps[C * j:C * (j + 1), 6, 0:CT], w2t[:, :], gh[:, j, :], start=True, stop=True)
                last.then_inc(conv["y"], 1)
                pe.wait_ge(conv["t1"], it + 1)
                layer_norm(it, 3, t1)
            pe.wait_ge(conv["norm"], 3 * G * NC)

            with pe.Fori(0, B) as b:
                pe.wait_ge(att["load"], b * 32 + 32)
                for n in range(2 * NK):
                    w = wqr if n < NK else wkr
                    if n >= 2:
                        pe.wait_ge(att["lo"], b * (2 * NK) + n - 1)
                    pe.matmul(ps[0:96, 4 + n % 2, 0:KN], w[:, :, :].rearrange("p r c -> p (r c)"),
                              xr[:, KN * (n % NK):KN * (n % NK) + KN], start=True, stop=True).then_inc(att["prod"], 1)
                for t in range(NT):
                    rows = tile_rows(t)
                    pe.matmul(ps[0:rows, t // 7, 65 * (t % 7):65 * (t % 7) + 65], xr[:, T * t:T * t + rows], wva[:, :],
                              start=True, stop=True).then_inc(att["vprod"], 1)
                pe.wait_ge(att["lo"], b * (2 * NK) + 2 * NK)

                def first_pass(k):
                    t, n = k // NK, k % NK
                    rows = tile_rows(t)
                    if k >= 2:
                        pe.wait_ge(att["max1"], b * NP1 + k - 1)
                    pe.matmul(ps[0:rows, 4 + k % 2, 0:KN], q2[0:96, T * t:T * t + rows], k2[0:96, KN * n:KN * n + KN],
                              start=True, stop=True).then_inc(att["score1"], 1)

                def max_row(c):
                    pe.wait_ge(att["maxall"], b * NT + chunk_tiles(c)[-1] + 1)
                    pe.wait_ge(att["mcopy"], b * NQ + c)
                    for t in chunk_tiles(c):
                        rows, i = tile_rows(t), t % 4
                        last = pe.matmul(ps[96:97, 7, T * i:T * i + rows],
                                         mq[:, 4 * (c % 2) + i:4 * (c % 2) + i + 1], cv("negident")[:, 0:rows],
                                         start=True, stop=True)
                    last.then_inc(att["mrow"], 1)

                def second_pass(c, r):
                    at_, n = NG * c + r, chunk_cols(c)
                    if at_ >= 2:
                        pe.wait_ge(att["exp"], b * (NG * NQ) + at_ - 1)
                    for t in range(2 * r, min(2 * r + 2, NT)):
                        rows = tile_rows(t)
                        last = pe.matmul(ps[0:rows, 2 * (at_ % 2) + t % 2, 0:n], k2[0:97, T * t:T * t + rows],
                                         q2[0:97, QC * c:QC * c + n], start=True, stop=True)
                    last.then_inc(att["score2"], 1)

                def values(c, r):
                    at_ = NG * c + r
                    pe.wait_ge(att["rest"], b * (NG * NQ) + at_ + 1)
                    for t in range(2 * r, min(2 * r + 2, NT)):
                        for q in chunk_tiles(c):
                            rows, i = tile_rows(q), q % 4
                            at0 = QC * (t % 2) + T * i
                            o = ps[0:rows, 6, 65 * i:65 * i + 65]
                            pe.matmul(o, pk[:, at_ % 2, at0:at0 + rows].bitcast(BF16)[:, 1::2], vh[:, t, 0:65],
                                      start=(t == 0 and i == 0), stop=False, skip_group_check=True)
                            last = pe.matmul(o[:, 0:33], pl[:, at_ % 2, at0:at0 + rows], vh[:, t, 0:33],
                                             start=False, stop=(t == NT - 1), skip_group_check=True)
                    last.then_inc(att["av"], 1)

                for k in range(NK * len(chunk_tiles(0))):
                    first_pass(k)
                max_row(0)
                pe.wait_ge(att["vrest"], b + 1)
                for c in range(NQ):
                    todo = [NK * t + n for t in (chunk_tiles(c + 1) if c + 1 < NQ else ()) for n in range(NK)]
                    done = 0
                    pe.wait_ge(att["mcopy"], b * NQ + c + 1)
                    pe.wait_ge(att["o"], b * NQ + c)
                    for r in range(NG + 1):
                        if r < NG:
                            second_pass(c, r)
                        upto = len(todo) * min(r + 1, NG) // NG
                        for k in todo[done:upto]:
                            first_pass(k)
                        done = upto
                        if r:
                            values(c, r - 1)
                    if c + 1 < NQ:
                        max_row(c + 1)

            pe.wait_ge(att["xf"], B)
            for h in range(B // PB):
                for gg in range(2):
                    g = 2 * h + gg
                    if g == 2:
                        pe.wait_ge(moe["add"], NT)
                    for n in range(NX):
                        if gg:
                            pe.wait_ge(moe["xftc_v"], 4 * g)
                            pe.wait_ge(moe["xftc_a"], 3 * g)
                            pe.wait_ge(moe["logitc"], NK * g)
                        for t in chunk_tiles(n):
                            rows = tile_rows(t)
                            last = pe.transpose(ps[:, n, T * (t % 4):T * (t % 4) + rows], xf[0:rows, t, GB * g:GB * g + GB, :].rearrange("p b c -> p (b c)"),
                                                ident(rows))
                        last.then_inc(moe["xft"], 1)
                    pe.wait_ge(moe["xftc_v"], 4 * (g + 1))
                    pe.wait_ge(moe["xftc_a"], 3 * (g + 1))
                    for n in range(NK):
                        pe.wait_ge(moe["logitc"], NK * g + n)
                        pe.matmul(ps[64 * gg:64 * gg + 64, 7, 0:KN], wgate[:, :, :].rearrange("p j e -> p (j e)"),
                                  xft[:, KN * n:KN * n + KN], start=True, stop=True).then_inc(moe["logit"], 1)
                pe.wait_ge(moe["mk"], 4 * (h + 1))
                for n in range(NX):
                    for t in chunk_tiles(n):
                        rows = tile_rows(t)
                        last = pe.transpose(ps[0:rows, n, 128 * (t % 4):128 * (t % 4) + 128], mk[:, T * t:T * t + rows],
                                            ident(128))
                    last.then_inc(moe["mt"], 1)
                pe.wait_ge(moe["mtc_v"], 4 * (h + 1))
                pe.wait_ge(moe["mtc_a"], 3 * (h + 1))
                pe.wait_ge(moe["logitc"], 2 * NK * (h + 1))
                for gg in range(2):
                    g = 2 * h + gg
                    for t in range(NT):
                        rows = tile_rows(t)
                        last = pe.matmul(ps[:, 7, 64 * gg:64 * gg + 64], xf[0:rows, t, GB * g:GB * g + GB, :].rearrange("p b c -> p (b c)"),
                                         mt[0:rows, t, 64 * gg:64 * gg + 64], start=(t == 0), stop=(t == NT - 1))
                last.then_inc(moe["pool"], 1)
                pe.wait_ge(moe["poolc"], h + 1)
                for e in range(E):
                    last = pe.matmul(ps[:, 0, PB * e:PB * (e + 1)], w1e[:, e, :], pooled[:, e, :], start=True, stop=True)
                last.then_inc(moe["hid"], 1)
                pe.wait_ge(moe["gelu"], h + 1)
                for e in range(E):
                    o = ps[0:C, 1, PB * e:PB * (e + 1)]
                    pe.matmul(o, w2e[:, e, :], eh[:, PB * e:PB * (e + 1)], start=True, stop=False)
                    last = pe.matmul(o, w2b[:, e, :], cv("one", 1), start=False, stop=True)
                last.then_inc(moe["out"], 1)
                pe.wait_ge(moe["outc"], h + 1)
                pe.transpose(ps[:, 2, 0:C], eo[:, :], ident(C)).then_inc(moe["outt"], 1)
                pe.wait_ge(moe["bdo"], h + 1)
                for t in range(NT):
                    rows = tile_rows(t)
                    if t >= 4:
                        pe.wait_ge(moe["add"], NT * h + t - 3)
                    pe.matmul(ps[0:rows, 3 + t % 4, 0:PB * C], mk[:, T * t:T * t + rows], bdo[:, :], start=True, stop=True)\
                      .then_inc(moe["scat"], 1)


_INS = ["x", "L0_conv_norm1_g", "L0_conv_norm1_b", "L0_conv_qkv_w", "L0_conv_qkv_b", "L0_conv_out_w", "L0_conv_out_b",
        "L0_conv_pe_table", "L0_conv_norm2_g", "L0_conv_norm2_b", "L0_conv_mlp_w1", "L0_conv_mlp_b1", "L0_conv_mlp_w2",
        "L0_conv_mlp_b2", "L1_attn_Wq", "L1_attn_bq", "L1_attn_Wk", "L1_attn_bk", "L1_attn_Wv", "L1_attn_bv",
        "L1_ffn_gate_w", "L1_ffn_gate_b", "L1_ffn_weight1", "L1_ffn_weight2"]


def kernel(**inputs):
    import concourse.bacc as _bacc
    from concourse.bass_utils import run_bass_kernel_spmd as _run

    nc = _bacc.Bacc("TRN2", target_bir_lowering=False, num_devices=1)
    arrays, args = {}, {}
    for name in _INS:
        v = np.ascontiguousarray(inputs[name])
        arrays[f"in_{name}"] = v
        args[name] = nc.dram_tensor(f"in_{name}", v.shape, mybir.dt.from_np(v.dtype), kind="ExternalInput").ap()
    arrays["constants"] = shape_constants()
    cst = nc.dram_tensor("constants", (128, NCONST), F32, kind="ExternalInput").ap()
    out = nc.dram_tensor("result", (B, H, W, C), F32, kind="ExternalOutput").ap()
    conv_attention_moe(nc, args, cst, out)
    r = _run(nc, [arrays], core_ids=[0])
    return r.results[0]["result"]
```

```python
from contextlib import ExitStack

import numpy as np

import concourse.bass as bass
from concourse import mybir

F32 = mybir.dt.float32
F16 = mybir.dt.float16
BF16 = mybir.dt.bfloat16
ALU = mybir.AluOpType
ACT = mybir.ActivationFunctionType
AX_X = mybir.AxisListType.X

B, H, W, C = 16, 56, 56, 32
S = H * W
WS, SHIFT, NH = 7, 3, 4
HD = C // NH
HIDDEN = 4 * C
L = WS * WS
GB = 4
G = B // GB
NC = H // WS
CT = WS * W
NU = W // WS // 2
HALO = H + SHIFT
SP = W // 2
PI = S // SP
T = 128
NT = -(-S // T)
TL = S - (NT - 1) * T
KN = 448
NK = S // KN
QC = 4 * T
NQ = -(-S // QC)
E, TOP, EH = 16, 8, 128
DEPTH = 4
LAG = 3
PB = 8
NEG = -3.0e38
VS_REP, VS_FOLD, VS_BV = 1, 5, 6
VS_GN = VS_BV + 2 + 2 * G
VS_STAGE0 = VS_GN + 2

CONST = {}
_at = 0
for _n, _w in (("ident", 128), ("negident", 128), ("center", 128), ("mean", 128), ("vhead", 2 * C), ("blk4", GB),
               ("head4", NH), ("blk8", PB), ("lo_q", 1), ("lo_k", 1), ("one", 8), ("eps", 1)):
    CONST[_n] = (_at, _w)
    _at += _w
NCONST = _at


def shape_constants():
    p = np.arange(128)
    c = np.zeros((128, NCONST), np.float32)

    def put(name, value):
        at, w = CONST[name]
        c[:, at:at + w] = value

    same = (p[:, None] // C == p[None, :] // C).astype(np.float32)
    put("ident", np.eye(128))
    put("negident", -np.eye(128))
    put("mean", same / C)
    put("center", np.eye(128) - same / C)
    pair, ch = np.meshgrid(np.arange(2), np.arange(C), indexing="ij")
    put("vhead", (ch // HD).reshape(1, -1) == 2 * pair.reshape(1, -1) + p[:, None] // 64)
    put("blk4", p[:, None] // C == np.arange(GB)[None, :])
    put("head4", (p[:, None] % C) // HD == np.arange(NH)[None, :])
    put("blk8", p[:, None] // E == np.arange(PB)[None, :])
    put("lo_q", -(p[:, None] // C == 1).astype(np.float32))
    put("lo_k", -(p[:, None] // C == 2).astype(np.float32))
    put("one", 1.0)
    put("eps", 1e-5)
    return c


def conv_attention_moe(nc, a, cst_d, out):
    ctx = ExitStack()
    with ctx:
        ctx.enter_context(nc.allow_non_contiguous_dma("small weights, token rows"))

        def sb(name, shape, dt=F32):
            return ctx.enter_context(nc.sbuf_tensor(name, shape, dt))

        def sem(name):
            return ctx.enter_context(nc.semaphore(name))

        xa_d = nc.dram_tensor("xa_scratch", (B * C, S), F32, kind="Internal").ap()
        res_d = nc.dram_tensor("res_scratch", (B * C, S), F32, kind="Internal").ap()

        cst = sb("cst", [128, NCONST])
        wp = sb("wp", [128, 4 * 128])
        w1t = sb("w1t", [128, HIDDEN])
        w1f = sb("w1f", [128, GB, HIDDEN])
        w2t = sb("w2t", [128, C])
        wsmall = sb("wsmall", [128, 5, GB, C])
        w1raw = sb("w1raw", [128, GB, C])
        w2raw = sb("w2raw", [C, HIDDEN])
        wrep = sb("wrep", [128, 5, C])
        wbd = sb("wbd", [128, 3, 128])
        wsum = sb("wsum", [128, GB])
        wgate = sb("wgate", [128, GB, E])
        pv = sb("pv", [128, 16])
        bv = sb("bv", [128, 17])
        wqr = sb("wqr", [96, 3, C])
        wkr = sb("wkr", [96, 3, C])
        wva = sb("wva", [96, 65])
        gateb = sb("gateb", [128, 1])
        relb = sb("relb", [128, NH, L])
        relr = sb("relr", [128, NH, L])
        gn = sb("gn", [128, G, 4])
        bns = sb("bns", [128, NC, 6])
        mb = sb("mb", [128, 16])
        tok = sb("tok", [128, B, NT, C])
        ximg = sb("ximg", [128, G * HALO, W])
        xf = ximg[:, :, :].rearrange("p r c -> p (r c)")[:, 0:B * NT * C].rearrange(
            "p (t b c) -> p t b c", b=B, t=NT)
        ARENA = 21600
        arena = sb("arena", [128, ARENA])
        at = [0]

        def carve(n, parts=128):
            v = arena[0:parts, at[0]:at[0] + n]
            at[0] += n
            assert at[0] <= ARENA
            return v

        xin = carve(GB * SP * C, PI).rearrange("p (b n c) -> p b n c", b=GB, c=C)
        xin2 = carve(2 * GB * SP * C, PI).rearrange("p (i n b c) -> p i n b c", i=2, b=GB, c=C)
        at[0] = 0
        xg = carve(CT)
        sq = carve(CT)
        sd = carve(3 * CT).rearrange("p (k n) -> p k n", k=3)
        rs = carve(3 * CT).rearrange("p (k n) -> p k n", k=3)
        xn = carve(2 * CT).rearrange("p (i n) -> p i n", i=2)
        xn2 = carve(CT)
        qz = carve(GB * CT).rearrange("p (j n) -> p j n", j=GB)
        kz = carve(NH * CT).rearrange("p (h n) -> p h n", h=NH)
        sc = carve(2 * GB * NH * L).rearrange("p (i n) -> p i n", i=2)
        ex = carve(2 * GB * NH * L).rearrange("p (i n) -> p i n", i=2)
        pr = carve(2 * GB * NH * 64).rearrange("p (i n) -> p i n", i=2)
        mx = carve(4 * GB * NH).rearrange("p (i n) -> p i n", i=4)
        pt = carve(2 * 8 * 113).rearrange("p (i n) -> p i n", i=2)
        vs = carve(2 * GB * 128).rearrange("p (i n) -> p i n", i=2)
        oc = carve(CT)
        gh = carve(GB * CT).rearrange("p (j n) -> p j n", j=GB)
        t1 = carve(CT)
        xa = carve(CT)
        rt = carve(CT)
        at[0] = 0
        xr = carve(S, 96)
        q2 = [carve(S // 2).bitcast(F16) for _ in range(2)]
        k2 = [carve(S // 2).bitcast(F16) for _ in range(2)]
        hi = carve(KN).bitcast(F16).rearrange("p (i n) -> p i n", i=2)
        pk = carve(DEPTH * 2 * QC).rearrange("p (i n) -> p i n", i=DEPTH)
        pl = carve(DEPTH * QC).bitcast(F16).rearrange("p (i n) -> p i n", i=DEPTH)
        vh = [carve(NT * 33).bitcast(F16).rearrange("p (t n) -> p t n", t=NT) for _ in range(2)]
        res = [carve(NT * C).rearrange("p (t c) -> p t c", t=NT) for _ in range(2)]
        mxp = carve(4 * 8).rearrange("p (t n) -> p t n", t=4)
        mq = carve(8)
        rden = carve(8)
        oa = carve(2 * 4 * C).rearrange("p (i t c) -> p i t c", i=2, t=4)
        ob = carve(2 * 4 * C).rearrange("p (i t c) -> p i t c", i=2, t=4)
        lnc = carve(NT * C).rearrange("p (t c) -> p t c", t=NT)
        lnq = carve(NT * C).rearrange("p (t c) -> p t c", t=NT)
        lnv = carve(5 * NT).rearrange("p (i t) -> p i t", i=5)
        half = sb("half", [128, NT])
        at[0] = 0
        xft = carve(S)
        lg = carve(S)
        pe_ = carve(S)
        mk = carve(S)
        mt = carve(NT * 128).rearrange("p (t n) -> p t n", t=NT)
        bdo = carve(PB * C)
        m8 = carve(8)
        st = carve(8)
        pooled = carve(E * PB, C + 1).rearrange("p (e b) -> p e b", e=E)
        eh = carve(E * PB)
        eo = carve(E * PB, C)
        w1e = carve(E * EH, C + 1).rearrange("p (e h) -> p e h", e=E)
        w2e = carve(E * C).rearrange("p (e c) -> p e c", e=E)
        w2b = carve(E * C, 1).rearrange("p (e c) -> p e c", e=E)

        ps = ctx.enter_context(nc.psum_tensor("ps", [128, 8, 512], F32))

        def cv(name, parts=128, at_=0):
            o, w = CONST[name]
            return cst[at_:at_ + parts, o:o + w]

        G1, B1N, QB, KB, VB, OB, G2, B2N, M2B, M1B = range(10)
        BK, BV, BO, B1, BKH, BQM, SQM = 0, 1, 2, 3, 4, 8, 12

        s_cst = sem("constants_loaded")
        s_w = sem("weights_loaded")
        s_bias = sem("relative_bias_loaded")
        s_clear = sem("cleared")
        s_vec = sem("setup_vector_steps")
        s_wt = sem("weights_transposed")
        s_wb = sem("bias_products")
        s_xin = sem("input_loaded")
        s_xt = sem("input_transposed")
        s_xorder = sem("input_ordered")
        s_xe = sem("input_evacuated")
        s_gsd = sem("groupnorm_std")
        s_clear2 = sem("attention_cleared")
        s_pow = sem("pow_steps")
        conv = {n: sem("conv_" + n) for n in (
            "xg", "qz", "kz", "score", "vprod", "bias", "max", "sub", "exp", "sum", "rsum", "prob", "ptrans", "pcopy_a",
            "pcopy_b", "vcopy", "av", "oc", "hid", "gelu", "y", "t1", "rt", "stored")}
        ln = [{n: sem(f"norm{k + 1}_{n}") for n in ("center", "square", "var", "std", "rstd", "norm")} for k in range(3)]
        att = {n: sem("attn_" + n) for n in (
            "load", "prod", "hi", "vprod", "vcopy", "score1", "mxp", "maxall", "mrow", "mcopy", "score2", "exp",
            "av", "rden", "o", "tok", "ln", "ss", "xf", "ring", "rest_v", "rest_p", "sum")}
        moe = {n: sem("moe_" + n) for n in (
            "xft", "xftc_v", "xftc_a", "logit", "logitc", "top", "exp", "mk", "mt", "mtc_v", "mtc_a", "pool", "poolc",
            "hid", "gelu", "out", "outc", "outt", "bdo", "scat", "add", "weights", "stored")}
        block = ctx.enter_context(nc.Block())

        VB_, PT_, XB, YB, ZB = 2, 3, 5, 6, 7

        x_d = a["x"].rearrange("b h w c -> b (h w) c")
        out_d = out.rearrange("b h w c -> b (h w) c")

        def col(v):
            return v.rearrange("(n o) -> n o", o=1)


        def image(g, row, rows):
            return ximg[:, bass.ds(g * HALO + row, rows), :]

        def tile_rows(t):
            return T if t < NT - 1 else TL

        def chunk_tiles(c):
            return range(4 * c, min(4 * c + 4, NT))

        def chunk_cols(c):
            return min(QC, S - QC * c)

        steps2 = []
        for c in range(NQ - 1):
            for t in range(0, NT - 1, 2):
                steps2.append((c, [(t, 0), (t + 1, QC)], [(T, 0, 2, QC)]))
            steps2.append((c, [(NT - 1, 0)], [(TL, 0, 1, QC)]))
        per = QC // TL
        steps2.append((NQ - 1, [(t, TL * t) for t in range(2 * per)], [(T, 0, 2, QC)]))
        steps2.append((NQ - 1, [(t, TL * (t - 2 * per)) for t in range(2 * per, NT)], [(T, 0, 1, QC), (TL, 1, 1, TL)]))
        NSTEP = len(steps2)
        assert NT == 3 * per + 1 and NSTEP % DEPTH == 0
        first_of = [[x[0] for x in steps2].index(c) for c in range(NQ)]
        last_of = [first_of[c + 1] - 1 for c in range(NQ - 1)] + [NSTEP - 1]
        on_vector = [(x % 13) in (3, 7, 11) or x == NSTEP - 1 for x in range(NSTEP)]
        rests_v = [sum(on_vector[:x + 1]) for x in range(NSTEP)]
        rests_p = [x + 1 - rests_v[x] for x in range(NSTEP)]
        NV = -(-NT // 7)
        FP = NK * NT
        lead = [("proj", n) for n in range(2 * NK)] + [("value", n) for n in range(NV)] + \
               [("max", k) for k in range(NK * 4)]
        jobs = [("max", k) for k in range(NK * 4, FP)] + lead
        NJ = len(jobs)

        def jobs_until(x):
            ahead = 10
            if x <= ahead:
                return 28 * (x + 1) // (ahead + 1)
            return min(NJ, 28 + (NJ - 28) * (x - ahead) // (NSTEP - 4 - ahead))

        def jobs_at(x, last):
            part = range(jobs_until(x - 1) if x else 0, jobs_until(x))
            return [(j, *jobs[j]) for j in part if not (last and j >= FP - 28)]

        turn_at = {}
        for c in range(1, NQ):
            need = min(NK * 4 * (c + 1), FP) - 28
            turn_at[min(x for x in range(NSTEP) if jobs_until(x) >= need) + 1] = c
        turn_at[min(x for x in range(NSTEP) if jobs_until(x) >= NJ) + 1] = NQ
        assert all(x <= (first_of + [NSTEP])[c] - 1 for x, c in turn_at.items()) and len(turn_at) == NQ
        LN_AT = 8

        NX = -(-NT // 4)
        weights = 5 + 2 + 9 * GB + 1 + 12 + 2 + PB

        @block.sync
        def _(sp):
            sp.dma_start(cst[:, :], cst_d).then_inc(s_cst, 16)
            count = [0]

            def load(dst, src):
                sp.dma_start(dst, src).then_inc(s_w, 16)
                count[0] += 1

            def load_input(g):
                if g:
                    sp.wait_ge(s_xorder, g)
                sp.dma_start(xin.rearrange("p b n c -> p b (n c)"), x_d[GB * g:GB * (g + 1)].rearrange("b (p n) c -> p b (n c)", p=PI))\
                  .then_inc(s_xin, 16)

            load_input(0)
            for i in range(3):
                load(wsmall[0:C, i, 0, :], a["L0_conv_qkv_w"][C * i:C * (i + 1), :])
            load(wsmall[0:C, 3, 0, :], a["L0_conv_out_w"])
            load(wsmall[0:E, 4, 0, :], a["L1_ffn_gate_w"])
            load(w1raw[:, 0, :], a["L0_conv_mlp_w1"])
            load(w2raw[:, :], a["L0_conv_mlp_w2"])
            qkvb = a["L0_conv_qkv_b"]
            for k, v in ((G1, a["L0_conv_norm1_g"]), (B1N, a["L0_conv_norm1_b"]), (QB, qkvb[0:C]), (KB, qkvb[C:2 * C]),
                         (VB, qkvb[2 * C:3 * C]), (OB, a["L0_conv_out_b"]), (G2, a["L0_conv_norm2_g"]),
                         (B2N, a["L0_conv_norm2_b"]), (M2B, a["L0_conv_mlp_b2"])):
                for j in range(GB):
                    load(pv[C * j:C * (j + 1), k:k + 1], col(v))
            load(pv[:, M1B:M1B + 1], col(a["L0_conv_mlp_b1"]))
            sp.wait_ge(s_clear, 2)
            for r in range(3):
                load(wqr[0:C, r, :], a["L1_attn_Wq"])
                load(wqr[C:C + 1, r, :], a["L1_attn_bq"].rearrange("(o n) -> o n", o=1))
                load(wkr[0:C, r, :], a["L1_attn_Wk"])
                load(wkr[C:C + 1, r, :], a["L1_attn_bk"].rearrange("(o n) -> o n", o=1))
            load(wva[0:C, 0:C], a["L1_attn_Wv"])
            load(wva[C:C + 1, 0:C], a["L1_attn_bv"].rearrange("(o n) -> o n", o=1))
            for b in range(PB):
                load(gateb[E * b:E * (b + 1), :], col(a["L1_ffn_gate_b"]))
            assert count[0] == weights
            for g in range(1, G):
                load_input(g)
            xa_g = xa_d.rearrange("(g p) n -> g p n", g=G)
            res_g = res_d.rearrange("(g p) n -> g p n", g=G)
            with sp.Fori(0, G) as g:
                with sp.Fori(0, NC) as c:
                    it = g * NC + c
                    sp.wait_ge(conv["rt"], it + 1)
                    sp.dma_start(xa_g[bass.ds(g, 1), :, bass.ds(c * CT, CT)].rearrange("o p n -> (o p) n"), xa[:, :])\
                      .then_inc(conv["stored"], 16)
                    sp.dma_start(res_g[bass.ds(g, 1), :, bass.ds(c * CT, CT)].rearrange("o p n -> (o p) n"), rt[:, :])\
                      .then_inc(conv["stored"], 16)
            sp.wait_ge(conv["stored"], 32 * G * NC)
            xa_b = xa_d.rearrange("(b p) n -> b p n", b=B)
            res_b = res_d.rearrange("(b p) n -> b p n", b=B)
            sp.wait_ge(s_clear2, 1)
            def load_image(b):
                if isinstance(b, int):
                    xa_i, res_i = xa_b[b], res_b[b]
                else:
                    xa_i, res_i = (v[bass.ds(b, 1)].rearrange("o p n -> (o p) n") for v in (xa_b, res_b))
                sp.dma_start(xr[0:C, :], xa_i).then_inc(att["load"], 16)
                sp.dma_start(xr[2 * C:3 * C, :], res_i).then_inc(att["load"], 16)

            load_image(0)
            with sp.Fori(1, B) as b:
                sp.wait_ge(att["vprod"], b * NV)
                load_image(b)
            sp.wait_ge(att["xf"], B + 1)
            sp.dma_start(w1e, a["L1_ffn_weight1"].rearrange("e d h -> d e h")).then_inc(moe["weights"], 16)
            sp.dma_start(w2e, a["L1_ffn_weight2"][:, 0:EH, :].rearrange("e h o -> h e o")).then_inc(moe["weights"], 16)
            sp.dma_start(w2b, a["L1_ffn_weight2"][:, EH:EH + 1, :].rearrange("e h o -> h e o")).then_inc(moe["weights"], 16)
            for h in range(B // PB):
                sp.wait_ge(moe["add"], NT * (h + 1))
                for k in range(PB * h, PB * (h + 1)):
                    b = (k - 1) % B
                    sp.dma_start(out_d[b, 0:(NT - 1) * T, :].rearrange("(t p) c -> p t c", p=T), tok[:, k, 0:NT - 1, :])\
                      .then_inc(moe["stored"], 16)
                    sp.dma_start(out_d[b, (NT - 1) * T:S, :], tok[0:TL, k, NT - 1, :]).then_inc(moe["stored"], 16)
            sp.wait_ge(moe["stored"], 32 * B)

        @block.gpsimd
        def _(pool):
            pool.memset(relr[:, :, :], 0.0).then_inc(s_clear, 1)
            pool.memset(wva[:, :], 0.0)
            pool.memset(wqr[:, :, :], 0.0)
            pool.memset(wkr[:, :, :], 0.0).then_inc(s_clear, 1)
            pool.memset(half[:, :], -0.5).then_inc(s_clear, 1)
            pool.memset(tok[:, 0, :, :], 0.0).then_inc(s_clear, 1)
            pool.memset(tok[:, 1:B, NT - 1, :], 0.0).then_inc(s_clear, 1)
            pool.wait_ge(s_clear, 5)

            def subtract(v, u):
                i = u % 2
                pool.wait_ge(conv["max"], v + 1)
                s3 = sc[0:113, i, :].rearrange("p (m k) -> p m k", k=L)
                pool.tensor_tensor(s3, s3, mx[0:113, i, :].rearrange("p (m o) -> p m o", o=1)
                                   .broadcast_to([113, GB * NH, L]), ALU.subtract).then_inc(conv["sub"], 1)

            def probabilities(v, u):
                i = u % 2
                pool.wait_ge(conv["rsum"], v + 1)
                pool.tensor_tensor(pr[0:113, i, :].rearrange("p (m k) -> p m k", k=64)[:, :, 0:L],
                                   ex[0:113, i, :].rearrange("p (m k) -> p m k", k=L),
                                   mx[0:113, 2 + i, :].rearrange("p (m o) -> p m o", o=1)
                                   .broadcast_to([113, GB * NH, L]), ALU.mult).then_inc(conv["prob"], 1)

            def residual(n):
                pool.wait_ge(ln[2]["norm"], n + 1)
                if not (isinstance(n, int) and n == 0):
                    pool.wait_ge(conv["stored"], n * 32)
                pool.tensor_tensor(rt[:, :], t1[:, :], xa[:, :], ALU.add).then_inc(conv["rt"], 1)

            def chunk(it, post=True, pre=True):
                for u in range(NU):
                    v = it * NU + u
                    if u + 1 < NU or pre:
                        probabilities(v + 1, u + 1)
                    if u == 0 and post:
                        residual(it - 2)
                    if u + 2 < NU or pre:
                        subtract(v + 2, u + 2)

            subtract(0, 0)
            probabilities(0, 0)
            subtract(1, 1)
            chunk(0, post=False)
            chunk(1, post=False)
            with pool.Fori(0, G * NC // 2 - 2) as i:
                chunk(i * 2 + 2)
                chunk(i * 2 + 3)
            chunk(G * NC - 2)
            chunk(G * NC - 1, pre=False)
            residual(G * NC - 2)
            residual(G * NC - 1)

            def slot(b):
                return 0 if isinstance(b, int) and b == B - 1 else b + 1

            def tokens(b, p, c):
                k, rows = len(chunk_tiles(c)), tile_rows(4 * c)
                i = (NQ * p + c) % 2
                pool.wait_ge(att["o"], b * NQ + c + 1)
                pool.tensor_tensor(oa[0:rows, i, 0:k, :], oa[0:rows, i, 0:k, :], ob[0:rows, i, 0:k, :], ALU.add)\
                    .then_inc(att["sum"], 1)
                pool.wait_ge(att["sum"], b * NQ + c + 1)
                pool.tensor_tensor(tok[0:rows, bass.ds(slot(b), 1), 4 * c:4 * c + k, :].rearrange("p o t c -> p (o t) c"),
                                   oa[0:rows, i, 0:k, :], res[p][0:rows, 4 * c:4 * c + k, :], ALU.add)\
                    .then_inc(att["tok"], 1)

            def normalize_slot(b):
                k = 0 if isinstance(b, int) and b == B else b
                pool.wait_ge(att["ln"], b * 5 + 5)
                pool.tensor_tensor(lnv[:, 4, :], lnv[:, 3, :], half[:, :], ALU.pow).then_inc(s_pow, 1)
                pool.wait_ge(s_pow, b + 1)
                pool.tensor_tensor(xf[:, :, bass.ds(k, 1), :].rearrange("p t o c -> p (t o) c"), lnc[:, :, :],
                                   lnv[:, 4, :].rearrange("p (t o) -> p t o", o=1).broadcast_to([128, NT, C]),
                                   ALU.mult).then_inc(att["xf"], 1)

            def rest(b, x):
                pool.wait_ge(att["exp"], b * NSTEP + x + 1)
                for rows, bank, k, n in steps2[x][2]:
                    full = pk[0:rows, x % DEPTH, QC * bank:QC * (bank + k)]
                    last = pool.tensor_tensor(
                        pl[0:rows, x % DEPTH, QC * bank:QC * (bank + k)].rearrange("p (k n) -> p k n", k=k)[:, :, 0:n],
                        full.rearrange("p (k n) -> p k n", k=k)[:, :, 0:n],
                        full.bitcast(BF16).rearrange("p (k n s) -> p k n s", k=k, s=2)[:, :, 0:n, 1], ALU.subtract)
                last.then_inc(att["rest_p"], 1)

            def image_steps(b, p):
                for x in range(NSTEP):
                    if not on_vector[x]:
                        rest(b, x)
                    if x == LN_AT + 4:
                        normalize_slot(b)
                    for c in range(NQ):
                        if min(last_of[c] + LAG, NSTEP - 1) == x:
                            tokens(b, p, c)

            with pool.Fori(0, B // 2 - 1) as i:
                image_steps(i * 2, 0)
                image_steps(i * 2 + 1, 1)
            image_steps(B - 2, 0)
            image_steps(B - 1, 1)
            normalize_slot(B)

        @block.scalar
        def _(act):
            tab = a["L0_conv_pe_table"].rearrange("h (y x) -> h y x", x=2 * WS - 1)
            act.wait_ge(s_clear, 2)
            for hf in range(2):
                for qy in range(WS):
                    for qx in range(WS):
                        p = 64 * hf + WS * qy + qx
                        act.dma_start(relr[p:p + 1, :, :].rearrange("p h (y x) -> p h y x", x=WS),
                                      tab[:, qy:qy + WS, qx:qx + WS].rearrange("h y (o x) -> o h y x", o=1))\
                           .then_inc(s_bias, 16)
            for g in range(G):
                act.wait_ge(s_xin, 16 * (g + 1))
                if g >= 2:
                    act.wait_ge(s_xt, NK * (g - 1))
                act.activation(xin2[:, g % 2], xin.rearrange("p b n c -> p n b c"), ACT.Copy).then_inc(s_xorder, 1)
            act.wait_ge(s_vec, VS_GN)
            act.activation(gn[:, :, 2], gn[:, :, 1], ACT.Sqrt, bias=cv("eps")[:, 0:1]).then_inc(s_gsd, 1)


            def square(n, k, bank, bias=None):
                act.wait_ge(ln[k]["center"], n + 1)
                if bias is None:
                    act.activation(sq[:, :], ps[:, bank, 0:CT], ACT.Square).then_inc(ln[k]["square"], 1)
                else:
                    act.activation(sq[:, :], ps[:, bank, 0:CT], ACT.Square, bias=bias).then_inc(ln[k]["square"], 1)

            def root(n, k):
                act.wait_ge(ln[k]["var"], n + 1)
                act.activation(sd[:, k, :], ps[:, ZB, 0:CT], ACT.Sqrt, bias=cv("eps")[:, 0:1]).then_inc(ln[k]["std"], 1)

            def exponentials(v, u):
                act.wait_ge(conv["sub"], v + 1)
                act.activation(ex[0:113, u % 2, :], sc[0:113, u % 2, :], ACT.Exp).then_inc(conv["exp"], 1)

            def probs_a(v, u):
                act.wait_ge(conv["ptrans"], 2 * v + 1)
                act.activation(pt[:, u % 2, 0:4 * 113].rearrange("p (n q) -> p n q", q=113),
                               ps[:, PT_, :].rearrange("p (n q) -> p n q", q=128)[:, :, 0:113], ACT.Copy)\
                   .then_inc(conv["pcopy_a"], 1)

            def weighted_copy(v, u):
                act.wait_ge(conv["av"], v + 1)
                at_ = 4 * C * 2 + 2 * L * (u % 2)
                act.activation(oc[:, :].rearrange("p (r w c) -> p w r c", r=WS, c=WS)[:, 2 * u:2 * u + 2],
                               ps[:, VB_, at_:at_ + 2 * L].rearrange("p (w r c) -> p w r c", r=WS, c=WS), ACT.Copy)\
                   .then_inc(conv["oc"], 1)

            def queries(n):
                act.wait_ge(conv["qz"], n * 2 + 1)
                for j in range(GB):
                    act.activation(qz[:, j, :], ps[:, YB, 0:CT], ACT.Identity, bias=bv[:, BQM + j:BQM + j + 1],
                                   scale=bv[:, SQM + j:SQM + j + 1])

            def keys(n):
                act.wait_ge(conv["qz"], n * 2 + 2)
                for h in range(NH):
                    last = act.activation(kz[:, h, :], ps[:, ZB, 0:CT], ACT.Identity, bias=bv[:, BKH + h:BKH + h + 1],
                                          scale=cv("head4")[:, h:h + 1])
                last.then_inc(conv["kz"], 1)

            def gelu(n, j):
                act.wait_ge(conv["hid"], n * GB + j + 1)
                act.activation(gh[:, j, :], ps[:, (XB, XB, XB, YB)[j], 0:CT], ACT.Gelu, bias=bv[:, B1:B1 + 1])\
                   .then_inc(conv["gelu"], 1)

            def chunk(it, post=True, pre=True):
                v, n = it * NU, it - 1
                if post:
                    weighted_copy(v - 1, NU - 1)
                    square(n, 1, XB, bv[:, BO:BO + 1])
                probs_a(v, 0)
                exponentials(v + 1, 1)
                if post:
                    root(n, 1)
                if pre:
                    square(it + 1, 0, YB)
                weighted_copy(v, 0)
                if pre:
                    root(it + 1, 0)
                probs_a(v + 1, 1)
                exponentials(v + 2, 2)
                if post:
                    gelu(n, 0)
                weighted_copy(v + 1, 1)
                if post:
                    gelu(n, 1)
                if pre:
                    queries(it + 1)
                probs_a(v + 2, 2)
                if pre:
                    keys(it + 1)
                exponentials(v + 3, 3)
                weighted_copy(v + 2, 2)
                if post:
                    gelu(n, 2)
                    gelu(n, 3)
                    square(n, 2, YB)
                probs_a(v + 3, 3)
                if pre:
                    exponentials(v + 4, 0)
                if post:
                    root(n, 2)

            square(0, 0, YB)
            root(0, 0)
            queries(0)
            keys(0)
            exponentials(0, 0)
            chunk(0, post=False)
            chunk(1)
            with act.Fori(0, G * NC // 2 - 2) as i:
                chunk(i * 2 + 2)
                chunk(i * 2 + 3)
            chunk(G * NC - 2)
            chunk(G * NC - 1, pre=False)
            weighted_copy(G * NC * NU - 1, NU - 1)
            square(G * NC - 1, 1, XB, bv[:, BO:BO + 1])
            root(G * NC - 1, 1)
            for j in range(GB):
                gelu(G * NC - 1, j)
            square(G * NC - 1, 2, YB)
            root(G * NC - 1, 2)

            def split_or_copy(b, kind, n, j):
                bank = 4 + j % 2
                if kind == "proj":
                    act.wait_ge(att["prod"], b * (2 * NK) + n + 1)
                    act.activation(hi[0:96, n % 2, :], ps[0:96, bank, 0:KN], ACT.Copy).then_inc(att["hi"], 1)
                elif kind == "value":
                    p = par(b)
                    act.wait_ge(att["vprod"], b * NV + n + 1)
                    k = min(7, NT - 7 * n)
                    if n == NV - 1:
                        k -= 1
                        src = ps[0:TL, bank, 65 * k:65 * (k + 1)]
                        act.activation(vh[p][0:TL, NT - 1, 0:C + 1], src[:, 0:C + 1], ACT.Copy)
                        act.activation(res[p][0:TL, NT - 1, :], src[:, C + 1:65], ACT.Copy)
                    src = ps[:, bank, 0:65 * k].rearrange("p (t n) -> p t n", n=65)
                    act.activation(vh[p][:, 7 * n:7 * n + k, 0:C + 1], src[:, :, 0:C + 1], ACT.Copy)
                    act.activation(res[p][:, 7 * n:7 * n + k, :], src[:, :, C + 1:65], ACT.Copy).then_inc(att["vcopy"], 1)

            def max_row(b, p, c):
                n = chunk_cols(c)
                act.wait_ge(att["mrow"], b * NQ + c + 1)
                act.activation(q2[p][96:97, QC * c:QC * c + n], ps[96:97, 7, 0:n], ACT.Copy).then_inc(att["mcopy"], 1)

            def image_steps(b, p, last):
                par_of[0] = p
                for x in range(NSTEP):
                    if x in turn_at and not (last and turn_at[x] == NQ):
                        if turn_at[x] == NQ:
                            max_row(b + 1, 1 - p, 0)
                        else:
                            max_row(b, p, turn_at[x])
                    act.wait_ge(att["score2"], b * NSTEP + x + 1)
                    if x >= DEPTH:
                        act.wait_ge(att["av"], b * NSTEP + x - DEPTH + 1)
                    for rows, bank, k, n in steps2[x][2]:
                        e = act.activation(
                            pk[0:rows, x % DEPTH, QC * bank:QC * (bank + k)].rearrange("p (k n) -> p k n", k=k)[:, :, 0:n],
                            ps[0:rows, 2 * (x % 2) + bank:2 * (x % 2) + bank + k, 0:n], ACT.Exp, scale=float(C) ** -0.5)
                    e.then_inc(att["exp"], 1)
                    for j, kind, n in jobs_at(x, last):
                        if kind != "max":
                            split_or_copy(b + 1, kind, n, j + NJ * p)

            par_of = [1]

            def par(b):
                return 1 - par_of[0]

            for j, (kind, n) in enumerate(lead):
                split_or_copy(0, kind, n, j)
            max_row(0, 0, 0)
            with act.Fori(0, B // 2 - 1) as i:
                image_steps(i * 2, 0, False)
                image_steps(i * 2 + 1, 1, False)
            image_steps(B - 2, 0, False)
            image_steps(B - 1, 1, True)

            for h in range(B // PB):
                for gg in range(2):
                    for n in range(1, NX, 2):
                        act.wait_ge(moe["xft"], NX * (2 * h + gg) + n + 1)
                        act.activation(xft[:, QC * n:QC * n + chunk_cols(n)], ps[:, n, 0:chunk_cols(n)], ACT.Copy)\
                           .then_inc(moe["xftc_a"], 1)
                    for n in range(NK):
                        act.wait_ge(moe["logit"], NK * (2 * h + gg) + n + 1)
                        act.activation(lg[64 * gg:64 * gg + 64, KN * n:KN * n + KN], ps[64 * gg:64 * gg + 64, 7, 0:KN],
                                       ACT.Identity, bias=gateb[64 * gg:64 * gg + 64, 0:1]).then_inc(moe["logitc"], 1)
                act.wait_ge(moe["top"], 2 * h + 2)
                act.activation(pe_[:, :], lg[:, :], ACT.Exp, bias=st[:, 0:1], accum_out=st[:, 1:2]).then_inc(moe["exp"], 1)
                for n in range(1, NX, 2):
                    act.wait_ge(moe["mt"], NX * h + n + 1)
                    k = len(chunk_tiles(n))
                    act.activation(mt[:, 4 * n:4 * n + k, :].rearrange("p t n -> p (t n)"), ps[:, n, 0:128 * k], ACT.Copy)\
                       .then_inc(moe["mtc_a"], 1)
                act.wait_ge(moe["hid"], h + 1)
                act.activation(eh[:, :], ps[:, 0, 0:E * PB], ACT.Gelu).then_inc(moe["gelu"], 1)

        @block.vector
        def _(dve):
            steps = [0]

            def step(ins, wait=True):
                steps[0] += 1
                ins.then_inc(s_vec, 1)
                if wait:
                    dve.wait_ge(s_vec, steps[0])

            def bcast(v, n):
                return v.rearrange("p (o c) -> p o c", o=1).broadcast_to([v.shape[0], n, v.shape[1]])

            dve.wait_ge(s_cst, 16)
            dve.wait_ge(s_w, 16 * weights)
            dve.memset(ps[:, 0:4, :], 0.0)
            for i in range(4):
                dve.tensor_copy(wsmall[0:C, i, 1:GB, :], bcast(wsmall[0:C, i, 0, :], GB - 1))
            dve.tensor_copy(wsmall[0:E, 4, 1:GB, :], bcast(wsmall[0:E, 4, 0, :], GB - 1))
            step(dve.tensor_copy(w1raw[:, 1:GB, :], bcast(w1raw[:, 0, :], GB - 1)))
            assert steps[0] == VS_REP
            dve.wait_ge(s_wt, 1)
            dve.tensor_copy(wrep[:, 0:4, :], ps[:, 4, 0:128].rearrange("p (i c) -> p i c", i=4))
            dve.tensor_copy(wrep[:, 4, 0:E], ps[:, 4, 128:128 + E])
            dve.tensor_copy(w1t[:, :], ps[:, 5, 0:128])
            step(dve.tensor_copy(w2t[:, :], ps[:, 6, 0:C]))

            def mask(name, n):
                return cv(name).rearrange("p (j o) -> p j o", o=1).broadcast_to([128, GB, n])

            for i in range(3):
                dve.tensor_tensor(wbd[:, i, :].rearrange("p (j c) -> p j c", j=GB), bcast(wrep[:, i, :], GB), mask("blk4", C),
                                  ALU.mult)
            dve.tensor_tensor(wp[:, 256:384].rearrange("p (j c) -> p j c", j=GB), bcast(wrep[:, 3, :], GB), mask("blk4", C),
                              ALU.mult)
            dve.tensor_tensor(wgate[:, :, :], bcast(wrep[:, 4, 0:E], GB), mask("blk4", E), ALU.mult)
            for j in range(GB):
                dve.tensor_scalar(w1f[:, j, :], w1t[:, :], pv[:, G2:G2 + 1], cv("blk4")[:, j:j + 1], ALU.mult, ALU.mult)
            step(dve.tensor_copy(wva[64:96, C + 1:65], cv("ident", 32, 64)[:, 64:96]))
            wo = wp[:, 256:384].rearrange("p (j c) -> p j c", j=GB)
            dve.tensor_reduce(wsum[:, :], wo, AX_X, ALU.add)
            step(dve.memset(wva[C:C + 1, C:C + 1], 1.0))
            dve.scalar_tensor_tensor(wo, wsum[:, :].rearrange("p (j o) -> p j o", o=1).broadcast_to([128, GB, C]),
                                     -1.0 / C, wo, ALU.mult, ALU.add)
            dve.tensor_scalar(wp[:, 384:512], wbd[:, 2, :], pv[:, G1:G1 + 1], None, ALU.mult)
            step(dve.tensor_scalar(wp[:, 0:256], wbd[:, 0:2, :].rearrange("p i c -> p (i c)"), pv[:, G1:G1 + 1], None,
                                   ALU.mult))
            assert steps[0] == VS_FOLD
            dve.wait_ge(s_wb, 1)
            dve.tensor_scalar(bv[:, 16:17], ps[:, 4, 0:1], pv[:, QB:QB + 1], float(HD) ** -0.5, ALU.add, ALU.mult)
            dve.tensor_scalar(bv[:, SQM:SQM + GB], cv("blk4"), float(HD) ** -0.5, None, ALU.mult)
            dve.tensor_scalar(bv[:, BK:BK + 1], ps[:, 4, 1:2], pv[:, KB:KB + 1], None, ALU.add)
            dve.tensor_scalar(bv[:, B1:B1 + 1], ps[:, 5, 0:1], pv[:, M1B:M1B + 1], None, ALU.add)
            step(dve.tensor_scalar(bv[:, BV:BV + 1], ps[:, 4, 2:3], pv[:, VB:VB + 1], None, ALU.add))
            assert steps[0] == VS_BV
            dve.tensor_scalar(bv[:, BQM:BQM + GB], cv("blk4"), bv[:, 16:17], None, ALU.mult)
            dve.tensor_scalar(bv[:, BKH:BKH + NH], cv("head4"), bv[:, BK:BK + 1], None, ALU.mult)
            dve.wait_ge(s_wb, 2)
            step(dve.tensor_copy(bv[:, BO:BO + 1], ps[:, 4, 3:4]))
            dve.wait_ge(s_bias, 16 * 2 * L)
            step(dve.tensor_copy(relb[:, :, :], relr[:, :, ::-1]))

            for g in range(G):
                img = ximg[:, g * HALO:(g + 1) * HALO, :].rearrange("p r c -> p (r c)")
                for n in range(NK):
                    dve.wait_ge(s_xt, NK * g + n + 1)
                    dve.tensor_copy(img[:, SHIFT * W:].rearrange("p (q j) -> p j q", j=SP)[:, 4 * n:4 * n + 4, :],
                                    ps[:, n, 0:KN].rearrange("p (j q) -> p j q", j=4)).then_inc(s_xe, 1)
                dve.wait_ge(s_xe, NK * (g + 1))
                dve.tensor_copy(img[:, 0:SHIFT * W], img[:, H * W:HALO * W])
                for c in range(NC):
                    last = dve.bn_stats(bns[:, c, :], img[:, SHIFT * W + CT * c:SHIFT * W + CT * (c + 1)])
                step(last)
                step(dve.bn_aggr(gn[:, g, 0:2], bns[:, :, :].rearrange("p c s -> p (c s)")))
            assert steps[0] == VS_GN
            dve.wait_ge(s_gsd, 1)
            step(dve.reciprocal(gn[:, :, 3], gn[:, :, 2]))
            dve.memset(pr[:, :, :], 0.0)
            step(dve.memset(ps[:, 0:VB_ + 1, :], 0.0))
            assert steps[0] == VS_STAGE0

            def place(n):
                return n // NC, n % NC

            def group_norm(n):
                g, c = place(n)
                mean = gn[:, bass.ds(g, 1), 0]
                rstd = gn[:, bass.ds(g, 1), 3]
                xg3 = xg[:, :].rearrange("p (r c) -> p r c", c=W)
                src = image(g, c * WS, WS)
                dve.tensor_scalar(xg3[:, :, SHIFT:W], src[:, :, 0:W - SHIFT], mean, rstd, ALU.subtract, ALU.mult)
                dve.tensor_scalar(xg3[:, :, 0:SHIFT], src[:, :, W - SHIFT:W], mean, rstd, ALU.subtract, ALU.mult)\
                   .then_inc(conv["xg"], 1)

            def bias_and_max(v, u):
                i = u % 2
                dve.wait_ge(conv["score"], v + 1)
                dve.tensor_tensor(sc[0:113, i, :].rearrange("p (b j n) -> p b j n", b=2, j=2),
                                  ps[0:113, 0:2, 0:2 * NH * L].rearrange("p b (j n) -> p b j n", j=2),
                                  relb[0:113, :, :].rearrange("p (b j h) k -> p b j (h k)", b=1, j=1)
                                  .broadcast_to([113, 2, 2, NH * L]), ALU.add).then_inc(conv["bias"], 1)
                dve.wait_ge(conv["bias"], v + 1)
                dve.tensor_reduce(mx[0:113, i, :], sc[0:113, i, :].rearrange("p (m k) -> p m k", k=L), AX_X, ALU.max)\
                   .then_inc(conv["max"], 1)

            def sums(v, u):
                i = u % 2
                dve.wait_ge(conv["exp"], v + 1)
                dve.tensor_reduce(mx[0:113, 2 + i, :], ex[0:113, i, :].rearrange("p (m k) -> p m k", k=L), AX_X, ALU.add)\
                   .then_inc(conv["sum"], 1)
                dve.wait_ge(conv["sum"], v + 1)
                dve.reciprocal(mx[0:113, 2 + i, :], mx[0:113, 2 + i, :]).then_inc(conv["rsum"], 1)

            def probs_b(v, u):
                dve.wait_ge(conv["ptrans"], 2 * v + 2)
                dve.tensor_copy(pt[:, u % 2, 4 * 113:8 * 113].rearrange("p (n q) -> p n q", q=113),
                                ps[:, PT_ + 1, :].rearrange("p (n q) -> p n q", q=128)[:, :, 0:113])\
                   .then_inc(conv["pcopy_b"], 1)

            def values_copy(v, u):
                dve.wait_ge(conv["vprod"], v + 1)
                dve.tensor_tensor(vs[0:113, u % 2, :].rearrange("p (m a c) -> p m a c", a=2, c=C),
                                  ps[0:113, VB_, 0:2 * GB * C].rearrange("p (m a c) -> p m a c", a=1, c=C)
                                  .broadcast_to([113, 2 * GB, 2, C]),
                                  cv("vhead", 113).rearrange("p (m a c) -> p m a c", m=1, a=2)
                                  .broadcast_to([113, 2 * GB, 2, C]), ALU.mult).then_inc(conv["vcopy"], 1)

            def normalize(n, k, bank, dst):
                dve.wait_ge(ln[k]["std"], n + 1)
                dve.reciprocal(rs[:, k, :], sd[:, k, :]).then_inc(ln[k]["rstd"], 1)
                dve.wait_ge(ln[k]["rstd"], n + 1)
                src = ps[:, bank, 0:CT]
                if k == 0:
                    def rows(v):
                        return v.rearrange("p (r w c) -> p r w c", r=WS, c=WS)
                    last = dve.tensor_tensor(dst.rearrange("p (w r c) -> p r w c", r=WS, c=WS), rows(src),
                                             rows(rs[:, k, :]), ALU.mult)
                elif k == 1:
                    last = dve.scalar_tensor_tensor(dst, src, bv[:, BO:BO + 1], rs[:, k, :], ALU.add, ALU.mult)
                else:
                    last = dve.tensor_tensor(dst, src, rs[:, k, :], ALU.mult)
                last.then_inc(ln[k]["norm"], 1)

            def attention_norm(n):
                if not (isinstance(n, int) and n == 0):
                    dve.wait_ge(conv["stored"], n * 32)
                normalize(n, 2, YB, xa[:, :])

            def skip_connection(n):
                g, c = place(n)
                if not (isinstance(n, int) and n == 0):
                    dve.wait_ge(conv["rt"], n)
                dve.wait_ge(conv["y"], n + 1)
                dve.scalar_tensor_tensor(t1[:, :], ps[:, ZB, 0:CT], pv[:, M2B:M2B + 1],
                                         image(g, c * WS + SHIFT, WS).rearrange("p r c -> p (r c)"), ALU.add, ALU.add)\
                   .then_inc(conv["t1"], 1)

            def chunk(it, p, post=True, pre=True, norm=True):
                v, n = it * NU, it - 1
                values_copy(v + 1, 1)
                if pre:
                    group_norm(it + 1)
                if norm:
                    attention_norm(it - 2)
                probs_b(v, 0)
                sums(v + 1, 1)
                bias_and_max(v + 2, 2)
                if post:
                    normalize(n, 1, XB, xn2[:, :])
                values_copy(v + 2, 2)
                probs_b(v + 1, 1)
                if pre:
                    normalize(it + 1, 0, YB, xn[:, 1 - p, :])
                sums(v + 2, 2)
                bias_and_max(v + 3, 3)
                values_copy(v + 3, 3)
                probs_b(v + 2, 2)
                sums(v + 3, 3)
                if pre:
                    bias_and_max(v + 4, 0)
                if post:
                    skip_connection(n)
                if pre:
                    values_copy(v + 4, 0)
                probs_b(v + 3, 3)
                if pre:
                    sums(v + 4, 0)
                    bias_and_max(v + 5, 1)

            group_norm(0)
            normalize(0, 0, YB, xn[:, 0, :])
            bias_and_max(0, 0)
            values_copy(0, 0)
            sums(0, 0)
            bias_and_max(1, 1)
            chunk(0, 0, post=False, norm=False)
            chunk(1, 1, norm=False)
            with dve.Fori(0, G * NC // 2 - 2) as i:
                chunk(i * 2 + 2, 0)
                chunk(i * 2 + 3, 1)
            chunk(G * NC - 2, 0)
            chunk(G * NC - 1, 1, pre=False)
            attention_norm(G * NC - 2)
            normalize(G * NC - 1, 1, XB, xn2[:, :])
            skip_connection(G * NC - 1)
            attention_norm(G * NC - 1)

            dve.wait_ge(conv["stored"], 32 * G * NC)
            dve.memset(xr[32:64, :], 0.0).then_inc(s_vec, 1)
            dve.wait_ge(s_vec, VS_STAGE0 + 1)
            dve.memset(xr[32:33, :], 1.0)
            for p in range(2):
                dve.memset(vh[p][:, NT - 1, :], 0.0)
                last = dve.memset(k2[p][96:97, :], 1.0)
            last.then_inc(s_clear2, 1)
            def consume(b, p, kind, n, j, done):
                bank = 4 + j % 2
                if kind == "proj":
                    dst, m = (q2[p], "lo_q") if n < NK else (k2[p], "lo_k")
                    cols = slice(KN * (n % NK), KN * (n % NK) + KN)
                    dve.wait_ge(att["hi"], b * (2 * NK) + n + 1)
                    dve.scalar_tensor_tensor(dst[0:96, cols], hi[0:96, n % 2, :], cv(m, 96), ps[0:96, bank, 0:KN],
                                             ALU.mult, ALU.add).then_inc(att["ring"], 1)
                elif kind == "value":
                    dve.wait_ge(att["vcopy"], b * NV + n + 1)
                    k = min(7, NT - 7 * n)
                    if n == NV - 1:
                        k -= 1
                        dve.tensor_tensor(vh[p][0:TL, NT - 1, 33:65], ps[0:TL, bank, 65 * k:65 * k + C],
                                          vh[p][0:TL, NT - 1, 0:C], ALU.subtract)
                    dve.tensor_tensor(vh[p][:, 7 * n:7 * n + k, 33:65],
                                      ps[:, bank, 0:65 * k].rearrange("p (t n) -> p t n", n=65)[:, :, 0:C],
                                      vh[p][:, 7 * n:7 * n + k, 0:C], ALU.subtract).then_inc(att["ring"], 1)
                else:
                    t, m = n // NK, n % NK
                    c = t // 4
                    rows, i = tile_rows(t), t % 4
                    dve.wait_ge(att["score1"], b * FP + n + 1)
                    dve.tensor_reduce(mxp[0:rows, i, m:m + 1], ps[0:rows, bank, 0:KN], AX_X, ALU.max)\
                       .then_inc(att["ring"], 1)
                    if m == NK - 1:
                        dve.wait_ge(att["ring"], done)
                        at_ = 4 * ((NQ * p + c) % 2) + i
                        dve.tensor_reduce(mq[0:rows, at_:at_ + 1], mxp[0:rows, i, 0:NK], AX_X, ALU.max)\
                           .then_inc(att["maxall"], 1)

            def rest(b, x):
                dve.wait_ge(att["exp"], b * NSTEP + x + 1)
                for rows, bank, k, n in steps2[x][2]:
                    full = pk[0:rows, x % DEPTH, QC * bank:QC * (bank + k)]
                    last = dve.tensor_tensor(
                        pl[0:rows, x % DEPTH, QC * bank:QC * (bank + k)].rearrange("p (k n) -> p k n", k=k)[:, :, 0:n],
                        full.rearrange("p (k n) -> p k n", k=k)[:, :, 0:n],
                        full.bitcast(BF16).rearrange("p (k n s) -> p k n s", k=k, s=2)[:, :, 0:n, 1], ALU.subtract)
                last.then_inc(att["rest_v"], 1)

            def weighted(b, p, c):
                k, rows = len(chunk_tiles(c)), tile_rows(4 * c)
                i = (NQ * p + c) % 2
                o4 = ps[0:rows, 6, 0:65 * k].rearrange("p (t n) -> p t n", n=65)
                dve.wait_ge(att["av"], b * NSTEP + last_of[c] + 1)
                if c >= 1:
                    dve.wait_ge(att["tok"], b * NQ + c - 1)
                dve.reciprocal(rden[0:rows, 0:k], o4[:, :, C]).then_inc(att["rden"], 1)
                dve.wait_ge(att["rden"], b * NQ + c + 1)
                rd = rden[0:rows, 0:k].rearrange("p (t o) -> p t o", o=1).broadcast_to([rows, k, C])
                dve.tensor_tensor(oa[0:rows, i, 0:k, :], o4[:, :, 0:C], rd, ALU.mult)
                dve.tensor_tensor(ob[0:rows, i, 0:k, :], o4[:, :, 33:65], rd, ALU.mult).then_inc(att["o"], 1)

            def center_slot(b):
                k = 0 if isinstance(b, int) and b == B else b
                tb = tok[:, bass.ds(k, 1), :, :].rearrange("p o t c -> p (o t) c")
                dve.wait_ge(att["tok"], b * NQ)
                dve.wait_ge(att["xf"], b)
                dve.tensor_reduce(lnv[:, 0, :], tb, AX_X, ALU.add).then_inc(att["ln"], 1)
                dve.wait_ge(att["ln"], b * 5 + 1)
                dve.tensor_scalar(lnv[:, 1, :], lnv[:, 0, :], 1.0 / C, None, ALU.mult).then_inc(att["ln"], 1)
                dve.wait_ge(att["ln"], b * 5 + 2)
                dve.tensor_tensor(lnc[:, :, :], tb,
                                  lnv[:, 1, :].rearrange("p (t o) -> p t o", o=1).broadcast_to([128, NT, C]), ALU.subtract)\
                   .then_inc(att["ln"], 1)
                dve.wait_ge(att["ln"], b * 5 + 3)
                dve.tensor_tensor(lnq[:, :, :], lnc[:, :, :], lnc[:, :, :], ALU.mult).then_inc(att["ln"], 1)
                dve.wait_ge(att["ln"], b * 5 + 4)
                dve.tensor_reduce(lnv[:, 2, :], lnq[:, :, :], AX_X, ALU.add).then_inc(att["ss"], 1)
                dve.wait_ge(att["ss"], b + 1)
                dve.tensor_scalar(lnv[:, 3, :], lnv[:, 2, :], 1.0 / C, 1e-5, ALU.mult, ALU.add).then_inc(att["ln"], 1)

            def image_steps(b, p, last):
                for x in range(NSTEP):
                    for j, kind, n in jobs_at(x, last):
                        ahead = j >= FP - 28
                        consume(b + 1 if ahead else b, 1 - p if ahead else p, kind, n, j + NJ * p,
                                b * NJ + len(lead) + j + 1)
                    if on_vector[x]:
                        rest(b, x)
                    if x == LN_AT:
                        center_slot(b)
                    for c in range(NQ):
                        if min(last_of[c] + LAG, NSTEP - 1) == x:
                            weighted(b, p, c)

            for j, (kind, n) in enumerate(lead):
                consume(0, 0, kind, n, j, j + 1)
            with dve.Fori(0, B // 2 - 1) as i:
                image_steps(i * 2, 0, False)
                image_steps(i * 2 + 1, 1, False)
            image_steps(B - 2, 0, False)
            image_steps(B - 1, 1, True)
            center_slot(B)

            dve.wait_ge(att["xf"], B + 1)
            dve.memset(pooled[C:C + 1, :, :], 1.0)
            mstep = [0]

            def mwait(ins):
                mstep[0] += 1
                ins.then_inc(moe["mk"], 1)
                dve.wait_ge(moe["mk"], mstep[0])

            for h in range(B // PB):
                for gg in range(2):
                    for n in range(0, NX, 2):
                        dve.wait_ge(moe["xft"], NX * (2 * h + gg) + n + 1)
                        dve.tensor_copy(xft[:, QC * n:QC * n + chunk_cols(n)], ps[:, n, 0:chunk_cols(n)])\
                           .then_inc(moe["xftc_v"], 1)
                dve.wait_ge(moe["logitc"], 2 * NK * (h + 1))
                dve.max(m8[:, :], lg[:, :]).then_inc(moe["top"], 1)
                dve.wait_ge(moe["top"], 2 * h + 1)
                dve.tensor_scalar(st[:, 0:1], m8[:, 0:1], -1.0, None, ALU.mult).then_inc(moe["top"], 1)
                mwait(dve.match_replace(mk[:, :], m8[:, :], lg[:, :], NEG))
                mwait(dve.tensor_tensor(mk[:, :], lg[:, :], mk[:, :], ALU.not_equal))
                dve.wait_ge(moe["exp"], h + 1)
                mwait(dve.reciprocal(st[:, 2:3], st[:, 1:2]))
                mwait(dve.scalar_tensor_tensor(mk[:, :], pe_[:, :], st[:, 2:3], mk[:, :], ALU.mult, ALU.mult))
                for n in range(0, NX, 2):
                    dve.wait_ge(moe["mt"], NX * h + n + 1)
                    k = len(chunk_tiles(n))
                    rows = tile_rows(4 * n)
                    dve.tensor_copy(mt[0:rows, 4 * n:4 * n + k, :].rearrange("p t n -> p (t n)"), ps[0:rows, n, 0:128 * k])\
                       .then_inc(moe["mtc_v"], 1)
                dve.wait_ge(moe["pool"], h + 1)
                for b in range(PB):
                    j, gg = b % GB, b // GB
                    last = dve.tensor_copy(pooled[0:C, :, b], ps[C * j:C * j + C, 7, 64 * gg + E * j:64 * gg + E * j + E])
                last.then_inc(moe["poolc"], 1)
                dve.wait_ge(moe["out"], h + 1)
                dve.tensor_copy(eo[:, :].rearrange("p (b e) -> p e b", b=PB),
                                ps[0:C, 1, 0:E * PB].rearrange("p (e b) -> p e b", e=E)).then_inc(moe["outc"], 1)
                dve.wait_ge(moe["outt"], h + 1)
                dve.tensor_tensor(bdo[:, :].rearrange("p (b c) -> p b c", b=PB), bcast(ps[:, 2, 0:C], PB),
                                  cv("blk8").rearrange("p (b o) -> p b o", o=1).broadcast_to([128, PB, C]), ALU.mult)\
                   .then_inc(moe["bdo"], 1)
                for t in range(NT):
                    rows = tile_rows(t)
                    dve.wait_ge(moe["scat"], NT * h + t + 1)
                    v = tok[0:rows, PB * h:PB * (h + 1), t, :]
                    dve.tensor_tensor(v, v, ps[0:rows, 3 + t % 4, 0:PB * C].rearrange("p (b c) -> p b c", b=PB), ALU.add)\
                       .then_inc(moe["add"], 1)

        @block.tensor
        def _(pe):
            def ident(n):
                return cv("ident", n)[:, 0:n]

            pe.wait_ge(s_cst, 16)
            pe.wait_ge(s_vec, VS_REP)
            for i in range(4):
                pe.transpose(ps[:, 4, C * i:C * (i + 1)], wsmall[0:C, i, :, :].rearrange("p j c -> p (j c)"), ident(C))
            pe.transpose(ps[:, 4, 128:128 + E], wsmall[0:E, 4, :, :].rearrange("p j c -> p (j c)"), ident(E))
            pe.transpose(ps[:, 5, 0:128], w1raw[:, :, :].rearrange("p j c -> p (j c)"), ident(128))
            pe.transpose(ps[:, 6, 0:C], w2raw[:, :], ident(C)).then_inc(s_wt, 1)
            pe.wait_ge(s_vec, VS_FOLD)
            for i in range(3):
                pe.matmul(ps[:, 4, i:i + 1], wbd[:, i, :], pv[:, B1N:B1N + 1], start=True, stop=True)
            pe.matmul(ps[:, 5, 0:1], w1t[0:C, :], pv[0:C, B2N:B2N + 1], start=True, stop=True).then_inc(s_wb, 1)
            pe.wait_ge(s_vec, VS_BV)
            pe.matmul(ps[:, 4, 3:4], wp[:, 256:384], bv[:, BV:BV + 1], start=True, stop=False)
            pe.matmul(ps[:, 4, 3:4], cv("center"), pv[:, OB:OB + 1], start=False, stop=True).then_inc(s_wb, 1)
            pe.wait_ge(s_vec, VS_BV + 1)

            for g in range(G):
                pe.wait_ge(s_xorder, g + 1)
                for n in range(NK):
                    if g:
                        pe.wait_ge(s_xe, NK * (g - 1) + n + 1)
                    for j in range(4):
                        k = 4 * n + j
                        last = pe.transpose(ps[:, n, PI * j:PI * (j + 1)], xin2[:, g % 2, k].rearrange("p b c -> p (b c)"), ident(PI))
                    last.then_inc(s_xt, 1)

            pe.wait_ge(s_vec, VS_STAGE0)
            pe.wait_ge(s_clear, 5)

            def variance(n, k):
                pe.wait_ge(ln[k]["square"], n + 1)
                pe.matmul(ps[:, ZB, 0:CT], cv("mean"), sq[:, :], start=True, stop=True).then_inc(ln[k]["var"], 1)

            def scores(v, u):
                if not (isinstance(v, int) and v == 0):
                    pe.wait_ge(conv["bias"], v)
                for hf in range(2):
                    w = slice(L * (2 * u + hf), L * (2 * u + hf + 1))
                    for j in range(GB):
                        last = pe.matmul(ps[64 * hf:64 * hf + L, j // 2, NH * L * (j % 2):NH * L * (j % 2 + 1)],
                                         qz[:, j, w], kz[:, :, w], start=True, stop=True)
                last.then_inc(conv["score"], 1)

            def values(v, u, p):
                if not (isinstance(v, int) and v < 2):
                    pe.wait_ge(conv["oc"], v - 1)
                elif v == 1:
                    pe.wait_ge(conv["vcopy"], 1)
                for hf in range(2):
                    w = slice(L * (2 * u + hf), L * (2 * u + hf + 1))
                    for hh in range(2):
                        last = pe.matmul(ps[64 * hh:64 * hh + L, VB_, 128 * hf:128 * hf + 128], xn[:, p, w],
                                         wp[:, 384:512], start=True, stop=True)
                last.then_inc(conv["vprod"], 1)

            def transposes(v, u):
                i = u % 2
                pe.wait_ge(conv["prob"], v + 1)
                for k in range(2):
                    if not (isinstance(v, int) and v == 0):
                        pe.wait_ge(conv[("pcopy_a", "pcopy_b")[k]], v)
                    for n in range(4):
                        m = 4 * k + n
                        last = pe.transpose(ps[:, PT_ + k, 128 * n:128 * n + 113], pr[0:113, i, 128 * m:128 * m + 128],
                                            ident(113))
                    last.then_inc(conv["ptrans"], 1)

            def weighted_values(v, u, more):
                i = u % 2
                pe.wait_ge(conv["pcopy_a"], v + 1)
                pe.wait_ge(conv["pcopy_b"], v + 1)
                pe.wait_ge(conv["vcopy"], v + 1 + more)
                for hf in range(2):
                    for pair in range(2):
                        for j in range(GB):
                            w = 2 * (u % 2) + hf
                            s_ = 256 * hf + 64 * j + C * pair
                            q = 113 * (2 * j + pair) + 64 * hf
                            last = pe.matmul(ps[C * j:C * (j + 1), VB_, 2 * GB * C + L * w:2 * GB * C + L * (w + 1)],
                                             vs[0:113, i, s_:s_ + C], pt[0:113, i, q:q + L], start=(pair == 0),
                                             stop=(pair == 1), skip_group_check=True)
                last.then_inc(conv["av"], 1)

            def out_projection(n):
                pe.wait_ge(conv["oc"], n * NU + NU)
                pe.matmul(ps[:, XB, 0:CT], wp[:, 256:384], oc[:, :], start=True, stop=True).then_inc(ln[1]["center"], 1)

            def hidden(n, j):
                pe.wait_ge(ln[1]["norm"], n + 1)
                if j in (1, 2):
                    pe.wait_ge(conv["gelu"], n * GB + j)
                pe.matmul(ps[:, (XB, XB, XB, YB)[j], 0:CT], w1f[:, j, :], xn2[:, :], start=True, stop=True)\
                  .then_inc(conv["hid"], 1)

            def mlp_out(n):
                for j in range(GB):
                    pe.wait_ge(conv["gelu"], n * GB + j + 1)
                    last = pe.matmul(ps[C * j:C * (j + 1), ZB, 0:CT], w2t[:, :], gh[:, j, :], start=True, stop=True)
                last.then_inc(conv["y"], 1)

            def center_window(n):
                pe.wait_ge(conv["xg"], n + 1)
                pe.matmul(ps[:, YB, 0:CT], cv("center"), xg[:, :], start=True, stop=True).then_inc(ln[0]["center"], 1)

            def center_sum(n):
                pe.wait_ge(conv["t1"], n + 1)
                pe.matmul(ps[:, YB, 0:CT], cv("center"), t1[:, :], start=True, stop=True).then_inc(ln[2]["center"], 1)

            def project(n, p):
                pe.wait_ge(ln[0]["norm"], n + 1)
                pe.matmul(ps[:, YB, 0:CT], wp[:, 0:128], xn[:, p, :], start=True, stop=True).then_inc(conv["qz"], 1)
                pe.matmul(ps[:, ZB, 0:CT], wp[:, 128:256], xn[:, p, :], start=True, stop=True).then_inc(conv["qz"], 1)

            def chunk(it, p, post=True, pre=True, norm=True):
                v, n = it * NU, it - 1
                if post:
                    out_projection(n)
                values(v + 1, 1, p)
                transposes(v, 0)
                if post:
                    if norm:
                        pe.wait_ge(ln[2]["std"], n)
                    variance(n, 1)
                scores(v + 2, 2)
                if pre:
                    if norm:
                        pe.wait_ge(ln[2]["norm"], n)
                    center_window(it + 1)
                weighted_values(v, 0, 1)
                if pre:
                    if post:
                        pe.wait_ge(ln[1]["std"], n + 1)
                    variance(it + 1, 0)
                values(v + 2, 2, p)
                transposes(v + 1, 1)
                if post:
                    hidden(n, 0)
                scores(v + 3, 3)
                weighted_values(v + 1, 1, 1)
                if pre:
                    project(it + 1, 1 - p)
                if post:
                    hidden(n, 1)
                values(v + 3, 3, p)
                transposes(v + 2, 2)
                weighted_values(v + 2, 2, 1)
                if post:
                    hidden(n, 2)
                if pre:
                    pe.wait_ge(conv["kz"], it + 2)
                    scores(v + 4, 0)
                elif norm:
                    pe.wait_ge(ln[2]["norm"], n)
                if post:
                    hidden(n, 3)
                    mlp_out(n)
                if pre:
                    values(v + 4, 0, 1 - p)
                if post:
                    center_sum(n)
                transposes(v + 3, 3)
                if post:
                    variance(n, 2)
                if pre:
                    scores(v + 5, 1)
                weighted_values(v + 3, 3, int(pre))

            center_window(0)
            variance(0, 0)
            project(0, 0)
            pe.wait_ge(conv["kz"], 1)
            scores(0, 0)
            values(0, 0, 0)
            scores(1, 1)
            chunk(0, 0, post=False, norm=False)
            chunk(1, 1, norm=False)
            with pe.Fori(0, G * NC // 2 - 2) as i:
                chunk(i * 2 + 2, 0)
                chunk(i * 2 + 3, 1)
            chunk(G * NC - 2, 0)
            chunk(G * NC - 1, 1, pre=False)
            n = G * NC - 1
            out_projection(n)
            pe.wait_ge(ln[2]["std"], n)
            variance(n, 1)
            for j in range(GB):
                if j == 3:
                    pe.wait_ge(ln[2]["norm"], n)
                hidden(n, j)
            mlp_out(n)
            center_sum(n)
            variance(n, 2)
            pe.wait_ge(ln[2]["norm"], G * NC)

            def produce(b, p, kind, n, j, done):
                bank = 4 + j % 2
                if not (isinstance(done, int) and done <= 0):
                    pe.wait_ge(att["ring"], done)
                if kind == "proj":
                    if n == 0:
                        pe.wait_ge(att["load"], b * 32 + 32)
                    w = wqr if n < NK else wkr
                    pe.matmul(ps[0:96, bank, 0:KN], w[:, :, :].rearrange("p r c -> p (r c)"),
                              xr[:, KN * (n % NK):KN * (n % NK) + KN], start=True, stop=True).then_inc(att["prod"], 1)
                elif kind == "value":
                    for t in range(7 * n, min(7 * n + 7, NT)):
                        rows = tile_rows(t)
                        last = pe.matmul(ps[0:rows, bank, 65 * (t % 7):65 * (t % 7) + 65], xr[:, T * t:T * t + rows],
                                         wva[:, :], start=True, stop=True)
                    last.then_inc(att["vprod"], 1)
                else:
                    t, m = n // NK, n % NK
                    rows = tile_rows(t)
                    pe.matmul(ps[0:rows, bank, 0:KN], q2[p][0:96, T * t:T * t + rows], k2[p][0:96, KN * m:KN * m + KN],
                              start=True, stop=True).then_inc(att["score1"], 1)

            def max_row(b, p, c):
                pe.wait_ge(att["maxall"], b * NT + chunk_tiles(c)[-1] + 1)
                if not (isinstance(b, int) and b == 0 and c == 0):
                    pe.wait_ge(att["mcopy"], b * NQ + c)
                for t in chunk_tiles(c):
                    rows, i = tile_rows(t), t % 4
                    at_ = 4 * ((NQ * p + c) % 2) + i
                    last = pe.matmul(ps[96:97, 7, T * i:T * i + rows], mq[:, at_:at_ + 1], cv("negident")[:, 0:rows],
                                     start=True, stop=True)
                last.then_inc(att["mrow"], 1)

            def second_pass(b, p, x):
                c, tiles, _ = steps2[x]
                n = chunk_cols(c)
                if x == first_of[c]:
                    pe.wait_ge(att["mcopy"], b * NQ + c + 1)
                if x >= 2:
                    pe.wait_ge(att["exp"], b * NSTEP + x - 1)
                for t, at_ in tiles:
                    rows = tile_rows(t)
                    last = pe.matmul(ps[0:rows, 2 * (x % 2) + at_ // QC, at_ % QC:at_ % QC + n],
                                     k2[p][0:97, T * t:T * t + rows], q2[p][0:97, QC * c:QC * c + n], start=True, stop=True)
                last.then_inc(att["score2"], 1)

            def values(b, p, x):
                c, tiles, _ = steps2[x]
                if rests_v[x]:
                    pe.wait_ge(att["rest_v"], b * rests_v[-1] + rests_v[x])
                if rests_p[x]:
                    pe.wait_ge(att["rest_p"], b * rests_p[-1] + rests_p[x])
                if x == first_of[c] and c:
                    pe.wait_ge(att["o"], b * NQ + c)
                for t, at_ in tiles:
                    for q in chunk_tiles(c):
                        rows, i = tile_rows(q), q % 4
                        o = ps[0:rows, 6, 65 * i:65 * i + 65]
                        cols = slice(at_ + T * i, at_ + T * i + rows)
                        pe.matmul(o, pk[:, x % DEPTH, cols].bitcast(BF16)[:, 1::2], vh[p][:, t, 0:65],
                                  start=(t == 0 and i == 0), stop=False, skip_group_check=True)
                        last = pe.matmul(o[:, 0:33], pl[:, x % DEPTH, cols], vh[p][:, t, 0:33], start=False,
                                         stop=(t == NT - 1), skip_group_check=True)
                last.then_inc(att["av"], 1)

            def image_steps(b, p, last):
                for x in range(NSTEP + LAG):
                    if x < NSTEP:
                        if x in turn_at and not (last and turn_at[x] == NQ):
                            if turn_at[x] == NQ:
                                max_row(b + 1, 1 - p, 0)
                            else:
                                max_row(b, p, turn_at[x])
                        second_pass(b, p, x)
                        for j, kind, n in jobs_at(x, last):
                            ahead = j >= FP - 28
                            produce(b + 1 if ahead else b, 1 - p if ahead else p, kind, n, j + NJ * p,
                                    b * NJ + len(lead) + j - 1)
                    if x >= LAG:
                        if x == LAG:
                            pe.wait_ge(att["o"], b * NQ)
                        values(b, p, x - LAG)

            pe.wait_ge(s_clear2, 1)
            for j, (kind, n) in enumerate(lead):
                produce(0, 0, kind, n, j, j - 1)
            max_row(0, 0, 0)
            with pe.Fori(0, B // 2 - 1) as i:
                image_steps(i * 2, 0, False)
                image_steps(i * 2 + 1, 1, False)
            image_steps(B - 2, 0, False)
            image_steps(B - 1, 1, True)

            pe.wait_ge(att["xf"], B + 1)
            for h in range(B // PB):
                for gg in range(2):
                    g = 2 * h + gg
                    if g == 2:
                        pe.wait_ge(moe["add"], NT)
                    for n in range(NX):
                        if gg:
                            pe.wait_ge(moe["xftc_v"], 4 * g)
                            pe.wait_ge(moe["xftc_a"], 3 * g)
                            pe.wait_ge(moe["logitc"], NK * g)
                        for t in chunk_tiles(n):
                            rows = tile_rows(t)
                            last = pe.transpose(ps[:, n, T * (t % 4):T * (t % 4) + rows], xf[0:rows, t, GB * g:GB * g + GB, :].rearrange("p b c -> p (b c)"),
                                                ident(rows))
                        last.then_inc(moe["xft"], 1)
                    pe.wait_ge(moe["xftc_v"], 4 * (g + 1))
                    pe.wait_ge(moe["xftc_a"], 3 * (g + 1))
                    for n in range(NK):
                        pe.wait_ge(moe["logitc"], NK * g + n)
                        pe.matmul(ps[64 * gg:64 * gg + 64, 7, 0:KN], wgate[:, :, :].rearrange("p j e -> p (j e)"),
                                  xft[:, KN * n:KN * n + KN], start=True, stop=True).then_inc(moe["logit"], 1)
                pe.wait_ge(moe["mk"], 4 * (h + 1))
                for n in range(NX):
                    for t in chunk_tiles(n):
                        rows = tile_rows(t)
                        last = pe.transpose(ps[0:rows, n, 128 * (t % 4):128 * (t % 4) + 128], mk[:, T * t:T * t + rows],
                                            ident(128))
                    last.then_inc(moe["mt"], 1)
                pe.wait_ge(moe["mtc_v"], 4 * (h + 1))
                pe.wait_ge(moe["mtc_a"], 3 * (h + 1))
                pe.wait_ge(moe["logitc"], 2 * NK * (h + 1))
                for gg in range(2):
                    g = 2 * h + gg
                    for t in range(NT):
                        rows = tile_rows(t)
                        last = pe.matmul(ps[:, 7, 64 * gg:64 * gg + 64], xf[0:rows, t, GB * g:GB * g + GB, :].rearrange("p b c -> p (b c)"),
                                         mt[0:rows, t, 64 * gg:64 * gg + 64], start=(t == 0), stop=(t == NT - 1))
                last.then_inc(moe["pool"], 1)
                pe.wait_ge(moe["poolc"], h + 1)
                pe.wait_ge(moe["weights"], 48)
                for e in range(E):
                    last = pe.matmul(ps[:, 0, PB * e:PB * (e + 1)], w1e[:, e, :], pooled[:, e, :], start=True, stop=True)
                last.then_inc(moe["hid"], 1)
                pe.wait_ge(moe["gelu"], h + 1)
                for e in range(E):
                    o = ps[0:C, 1, PB * e:PB * (e + 1)]
                    pe.matmul(o, w2e[:, e, :], eh[:, PB * e:PB * (e + 1)], start=True, stop=False)
                    last = pe.matmul(o, w2b[:, e, :], cv("one", 1), start=False, stop=True)
                last.then_inc(moe["out"], 1)
                pe.wait_ge(moe["outc"], h + 1)
                pe.transpose(ps[:, 2, 0:C], eo[:, :], ident(C)).then_inc(moe["outt"], 1)
                pe.wait_ge(moe["bdo"], h + 1)
                for t in range(NT):
                    rows = tile_rows(t)
                    if t >= 4:
                        pe.wait_ge(moe["add"], NT * h + t - 3)
                    pe.matmul(ps[0:rows, 3 + t % 4, 0:PB * C], mk[:, T * t:T * t + rows], bdo[:, :], start=True, stop=True)\
                      .then_inc(moe["scat"], 1)


_INS = ["x", "L0_conv_norm1_g", "L0_conv_norm1_b", "L0_conv_qkv_w", "L0_conv_qkv_b", "L0_conv_out_w", "L0_conv_out_b",
        "L0_conv_pe_table", "L0_conv_norm2_g", "L0_conv_norm2_b", "L0_conv_mlp_w1", "L0_conv_mlp_b1", "L0_conv_mlp_w2",
        "L0_conv_mlp_b2", "L1_attn_Wq", "L1_attn_bq", "L1_attn_Wk", "L1_attn_bk", "L1_attn_Wv", "L1_attn_bv",
        "L1_ffn_gate_w", "L1_ffn_gate_b", "L1_ffn_weight1", "L1_ffn_weight2"]


def kernel(**inputs):
    import concourse.bacc as _bacc
    from concourse.bass_utils import run_bass_kernel_spmd as _run

    nc = _bacc.Bacc("TRN2", target_bir_lowering=False, num_devices=1)
    arrays, args = {}, {}
    for name in _INS:
        v = np.ascontiguousarray(inputs[name])
        arrays[f"in_{name}"] = v
        args[name] = nc.dram_tensor(f"in_{name}", v.shape, mybir.dt.from_np(v.dtype), kind="ExternalInput").ap()
    arrays["constants"] = shape_constants()
    cst = nc.dram_tensor("constants", (128, NCONST), F32, kind="ExternalInput").ap()
    out = nc.dram_tensor("result", (B, H, W, C), F32, kind="ExternalOutput").ap()
    conv_attention_moe(nc, args, cst, out)
    r = _run(nc, [arrays], core_ids=[0])
    return r.results[0]["result"]
```

```python
from contextlib import ExitStack

import numpy as np

import concourse.bass as bass
from concourse import mybir

F32 = mybir.dt.float32
F16 = mybir.dt.float16
ALU = mybir.AluOpType
ACT = mybir.ActivationFunctionType
AX_X = mybir.AxisListType.X

B, H, W, C = 16, 56, 56, 32
S = H * W
WS, SHIFT, NH = 7, 3, 4
HD = C // NH
HIDDEN = 4 * C
L = WS * WS
GB = 4
G = B // GB
NC = H // WS
CT = WS * W
NU = W // WS // 2
HALO = H + SHIFT
SP = W // 2
PI = S // SP
T = 128
NT = -(-S // T)
TL = S - (NT - 1) * T
KN = 448
NK = S // KN
QC = 4 * T
NQ = -(-S // QC)
E, TOP, EH = 16, 8, 128
DEPTH = 4
LAG = 2
PB = 8
NEG = -3.0e38
VS_GN = 2 * G
VS_REP = VS_GN + 2
VS_FOLD = VS_REP + 4
VS_BV = VS_FOLD + 1
VS_STAGE0 = VS_BV + 2

CONST = {}
_at = 0
for _n, _w in (("ident", 128), ("negident", 128), ("center", 128), ("mean", 128), ("vhead", 2 * C), ("blk4", GB),
               ("head4", NH), ("blk8", PB), ("vmix", 128), ("lo_q", 1), ("lo_k", 1), ("one", 8), ("eps", 1)):
    CONST[_n] = (_at, _w)
    _at += _w
NCONST = _at


def shape_constants():
    p = np.arange(128)
    c = np.zeros((128, NCONST), np.float32)

    def put(name, value):
        at, w = CONST[name]
        c[:, at:at + w] = value

    same = (p[:, None] // C == p[None, :] // C).astype(np.float32)
    put("ident", np.eye(128))
    put("negident", -np.eye(128))
    put("mean", same / C)
    put("center", np.eye(128) - same / C)
    pair, ch = np.meshgrid(np.arange(2), np.arange(C), indexing="ij")
    put("vhead", (ch // HD).reshape(1, -1) == 2 * pair.reshape(1, -1) + p[:, None] // 64)
    put("blk4", p[:, None] // C == np.arange(GB)[None, :])
    put("head4", (p[:, None] % C) // HD == np.arange(NH)[None, :])
    put("blk8", p[:, None] // E == np.arange(PB)[None, :])
    mix = np.zeros((128, 128))
    for g in range(128 // C):
        for i in range(C - 1):
            mix[i, g * C + i], mix[C - 1, g * C + i] = 1, -1
        mix[C, g * C + C - 1] = 1
    put("vmix", mix)
    put("lo_q", -(p[:, None] // C == 1).astype(np.float32))
    put("lo_k", -(p[:, None] // C == 2).astype(np.float32))
    put("one", 1.0)
    put("eps", 1e-5)
    return c


def conv_attention_moe(nc, a, cst_d, out):
    ctx = ExitStack()
    with ctx:
        ctx.enter_context(nc.allow_non_contiguous_dma("small weights, token rows"))

        def sb(name, shape, dt=F32):
            return ctx.enter_context(nc.sbuf_tensor(name, shape, dt))

        def sem(name):
            return ctx.enter_context(nc.semaphore(name))

        xa_d = nc.dram_tensor("xa_scratch", (B * C, S), F32, kind="Internal").ap()
        res_d = nc.dram_tensor("res_scratch", (B * C, S), F32, kind="Internal").ap()

        cst = sb("cst", [128, NCONST])
        wp = sb("wp", [128, 4 * 128])
        w1t = sb("w1t", [128, HIDDEN])
        w1f = sb("w1f", [128, GB, HIDDEN])
        w2t = sb("w2t", [128, C])
        wsmall = sb("wsmall", [128, 5, GB, C])
        w1raw = sb("w1raw", [128, GB, C])
        w2raw = sb("w2raw", [C, HIDDEN])
        wrep = sb("wrep", [128, 5, C])
        wbd = sb("wbd", [128, 3, 128])
        wsum = sb("wsum", [128, GB])
        wgate = sb("wgate", [128, GB, E])
        pv = sb("pv", [128, 16])
        bv = sb("bv", [128, 17])
        wqr = sb("wqr", [96, 3, C])
        wkr = sb("wkr", [96, 3, C])
        wvb = sb("wvb", [C + 1, C + 1])
        wvo = sb("wvo", [128, C + 1])
        wva = sb("wva", [96, 2 * C])
        gateb = sb("gateb", [128, 1])
        relb = sb("relb", [128, NH, L])
        relr = sb("relr", [128, NH, L])
        gn = sb("gn", [128, G, 4])
        bns = sb("bns", [128, NC, 6])
        mb = sb("mb", [128, 16])
        tok = sb("tok", [128, B, NT, C])
        ximg = sb("ximg", [128, G * HALO, W])
        xf = ximg[:, :, :].rearrange("p r c -> p (r c)")[:, 0:B * NT * C].rearrange(
            "p (t b c) -> p t b c", b=B, t=NT)
        ARENA = 21600
        arena = sb("arena", [128, ARENA])
        at = [0]

        def carve(n, parts=128):
            v = arena[0:parts, at[0]:at[0] + n]
            at[0] += n
            assert at[0] <= ARENA
            return v

        xin = carve(GB * SP * C, PI).rearrange("p (b n c) -> p b n c", b=GB, c=C)
        xin2 = carve(2 * GB * SP * C, PI).rearrange("p (i n b c) -> p i n b c", i=2, b=GB, c=C)
        at[0] = 0
        xg = carve(CT)
        sq = carve(CT)
        sd = carve(3 * CT).rearrange("p (k n) -> p k n", k=3)
        rs = carve(3 * CT).rearrange("p (k n) -> p k n", k=3)
        xn = carve(2 * CT).rearrange("p (i n) -> p i n", i=2)
        xn2 = carve(CT)
        qz = carve(GB * CT).rearrange("p (j n) -> p j n", j=GB)
        kz = carve(NH * CT).rearrange("p (h n) -> p h n", h=NH)
        sc = carve(2 * GB * NH * L).rearrange("p (i n) -> p i n", i=2)
        ex = carve(2 * GB * NH * L).rearrange("p (i n) -> p i n", i=2)
        pr = carve(2 * GB * NH * 64).rearrange("p (i n) -> p i n", i=2)
        mx = carve(4 * GB * NH).rearrange("p (i n) -> p i n", i=4)
        pt = carve(2 * 8 * 113).rearrange("p (i n) -> p i n", i=2)
        vs = carve(2 * GB * 128).rearrange("p (i n) -> p i n", i=2)
        oc = carve(CT)
        gh = carve(GB * CT).rearrange("p (j n) -> p j n", j=GB)
        t1 = carve(CT)
        xa = carve(CT)
        rt = carve(CT)
        at[0] = 0
        xr = carve(S, 96)
        q2 = [carve(S // 2).bitcast(F16) for _ in range(2)]
        k2 = [carve(S // 2).bitcast(F16) for _ in range(2)]
        hi = carve(2 * KN).bitcast(F16).rearrange("p (i n) -> p i n", i=4)
        pk = carve(DEPTH * 2 * QC).rearrange("p (i n) -> p i n", i=DEPTH)
        vf = [carve(NT * C).rearrange("p (t n) -> p t n", t=NT) for _ in range(2)]
        ua = carve(QC)
        res = [carve(NT * C).rearrange("p (t c) -> p t c", t=NT) for _ in range(2)]
        mxp = carve(5 * 8).rearrange("p (t n) -> p t n", t=5)
        mq = carve(8)
        rden = carve(8)
        oa = carve(2 * 4 * C).rearrange("p (i t c) -> p i t c", i=2, t=4)
        lnc = carve(NT * C).rearrange("p (t c) -> p t c", t=NT)
        lnq = carve(NT * C).rearrange("p (t c) -> p t c", t=NT)
        lnv = carve(5 * NT).rearrange("p (i t) -> p i t", i=5)
        half = sb("half", [128, NT])
        at[0] = 0
        xft = carve(S)
        lg = carve(S)
        pe_ = carve(S)
        mk = carve(S)
        mt = carve(NT * 128).rearrange("p (t n) -> p t n", t=NT)
        bdo = carve(PB * C)
        m8 = carve(8)
        st = carve(8)
        pooled = carve(E * PB, C + 1).rearrange("p (e b) -> p e b", e=E)
        eh = carve(E * PB)
        eo = carve(E * PB, C)
        w1e = carve(E * EH, C + 1).rearrange("p (e h) -> p e h", e=E)
        w2e = carve(E * C).rearrange("p (e c) -> p e c", e=E)
        w2b = carve(E * C, 1).rearrange("p (e c) -> p e c", e=E)

        ps = ctx.enter_context(nc.psum_tensor("ps", [128, 8, 512], F32))

        def cv(name, parts=128, at_=0):
            o, w = CONST[name]
            return cst[at_:at_ + parts, o:o + w]

        G1, B1N, QB, KB, VB, OB, G2, B2N, M2B, M1B = range(10)
        BK, BV, BO, B1, BKH, BQM, SQM = 0, 1, 2, 3, 4, 8, 12

        s_cst = sem("constants_loaded")
        s_w = sem("weights_loaded")
        s_bias = sem("relative_bias_loaded")
        s_clear = sem("cleared")
        s_vec = sem("setup_vector_steps")
        s_wt = sem("weights_transposed")
        s_wb = sem("bias_products")
        s_xin = sem("input_loaded")
        s_xt = sem("input_transposed")
        s_xorder = sem("input_ordered")
        s_xe = sem("input_evacuated")
        s_gsd = sem("groupnorm_std")
        s_clear2 = sem("attention_cleared")
        s_pow = sem("pow_steps")
        conv = {n: sem("conv_" + n) for n in (
            "xg", "qk", "qz", "kz", "score", "vprod", "bias", "max", "sub", "exp", "sum", "rsum", "prob", "ptrans", "pcopy_a",
            "pcopy_b", "vcopy", "av", "oc", "hid", "gelu", "y", "t1", "rt", "stored")}
        ln = [{n: sem(f"norm{k + 1}_{n}") for n in ("center", "square", "var", "std", "rstd", "norm")} for k in range(3)]
        att = {n: sem("attn_" + n) for n in (
            "load", "prod", "hi", "vprod", "vcopy", "score1", "maxall", "mrow", "score2", "exp",
            "av", "acopy", "out", "rden", "o", "tok", "ln", "ss", "xf", "ring")}
        moe = {n: sem("moe_" + n) for n in (
            "xft", "xftc_v", "xftc_a", "logit", "logitc", "top", "exp", "mk", "mt", "mtc_v", "mtc_a", "pool", "poolc",
            "hid", "gelu", "out", "outc", "outt", "bdo", "scat", "add", "weights", "stored")}
        block = ctx.enter_context(nc.Block())

        VB_, PT_, XB, YB, ZB = 2, 3, 5, 6, 7

        x_d = a["x"].rearrange("b h w c -> b (h w) c")
        out_d = out.rearrange("b h w c -> b (h w) c")

        def col(v):
            return v.rearrange("(n o) -> n o", o=1)


        def image(g, row, rows):
            return ximg[:, bass.ds(g * HALO + row, rows), :]

        def tile_rows(t):
            return T if t < NT - 1 else TL

        def chunk_tiles(c):
            return range(4 * c, min(4 * c + 4, NT))

        def chunk_cols(c):
            return min(QC, S - QC * c)

        steps2 = []
        for c in range(NQ - 1):
            for t in range(0, NT - 1, 2):
                steps2.append((c, [(t, 0), (t + 1, QC)], [(T, 0, 2, QC)]))
            steps2.append((c, [(NT - 1, 0)], [(TL, 0, 1, QC)]))
        per = QC // TL
        steps2.append((NQ - 1, [(t, TL * t) for t in range(2 * per)], [(T, 0, 2, QC)]))
        steps2.append((NQ - 1, [(t, TL * (t - 2 * per)) for t in range(2 * per, NT)], [(T, 0, 1, QC), (TL, 1, 1, TL)]))
        NSTEP = len(steps2)
        assert NT == 3 * per + 1 and NSTEP % DEPTH == 0
        first_of = [[x[0] for x in steps2].index(c) for c in range(NQ)]
        last_of = [first_of[c + 1] - 1 for c in range(NQ - 1)] + [NSTEP - 1]
        def sums_at(x):
            y = x - LAG
            k = (y + (NSTEP if y < 0 else 0)) - first_of[steps2[y][0]]
            if k == NT // 2:
                return [y]
            return [y - 1, y] if k % 2 else []

        summed_at = [x + LAG for x in last_of]
        out_at = [x + LAG + 1 for x in last_of]
        over_at = [x + LAG + 2 for x in last_of]

        def chunks_at(when, x):
            return [(c, 0) for c in range(NQ) if when[c] == x] + [(c, 1) for c in range(NQ) if when[c] == x + NSTEP]

        NV = -(-NT // 7)
        FP = NK * NT
        AHEAD = 5 * NK
        EARLY = 14
        lead = [("proj", n) for n in range(2 * NK)] + [("value", n) for n in range(NV)] + \
               [("max", k) for k in range(AHEAD)]
        jobs = [(0, "max", k) for k in range(AHEAD, FP)]
        fresh = [x for x in lead if x[0] != "max"]
        for i, x in enumerate(fresh):
            jobs.insert(EARLY + (FP - AHEAD - EARLY) * i // len(fresh) + i, (1, *x))
        jobs += [(1, "max", k) for k in range(AHEAD)]
        NJ = len(jobs)

        def jobs_until(x):
            return min(NJ, NJ * (x + 1) // (NSTEP - 2))

        def jobs_at(x, last):
            part = range(jobs_until(x - 1) if x else 0, jobs_until(x))
            if last:
                return [(sum(1 - y[0] for y in jobs[:j]), *jobs[j]) for j in part if not jobs[j][0]]
            return [(j, *jobs[j]) for j in part]

        JB = (4, 5, 3, 7)

        def turn(j, total, banks):
            m = j % banks
            return m, (j - banks + 1 if j >= banks else -((total - 1 - m) % banks))

        turn_at, TURN = {}, 1
        for c in range(1, NQ + 1):
            need = jobs.index((0, "max", min(NK * 4 * (c + 1), FP) - 1) if c < NQ else (1, "max", NK * 4 - 1)) + 1
            turn_at[min(x for x in range(NSTEP) if jobs_until(x) >= need) + TURN] = c

        assert all(x <= (first_of + [NSTEP])[c] - 1 for x, c in turn_at.items()) and len(turn_at) == NQ

        SB = 3
        units, row_unit, NUNIT = [], {}, 0
        for x, (c, tiles, blocks) in enumerate(steps2):
            units.append([])
            for rows, bank, k, n in blocks:
                for m in range(bank, bank + k):
                    units[-1].append((NUNIT, m, rows, chunk_cols(c) if c < NQ - 1 else n,
                                      [(t, at_) for t, at_ in tiles if at_ // QC == m]))
                    NUNIT += 1
            if x in turn_at:
                row_unit[turn_at[x]] = NUNIT
                NUNIT += 1

        def score_no(w):
            return w + 1 - sum(v < w for v in row_unit.values())

        def place_of(w, last):
            return w - int(last and w > row_unit[NQ])
        LN_AT = 24

        NX = -(-NT // 4)
        weights = 5 + 2 + 9 + GB - 1 + 1 + 12 + 2 + PB

        @block.sync
        def _(sp):
            sp.dma_start(cst[:, :], cst_d).then_inc(s_cst, 16)
            count = [0]

            def load(dst, src):
                sp.dma_start(dst, src).then_inc(s_w, 16)
                count[0] += 1

            def load_input(g):
                if g:
                    sp.wait_ge(s_xorder, g)
                sp.dma_start(xin.rearrange("p b n c -> p b (n c)"), x_d[GB * g:GB * (g + 1)].rearrange("b (p n) c -> p b (n c)", p=PI))\
                  .then_inc(s_xin, 16)

            load_input(0)
            for i in range(3):
                load(wsmall[0:C, i, 0, :], a["L0_conv_qkv_w"][C * i:C * (i + 1), :])
            load(wsmall[0:C, 3, 0, :], a["L0_conv_out_w"])
            load(wsmall[0:E, 4, 0, :], a["L1_ffn_gate_w"])
            load(w1raw[:, 0, :], a["L0_conv_mlp_w1"])
            load(w2raw[:, :], a["L0_conv_mlp_w2"])
            qkvb = a["L0_conv_qkv_b"]
            for k, v in ((G1, a["L0_conv_norm1_g"]), (B1N, a["L0_conv_norm1_b"]), (QB, qkvb[0:C]), (KB, qkvb[C:2 * C]),
                         (VB, qkvb[2 * C:3 * C]), (OB, a["L0_conv_out_b"]), (G2, a["L0_conv_norm2_g"]),
                         (B2N, a["L0_conv_norm2_b"]), (M2B, a["L0_conv_mlp_b2"])):
                load(pv[0:C, k:k + 1], col(v))
            load_input(1)
            vectors = count[0]
            load(pv[:, M1B:M1B + 1], col(a["L0_conv_mlp_b1"]))
            sp.wait_ge(s_clear, 2)
            for r in range(3):
                load(wqr[0:C, r, :], a["L1_attn_Wq"])
                load(wqr[C:C + 1, r, :], a["L1_attn_bq"].rearrange("(o n) -> o n", o=1))
                load(wkr[0:C, r, :], a["L1_attn_Wk"])
                load(wkr[C:C + 1, r, :], a["L1_attn_bk"].rearrange("(o n) -> o n", o=1))
            load_input(2)
            load(wvb[0:C, 0:C], a["L1_attn_Wv"])
            load(wvb[C:C + 1, 0:C], a["L1_attn_bv"].rearrange("(o n) -> o n", o=1))
            for b in range(PB):
                load(gateb[E * b:E * (b + 1), :], col(a["L1_ffn_gate_b"]))
            sp.wait_ge(s_w, 16 * vectors)
            for j in range(1, GB):
                load(pv[C * j:C * (j + 1), 0:M1B], pv[0:C, 0:M1B])
            assert count[0] == weights
            load_input(3)
            sp.wait_ge(s_bias, 16 * L)
            sp.dma_start(relr[64:64 + L, :, :], relr[0:L, :, :]).then_inc(s_bias, 16)
            xa_g = xa_d.rearrange("(g p) n -> g p n", g=G)
            res_g = res_d.rearrange("(g p) n -> g p n", g=G)
            with sp.Fori(0, G) as g:
                with sp.Fori(0, NC) as c:
                    it = g * NC + c
                    sp.wait_ge(conv["rt"], it + 1)
                    sp.dma_start(xa_g[bass.ds(g, 1), :, bass.ds(c * CT, CT)].rearrange("o p n -> (o p) n"), xa[:, :])\
                      .then_inc(conv["stored"], 16)
                    sp.dma_start(res_g[bass.ds(g, 1), :, bass.ds(c * CT, CT)].rearrange("o p n -> (o p) n"), rt[:, :])\
                      .then_inc(conv["stored"], 16)
            sp.wait_ge(conv["stored"], 32 * G * NC)
            xa_b = xa_d.rearrange("(b p) n -> b p n", b=B)
            res_b = res_d.rearrange("(b p) n -> b p n", b=B)
            sp.wait_ge(s_clear2, 1)
            def load_image(b):
                if isinstance(b, int):
                    xa_i, res_i = xa_b[b], res_b[b]
                else:
                    xa_i, res_i = (v[bass.ds(b, 1)].rearrange("o p n -> (o p) n") for v in (xa_b, res_b))
                sp.dma_start(xr[0:C, :], xa_i).then_inc(att["load"], 16)
                sp.dma_start(xr[2 * C:3 * C, :], res_i).then_inc(att["load"], 16)

            load_image(0)
            with sp.Fori(1, B) as b:
                sp.wait_ge(att["vprod"], b * NV)
                load_image(b)
            sp.wait_ge(att["xf"], B + 1)
            sp.dma_start(w1e, a["L1_ffn_weight1"].rearrange("e d h -> d e h")).then_inc(moe["weights"], 16)
            sp.dma_start(w2e, a["L1_ffn_weight2"][:, 0:EH, :].rearrange("e h o -> h e o")).then_inc(moe["weights"], 16)
            sp.dma_start(w2b, a["L1_ffn_weight2"][:, EH:EH + 1, :].rearrange("e h o -> h e o")).then_inc(moe["weights"], 16)
            for h in range(B // PB):
                sp.wait_ge(moe["add"], NT * (h + 1))
                for k in range(PB * h, PB * (h + 1)):
                    b = (k - 1) % B
                    sp.dma_start(out_d[b, 0:(NT - 1) * T, :].rearrange("(t p) c -> p t c", p=T), tok[:, k, 0:NT - 1, :])\
                      .then_inc(moe["stored"], 16)
                    sp.dma_start(out_d[b, (NT - 1) * T:S, :], tok[0:TL, k, NT - 1, :]).then_inc(moe["stored"], 16)
            sp.wait_ge(moe["stored"], 32 * B)

        @block.gpsimd
        def _(pool):
            pool.memset(relr[:, :, :], 0.0).then_inc(s_clear, 1)
            pool.memset(wva[:, :], 0.0)
            pool.memset(wvb[:, :], 0.0)
            pool.memset(wqr[:, :, :], 0.0)
            pool.memset(wkr[:, :, :], 0.0).then_inc(s_clear, 1)
            pool.memset(half[:, :], -0.5).then_inc(s_clear, 1)
            pool.memset(tok[:, 0, :, :], 0.0).then_inc(s_clear, 1)
            pool.memset(tok[:, 1:B, NT - 1, :], 0.0).then_inc(s_clear, 1)
            pool.wait_ge(s_clear, 5)

            def subtract(v, u):
                i = u % 2
                pool.wait_ge(conv["max"], v + 1)
                s3 = sc[0:113, i, :].rearrange("p (m k) -> p m k", k=L)
                pool.tensor_tensor(s3, s3, mx[0:113, i, :].rearrange("p (m o) -> p m o", o=1)
                                   .broadcast_to([113, GB * NH, L]), ALU.subtract).then_inc(conv["sub"], 1)

            def probabilities(v, u):
                i = u % 2
                pool.wait_ge(conv["rsum"], v + 1)
                pool.tensor_tensor(pr[0:113, i, :].rearrange("p (m k) -> p m k", k=64)[:, :, 0:L],
                                   ex[0:113, i, :].rearrange("p (m k) -> p m k", k=L),
                                   mx[0:113, 2 + i, :].rearrange("p (m o) -> p m o", o=1)
                                   .broadcast_to([113, GB * NH, L]), ALU.mult).then_inc(conv["prob"], 1)

            def residual(n):
                pool.wait_ge(ln[2]["norm"], n + 1)
                if not (isinstance(n, int) and n == 0):
                    pool.wait_ge(conv["stored"], n * 32)
                pool.tensor_tensor(rt[:, :], t1[:, :], xa[:, :], ALU.add).then_inc(conv["rt"], 1)

            def chunk(it, post=True, pre=True):
                for u in range(NU):
                    v = it * NU + u
                    if u + 1 < NU or pre:
                        probabilities(v + 1, u + 1)
                    if u == 0 and post:
                        residual(it - 2)
                    if u + 2 < NU or pre:
                        subtract(v + 2, u + 2)

            subtract(0, 0)
            probabilities(0, 0)
            subtract(1, 1)
            chunk(0, post=False)
            chunk(1, post=False)
            chunk(2)
            chunk(3)
            with pool.Fori(0, G * NC // 2 - 3) as i:
                chunk(i * 2 + 4)
                chunk(i * 2 + 5)
            chunk(G * NC - 2)
            chunk(G * NC - 1, pre=False)
            residual(G * NC - 2)
            residual(G * NC - 1)

            def slot(b):
                return 0 if isinstance(b, int) and b == B - 1 else b + 1

            def tokens(b, p, c):
                k, rows = len(chunk_tiles(c)), tile_rows(4 * c)
                i = (NQ * p + c) % 2
                pool.wait_ge(att["o"], b * NQ + c + 1)
                pool.tensor_tensor(tok[0:rows, bass.ds(slot(b), 1), 4 * c:4 * c + k, :].rearrange("p o t c -> p (o t) c"),
                                   oa[0:rows, i, 0:k, :], res[p][0:rows, 4 * c:4 * c + k, :], ALU.add)\
                    .then_inc(att["tok"], 1)

            def normalize_slot(b):
                k = 0 if isinstance(b, int) and b == B else b
                pool.wait_ge(att["ln"], b * 5 + 5)
                pool.tensor_tensor(lnv[:, 4, :], lnv[:, 3, :], half[:, :], ALU.pow).then_inc(s_pow, 1)
                pool.wait_ge(s_pow, b + 1)
                pool.tensor_tensor(xf[:, :, bass.ds(k, 1), :].rearrange("p t o c -> p (t o) c"), lnc[:, :, :],
                                   lnv[:, 4, :].rearrange("p (t o) -> p t o", o=1).broadcast_to([128, NT, C]),
                                   ALU.mult).then_inc(att["xf"], 1)

            def image_steps(b, p, first=False):
                for x in range(NSTEP):
                    for c, late in chunks_at(out_at, x):
                        if not (late and first):
                            tokens(b - late, (p + late) % 2, c)
                    if x == LN_AT + 12:
                        normalize_slot(b)

            image_steps(0, 0, first=True)
            with pool.Fori(0, B // 2 - 1) as i:
                image_steps(i * 2 + 1, 1)
                image_steps(i * 2 + 2, 0)
            image_steps(B - 1, 1)
            for x in range(LAG + 2):
                for c, late in chunks_at(out_at, x):
                    if late:
                        tokens(B - 1, 1, c)
            normalize_slot(B)

        @block.scalar
        def _(act):
            tab = a["L0_conv_pe_table"].rearrange("h (y x) -> h y x", x=2 * WS - 1)
            act.wait_ge(s_clear, 2)
            for qy in range(WS):
                if qy < G:
                    g = qy
                    act.wait_ge(s_xin, 16 * (g + 1))
                    if g >= 2:
                        act.wait_ge(s_xt, NK * (g - 1))
                    act.activation(xin2[:, g % 2], xin.rearrange("p b n c -> p n b c"), ACT.Copy).then_inc(s_xorder, 1)
                for qx in range(WS):
                    p = WS * qy + qx
                    act.dma_start(relr[p:p + 1, :, :].rearrange("p h (y x) -> p h y x", x=WS),
                                  tab[:, qy:qy + WS, qx:qx + WS].rearrange("h y (o x) -> o h y x", o=1))\
                       .then_inc(s_bias, 16)
            act.wait_ge(s_vec, VS_GN)
            act.activation(gn[:, :, 2], gn[:, :, 1], ACT.Sqrt, bias=cv("eps")[:, 0:1]).then_inc(s_gsd, 1)


            def square(n, k, bank, bias=None):
                act.wait_ge(ln[k]["center"], n + 1)
                if bias is None:
                    act.activation(sq[:, :], ps[:, bank, 0:CT], ACT.Square).then_inc(ln[k]["square"], 1)
                else:
                    act.activation(sq[:, :], ps[:, bank, 0:CT], ACT.Square, bias=bias).then_inc(ln[k]["square"], 1)

            def root(n, k):
                act.wait_ge(ln[k]["var"], n + 1)
                act.activation(sd[:, k, :], ps[:, ZB, 0:CT], ACT.Ln, bias=cv("eps")[:, 0:1]).then_inc(ln[k]["std"], 1)
                act.wait_ge(ln[k]["std"], n + 1)
                act.activation(rs[:, k, :], sd[:, k, :], ACT.Exp, scale=-0.5).then_inc(ln[k]["rstd"], 1)

            def log_and_exp():
                act.preload_act_table_set("natural_log_exp_and_others")

            def exponentials(v, u):
                act.wait_ge(conv["sub"], v + 1)
                act.activation(ex[0:113, u % 2, :], sc[0:113, u % 2, :], ACT.Exp).then_inc(conv["exp"], 1)

            def probs_a(v, u):
                act.wait_ge(conv["ptrans"], 2 * v + 1)
                act.activation(pt[:, u % 2, 0:4 * 113].rearrange("p (n q) -> p n q", q=113),
                               ps[:, PT_, :].rearrange("p (n q) -> p n q", q=128)[:, :, 0:113], ACT.Copy)\
                   .then_inc(conv["pcopy_a"], 1)

            def weighted_copy(v, u):
                act.wait_ge(conv["av"], v + 1)
                at_ = 4 * C * 2 + 2 * L * (u % 2)
                act.activation(oc[:, :].rearrange("p (r w c) -> p w r c", r=WS, c=WS)[:, 2 * u:2 * u + 2],
                               ps[:, VB_, at_:at_ + 2 * L].rearrange("p (w r c) -> p w r c", r=WS, c=WS), ACT.Copy)\
                   .then_inc(conv["oc"], 1)

            def queries(n):
                act.wait_ge(conv["qk"], n * 2 + 1)
                for j in range(GB):
                    last = act.activation(qz[:, j, :], ps[:, YB, 0:CT], ACT.Identity, bias=bv[:, BQM + j:BQM + j + 1],
                                          scale=bv[:, SQM + j:SQM + j + 1])
                last.then_inc(conv["qz"], 1)

            def gelu(n, j):
                act.wait_ge(conv["hid"], n * GB + j + 1)
                act.activation(gh[:, j, :], ps[:, (XB, XB, XB, YB)[j], 0:CT], ACT.Gelu, bias=bv[:, B1:B1 + 1])\
                   .then_inc(conv["gelu"], 1)

            def chunk(it, post=True, pre=True):
                v, n = it * NU, it - 1
                if post:
                    weighted_copy(v - 1, NU - 1)
                    square(n, 1, XB, bv[:, BO:BO + 1])
                probs_a(v, 0)
                exponentials(v + 1, 1)
                if post:
                    root(n, 1)
                if pre:
                    square(it + 1, 0, YB)
                weighted_copy(v, 0)
                if pre:
                    root(it + 1, 0)
                probs_a(v + 1, 1)
                exponentials(v + 2, 2)
                if post:
                    gelu(n, 0)
                weighted_copy(v + 1, 1)
                if post:
                    gelu(n, 1)
                probs_a(v + 2, 2)
                if pre:
                    queries(it + 1)
                if post:
                    log_and_exp()
                exponentials(v + 3, 3)
                weighted_copy(v + 2, 2)
                if post:
                    gelu(n, 2)
                    gelu(n, 3)
                    log_and_exp()
                    square(n, 2, YB)
                probs_a(v + 3, 3)
                if pre:
                    exponentials(v + 4, 0)
                if post:
                    root(n, 2)

            log_and_exp()
            square(0, 0, YB)
            root(0, 0)
            queries(0)
            exponentials(0, 0)
            chunk(0, post=False)
            chunk(1)
            with act.Fori(0, G * NC // 2 - 2) as i:
                chunk(i * 2 + 2)
                chunk(i * 2 + 3)
            chunk(G * NC - 2)
            chunk(G * NC - 1, pre=False)
            weighted_copy(G * NC * NU - 1, NU - 1)
            square(G * NC - 1, 1, XB, bv[:, BO:BO + 1])
            root(G * NC - 1, 1)
            for j in range(GB):
                gelu(G * NC - 1, j)
            log_and_exp()
            square(G * NC - 1, 2, YB)
            root(G * NC - 1, 2)

            def split_or_copy(b, kind, n, j):
                bank = JB[j % len(JB)]
                if kind == "proj":
                    act.wait_ge(att["prod"], b * (2 * NK) + n + 1)
                    act.activation(hi[0:96, n % 4, :], ps[0:96, bank, 0:KN], ACT.Copy).then_inc(att["hi"], 1)
                elif kind == "value":
                    p = par(b)
                    act.wait_ge(att["vprod"], b * NV + n + 1)
                    k = min(7, NT - 7 * n)
                    if n == NV - 1:
                        k -= 1
                        act.activation(vf[p][0:TL, NT - 1, :], ps[0:TL, bank, 2 * C * k:2 * C * k + C], ACT.Copy)
                    src = ps[:, bank, 0:2 * C * k].rearrange("p (t n) -> p t n", n=2 * C)
                    act.activation(vf[p][:, 7 * n:7 * n + k, :], src[:, :, 0:C], ACT.Copy).then_inc(att["vcopy"], 1)

            def max_row(b, p, c, w):
                n = chunk_cols(c)
                act.wait_ge(att["mrow"], b * NQ + c + 1)
                act.activation(q2[p][96:97, QC * c:QC * c + n], ps[96:97, w % SB, 0:n], ACT.Copy).then_inc(att["exp"], 1)

            def sums_copy(b, c):
                n = chunk_cols(c)
                act.wait_ge(att["av"], b * NSTEP + last_of[c] + 1)
                act.activation(ua[:, 0:n], ps[:, 6, 0:n], ACT.Copy).then_inc(att["acopy"], 1)

            def image_steps(b, p, first=False, last=False):
                par_of[0] = p
                for x in range(NSTEP):
                    if x >= DEPTH or not first:
                        act.wait_ge(att["av"], b * NSTEP + x - DEPTH + 1)
                    for w_, m, rows, n, _ in units[x]:
                        w = place_of(w_, last)
                        act.wait_ge(att["score2"], b * (NUNIT - NQ) + score_no(w_))
                        act.activation(pk[0:rows, x % DEPTH, QC * m:QC * m + n], ps[0:rows, w % SB, 0:n], ACT.Exp,
                                       scale=float(C) ** -0.5).then_inc(att["exp"], 1)
                    for j, ahead, kind, n in jobs_at(x, last):
                        if kind != "max":
                            split_or_copy(b + ahead, kind, n, j)
                    if x in turn_at and not (last and turn_at[x] == NQ):
                        if turn_at[x] == NQ:
                            max_row(b + 1, 1 - p, 0, row_unit[NQ])
                        else:
                            max_row(b, p, turn_at[x], row_unit[turn_at[x]])
                    for c, late in chunks_at(summed_at, x):
                        if not (late and first):
                            sums_copy(b - late, c)

            par_of = [1]

            def par(b):
                return 1 - par_of[0]

            for j, (kind, n) in enumerate(lead):
                split_or_copy(0, kind, n, j)
            max_row(0, 0, 0, 0)
            image_steps(0, 0, first=True)
            with act.Fori(0, B // 2 - 1) as i:
                image_steps(i * 2 + 1, 1)
                image_steps(i * 2 + 2, 0)
            image_steps(B - 1, 1, last=True)
            for x in range(LAG + 1):
                for c, late in chunks_at(summed_at, x):
                    if late:
                        sums_copy(B - 1, c)

            for h in range(B // PB):
                for gg in range(2):
                    for n in range(1, NX, 2):
                        act.wait_ge(moe["xft"], NX * (2 * h + gg) + n + 1)
                        act.activation(xft[:, QC * n:QC * n + chunk_cols(n)], ps[:, n, 0:chunk_cols(n)], ACT.Copy)\
                           .then_inc(moe["xftc_a"], 1)
                    for n in range(NK):
                        act.wait_ge(moe["logit"], NK * (2 * h + gg) + n + 1)
                        act.activation(lg[64 * gg:64 * gg + 64, KN * n:KN * n + KN], ps[64 * gg:64 * gg + 64, n, 0:KN],
                                       ACT.Identity, bias=gateb[64 * gg:64 * gg + 64, 0:1]).then_inc(moe["logitc"], 1)
                act.wait_ge(moe["top"], 2 * h + 2)
                act.activation(pe_[:, :], lg[:, :], ACT.Exp, bias=st[:, 0:1], accum_out=st[:, 1:2]).then_inc(moe["exp"], 1)
                for n in range(1, NX, 2):
                    act.wait_ge(moe["mt"], NX * h + n + 1)
                    k = len(chunk_tiles(n))
                    act.activation(mt[:, 4 * n:4 * n + k, :].rearrange("p t n -> p (t n)"), ps[:, n, 0:128 * k], ACT.Copy)\
                       .then_inc(moe["mtc_a"], 1)
                act.wait_ge(moe["hid"], h + 1)
                act.activation(eh[:, :], ps[:, 0, 0:E * PB], ACT.Gelu).then_inc(moe["gelu"], 1)

        @block.vector
        def _(dve):
            steps = [0]

            def step(ins, wait=True):
                steps[0] += 1
                ins.then_inc(s_vec, 1)
                if wait:
                    dve.wait_ge(s_vec, steps[0])

            def bcast(v, n):
                return v.rearrange("p (o c) -> p o c", o=1).broadcast_to([v.shape[0], n, v.shape[1]])

            dve.wait_ge(s_cst, 16)
            for g in range(G):
                img = ximg[:, g * HALO:(g + 1) * HALO, :].rearrange("p r c -> p (r c)")
                for n in range(NK):
                    dve.wait_ge(s_xt, NK * g + n + 1)
                    dve.tensor_copy(img[:, SHIFT * W:].rearrange("p (q j) -> p j q", j=SP)[:, 4 * n:4 * n + 4, :],
                                    ps[:, n, 0:KN].rearrange("p (j q) -> p j q", j=4)).then_inc(s_xe, 1)
                dve.wait_ge(s_xe, NK * (g + 1))
                dve.tensor_copy(img[:, 0:SHIFT * W], img[:, H * W:HALO * W])
                for c in range(NC):
                    last = dve.bn_stats(bns[:, c, :], img[:, SHIFT * W + CT * c:SHIFT * W + CT * (c + 1)])
                step(last)
                step(dve.bn_aggr(gn[:, g, 0:2], bns[:, :, :].rearrange("p c s -> p (c s)")))
            assert steps[0] == VS_GN
            dve.wait_ge(s_gsd, 1)
            step(dve.reciprocal(gn[:, :, 3], gn[:, :, 2]))

            dve.wait_ge(s_w, 16 * weights)
            for i in range(4):
                dve.tensor_copy(wsmall[0:C, i, 1:GB, :], bcast(wsmall[0:C, i, 0, :], GB - 1))
            dve.tensor_copy(wsmall[0:E, 4, 1:GB, :], bcast(wsmall[0:E, 4, 0, :], GB - 1))
            step(dve.tensor_copy(w1raw[:, 1:GB, :], bcast(w1raw[:, 0, :], GB - 1)))
            assert steps[0] == VS_REP
            dve.wait_ge(s_wt, 1)
            dve.tensor_copy(wrep[:, 0:4, :], ps[:, 4, 0:128].rearrange("p (i c) -> p i c", i=4))
            dve.tensor_copy(wrep[:, 4, 0:E], ps[:, 4, 128:128 + E])
            dve.tensor_copy(w1t[:, :], ps[:, 5, 0:128])
            step(dve.tensor_copy(w2t[:, :], ps[:, 6, 0:C]))

            def mask(name, n):
                return cv(name).rearrange("p (j o) -> p j o", o=1).broadcast_to([128, GB, n])

            for i in range(3):
                dve.tensor_tensor(wbd[:, i, :].rearrange("p (j c) -> p j c", j=GB), bcast(wrep[:, i, :], GB), mask("blk4", C),
                                  ALU.mult)
            dve.tensor_tensor(wp[:, 256:384].rearrange("p (j c) -> p j c", j=GB), bcast(wrep[:, 3, :], GB), mask("blk4", C),
                              ALU.mult)
            dve.tensor_tensor(wgate[:, :, :], bcast(wrep[:, 4, 0:E], GB), mask("blk4", E), ALU.mult)
            for j in range(GB):
                dve.tensor_scalar(w1f[:, j, :], w1t[:, :], pv[:, G2:G2 + 1], cv("blk4")[:, j:j + 1], ALU.mult, ALU.mult)
            dve.tensor_copy(wva[0:C, 0:C - 1], cv("ident", C)[:, 0:C - 1])
            step(dve.tensor_copy(wva[64:96, C:2 * C], cv("ident", 32, 64)[:, 64:96]))
            wo = wp[:, 256:384].rearrange("p (j c) -> p j c", j=GB)
            dve.tensor_reduce(wsum[:, :], wo, AX_X, ALU.add)
            dve.memset(wvb[C:C + 1, C:C + 1], 1.0)
            step(dve.memset(wva[C:C + 1, C - 1:C], 1.0))
            dve.scalar_tensor_tensor(wo, wsum[:, :].rearrange("p (j o) -> p j o", o=1).broadcast_to([128, GB, C]),
                                     -1.0 / C, wo, ALU.mult, ALU.add)
            dve.tensor_scalar(wp[:, 384:512], wbd[:, 2, :], pv[:, G1:G1 + 1], None, ALU.mult)
            step(dve.tensor_scalar(wp[:, 0:256], wbd[:, 0:2, :].rearrange("p i c -> p (i c)"), pv[:, G1:G1 + 1], None,
                                   ALU.mult))
            assert steps[0] == VS_FOLD
            dve.wait_ge(s_wb, 1)
            dve.tensor_scalar(bv[:, 16:17], ps[:, 4, 0:1], pv[:, QB:QB + 1], float(HD) ** -0.5, ALU.add, ALU.mult)
            dve.tensor_scalar(bv[:, SQM:SQM + GB], cv("blk4"), float(HD) ** -0.5, None, ALU.mult)
            dve.tensor_scalar(bv[:, BK:BK + 1], ps[:, 4, 1:2], pv[:, KB:KB + 1], None, ALU.add)
            dve.tensor_scalar(bv[:, B1:B1 + 1], ps[:, 5, 0:1], pv[:, M1B:M1B + 1], None, ALU.add)
            step(dve.tensor_scalar(bv[:, BV:BV + 1], ps[:, 4, 2:3], pv[:, VB:VB + 1], None, ALU.add))
            assert steps[0] == VS_BV
            dve.tensor_scalar(bv[:, BQM:BQM + GB], cv("blk4"), bv[:, 16:17], None, ALU.mult)
            dve.tensor_scalar(bv[:, BKH:BKH + NH], cv("head4"), bv[:, BK:BK + 1], None, ALU.mult)
            dve.wait_ge(s_wb, 2)
            dve.tensor_copy(wvo[:, :], ps[:, 5, 8:9 + C])
            step(dve.tensor_copy(bv[:, BO:BO + 1], ps[:, 4, 3:4]))
            dve.wait_ge(s_bias, 16 * (L + 1))
            dve.tensor_copy(relb[:, :, :], relr[:, :, ::-1])

            dve.memset(pr[:, :, :], 0.0)
            step(dve.memset(ps[:, 0:VB_ + 1, :], 0.0))
            assert steps[0] == VS_STAGE0

            def place(n):
                return n // NC, n % NC

            def group_norm(n):
                g, c = place(n)
                mean = gn[:, bass.ds(g, 1), 0]
                rstd = gn[:, bass.ds(g, 1), 3]
                xg3 = xg[:, :].rearrange("p (r c) -> p r c", c=W)
                src = image(g, c * WS, WS)
                dve.tensor_scalar(xg3[:, :, SHIFT:W], src[:, :, 0:W - SHIFT], mean, rstd, ALU.subtract, ALU.mult)
                dve.tensor_scalar(xg3[:, :, 0:SHIFT], src[:, :, W - SHIFT:W], mean, rstd, ALU.subtract, ALU.mult)\
                   .then_inc(conv["xg"], 1)

            def bias_and_max(v, u):
                i = u % 2
                dve.wait_ge(conv["score"], v + 1)
                dve.tensor_tensor(sc[0:113, i, :].rearrange("p (b j n) -> p b j n", b=2, j=2),
                                  ps[0:113, 0:2, 0:2 * NH * L].rearrange("p b (j n) -> p b j n", j=2),
                                  relb[0:113, :, :].rearrange("p (b j h) k -> p b j (h k)", b=1, j=1)
                                  .broadcast_to([113, 2, 2, NH * L]), ALU.add).then_inc(conv["bias"], 1)
                dve.wait_ge(conv["bias"], v + 1)
                dve.tensor_reduce(mx[0:113, i, :], sc[0:113, i, :].rearrange("p (m k) -> p m k", k=L), AX_X, ALU.max)\
                   .then_inc(conv["max"], 1)

            def sums(v, u):
                i = u % 2
                dve.wait_ge(conv["exp"], v + 1)
                dve.tensor_reduce(mx[0:113, 2 + i, :], ex[0:113, i, :].rearrange("p (m k) -> p m k", k=L), AX_X, ALU.add)\
                   .then_inc(conv["sum"], 1)
                dve.wait_ge(conv["sum"], v + 1)
                dve.reciprocal(mx[0:113, 2 + i, :], mx[0:113, 2 + i, :]).then_inc(conv["rsum"], 1)

            def probs_b(v, u):
                dve.wait_ge(conv["ptrans"], 2 * v + 2)
                dve.tensor_copy(pt[:, u % 2, 4 * 113:8 * 113].rearrange("p (n q) -> p n q", q=113),
                                ps[:, PT_ + 1, :].rearrange("p (n q) -> p n q", q=128)[:, :, 0:113])\
                   .then_inc(conv["pcopy_b"], 1)

            def values_copy(v, u):
                dve.wait_ge(conv["vprod"], v + 1)
                dve.tensor_tensor(vs[0:113, u % 2, :].rearrange("p (m a c) -> p m a c", a=2, c=C),
                                  ps[0:113, VB_, 0:2 * GB * C].rearrange("p (m a c) -> p m a c", a=1, c=C)
                                  .broadcast_to([113, 2 * GB, 2, C]),
                                  cv("vhead", 113).rearrange("p (m a c) -> p m a c", m=1, a=2)
                                  .broadcast_to([113, 2 * GB, 2, C]), ALU.mult).then_inc(conv["vcopy"], 1)

            def normalize(n, k, bank, dst):
                dve.wait_ge(ln[k]["rstd"], n + 1)
                src = ps[:, bank, 0:CT]
                if k == 0:
                    def rows(v):
                        return v.rearrange("p (r w c) -> p r w c", r=WS, c=WS)
                    last = dve.tensor_tensor(dst.rearrange("p (w r c) -> p r w c", r=WS, c=WS), rows(src),
                                             rows(rs[:, k, :]), ALU.mult)
                elif k == 1:
                    last = dve.scalar_tensor_tensor(dst, src, bv[:, BO:BO + 1], rs[:, k, :], ALU.add, ALU.mult)
                else:
                    last = dve.tensor_tensor(dst, src, rs[:, k, :], ALU.mult)
                last.then_inc(ln[k]["norm"], 1)

            def keys(n):
                dve.wait_ge(conv["qk"], n * 2 + 2)
                for h in range(NH):
                    last = dve.tensor_scalar(kz[:, h, :], ps[:, ZB, 0:CT], cv("head4")[:, h:h + 1],
                                             bv[:, BKH + h:BKH + h + 1], ALU.mult, ALU.add)
                last.then_inc(conv["kz"], 1)

            def attention_norm(n):
                if not (isinstance(n, int) and n == 0):
                    dve.wait_ge(conv["stored"], n * 32)
                normalize(n, 2, YB, xa[:, :])

            def skip_connection(n):
                g, c = place(n)
                if not (isinstance(n, int) and n == 0):
                    dve.wait_ge(conv["rt"], n)
                dve.wait_ge(conv["y"], n + 1)
                dve.scalar_tensor_tensor(t1[:, :], ps[:, ZB, 0:CT], pv[:, M2B:M2B + 1],
                                         image(g, c * WS + SHIFT, WS).rearrange("p r c -> p (r c)"), ALU.add, ALU.add)\
                   .then_inc(conv["t1"], 1)

            def chunk(it, p, post=True, pre=True, norm=True):
                v, n = it * NU, it - 1
                values_copy(v + 1, 1)
                if pre:
                    group_norm(it + 1)
                if norm:
                    attention_norm(it - 2)
                probs_b(v, 0)
                sums(v + 1, 1)
                bias_and_max(v + 2, 2)
                if post:
                    normalize(n, 1, XB, xn2[:, :])
                values_copy(v + 2, 2)
                probs_b(v + 1, 1)
                if pre:
                    normalize(it + 1, 0, YB, xn[:, 1 - p, :])
                sums(v + 2, 2)
                bias_and_max(v + 3, 3)
                values_copy(v + 3, 3)
                probs_b(v + 2, 2)
                if pre:
                    keys(it + 1)
                sums(v + 3, 3)
                if pre:
                    bias_and_max(v + 4, 0)
                if post:
                    skip_connection(n)
                if pre:
                    values_copy(v + 4, 0)
                probs_b(v + 3, 3)
                if pre:
                    sums(v + 4, 0)
                    bias_and_max(v + 5, 1)

            group_norm(0)
            normalize(0, 0, YB, xn[:, 0, :])
            keys(0)
            bias_and_max(0, 0)
            values_copy(0, 0)
            sums(0, 0)
            bias_and_max(1, 1)
            chunk(0, 0, post=False, norm=False)
            chunk(1, 1, norm=False)
            chunk(2, 0)
            chunk(3, 1)
            with dve.Fori(0, G * NC // 2 - 3) as i:
                chunk(i * 2 + 4, 0)
                chunk(i * 2 + 5, 1)
            chunk(G * NC - 2, 0)
            chunk(G * NC - 1, 1, pre=False)
            attention_norm(G * NC - 2)
            normalize(G * NC - 1, 1, XB, xn2[:, :])
            skip_connection(G * NC - 1)
            attention_norm(G * NC - 1)

            dve.wait_ge(conv["stored"], 32 * G * NC)
            dve.memset(xr[32:64, :], 0.0).then_inc(s_vec, 1)
            dve.wait_ge(s_vec, VS_STAGE0 + 1)
            dve.memset(xr[32:33, :], 1.0)
            for p in range(2):
                dve.memset(vf[p][:, NT - 1, :], 0.0)
                last = dve.memset(k2[p][96:97, :], 1.0)
            last.then_inc(s_clear2, 1)
            def consume(b, p, kind, n, j, done):
                bank = JB[j % len(JB)]
                if kind == "proj":
                    dst, m = (q2[p], "lo_q") if n < NK else (k2[p], "lo_k")
                    cols = slice(KN * (n % NK), KN * (n % NK) + KN)
                    dve.wait_ge(att["hi"], b * (2 * NK) + n + 1)
                    dve.scalar_tensor_tensor(dst[0:96, cols], hi[0:96, n % 4, :], cv(m, 96), ps[0:96, bank, 0:KN],
                                             ALU.mult, ALU.add).then_inc(att["ring"], 1)
                elif kind == "value":
                    dve.wait_ge(att["vcopy"], b * NV + n + 1)
                    k = min(7, NT - 7 * n)
                    if n == NV - 1:
                        k -= 1
                        dve.tensor_copy(res[p][0:TL, NT - 1, :], ps[0:TL, bank, 2 * C * k + C:2 * C * (k + 1)])
                    dve.tensor_copy(res[p][:, 7 * n:7 * n + k, :],
                                    ps[:, bank, 0:2 * C * k].rearrange("p (t n) -> p t n", n=2 * C)[:, :, C:2 * C])\
                       .then_inc(att["ring"], 1)
                else:
                    t, m = n // NK, n % NK
                    c = t // 4
                    rows, i = tile_rows(t), t % 4
                    dve.wait_ge(att["score1"], b * FP + n + 1)
                    dve.tensor_reduce(mxp[0:rows, t % 5, m:m + 1], ps[0:rows, bank, 0:KN], AX_X, ALU.max)\
                       .then_inc(att["ring"], 1)
                    if m == NK - 1:
                        dve.wait_ge(att["ring"], done)
                        at_ = 4 * ((NQ * p + c) % 2) + i
                        dve.tensor_reduce(mq[0:rows, at_:at_ + 1], mxp[0:rows, t % 5, 0:NK], AX_X, ALU.max)\
                           .then_inc(att["maxall"], 1)

            def weighted(b, p, c):
                k, rows = len(chunk_tiles(c)), tile_rows(4 * c)
                i = (NQ * p + c) % 2
                o4 = ps[0:rows, 6, 0:(C + 1) * k].rearrange("p (t n) -> p t n", n=C + 1)
                dve.wait_ge(att["out"], b * NQ + c + 1)
                if not (isinstance(b, int) and b == 0 and c < 2):
                    dve.wait_ge(att["tok"], b * NQ + c - 1)
                dve.reciprocal(rden[0:rows, 0:k], o4[:, :, C]).then_inc(att["rden"], 1)
                dve.wait_ge(att["rden"], b * NQ + c + 1)
                rd = rden[0:rows, 0:k].rearrange("p (t o) -> p t o", o=1).broadcast_to([rows, k, C])
                dve.tensor_tensor(oa[0:rows, i, 0:k, :], o4[:, :, 0:C], rd, ALU.mult).then_inc(att["o"], 1)

            def center_slot(b, part):
                k = 0 if isinstance(b, int) and b == B else b
                tb = tok[:, bass.ds(k, 1), :, :].rearrange("p o t c -> p (o t) c")
                if part == 0:
                    if not (isinstance(b, int) and b == 0):
                        dve.wait_ge(att["tok"], b * NQ)
                        dve.wait_ge(att["xf"], b)
                    dve.tensor_reduce(lnv[:, 0, :], tb, AX_X, ALU.add).then_inc(att["ln"], 1)
                elif part == 1:
                    dve.wait_ge(att["ln"], b * 5 + 1)
                    dve.tensor_scalar(lnv[:, 1, :], lnv[:, 0, :], 1.0 / C, None, ALU.mult).then_inc(att["ln"], 1)
                elif part == 2:
                    dve.wait_ge(att["ln"], b * 5 + 2)
                    dve.tensor_tensor(lnc[:, :, :], tb, lnv[:, 1, :].rearrange("p (t o) -> p t o", o=1)
                                      .broadcast_to([128, NT, C]), ALU.subtract).then_inc(att["ln"], 1)
                elif part == 3:
                    dve.wait_ge(att["ln"], b * 5 + 3)
                    dve.tensor_tensor(lnq[:, :, :], lnc[:, :, :], lnc[:, :, :], ALU.mult).then_inc(att["ln"], 1)
                elif part == 4:
                    dve.wait_ge(att["ln"], b * 5 + 4)
                    dve.tensor_reduce(lnv[:, 2, :], lnq[:, :, :], AX_X, ALU.add).then_inc(att["ss"], 1)
                else:
                    dve.wait_ge(att["ss"], b + 1)
                    dve.tensor_scalar(lnv[:, 3, :], lnv[:, 2, :], 1.0 / C, 1e-5, ALU.mult, ALU.add)\
                       .then_inc(att["ln"], 1)

            def image_steps(b, p, first=False, last=False):
                for x in range(NSTEP):
                    for c, late in chunks_at(over_at, x):
                        if not (late and first):
                            weighted(b - late, (p + late) % 2, c)
                    for j, ahead, kind, n in jobs_at(x, last):
                        consume(b + ahead, (p + ahead) % 2, kind, n, j, b * NJ + len(lead) + j + 1)
                    if LN_AT <= x < LN_AT + 12 and (x - LN_AT) % 2 == 0:
                        center_slot(b, (x - LN_AT) // 2)

            for j, (kind, n) in enumerate(lead):
                consume(0, 0, kind, n, j, j + 1)
            image_steps(0, 0, first=True)
            with dve.Fori(0, B // 2 - 1) as i:
                image_steps(i * 2 + 1, 1)
                image_steps(i * 2 + 2, 0)
            image_steps(B - 1, 1, last=True)
            for x in range(LAG + 3):
                for c, late in chunks_at(over_at, x):
                    if late:
                        weighted(B - 1, 1, c)
            for part in range(6):
                center_slot(B, part)

            dve.wait_ge(att["xf"], B + 1)
            dve.memset(pooled[C:C + 1, :, :], 1.0)
            mstep = [0]

            def mwait(ins):
                mstep[0] += 1
                ins.then_inc(moe["mk"], 1)
                dve.wait_ge(moe["mk"], mstep[0])

            for h in range(B // PB):
                for gg in range(2):
                    for n in range(0, NX, 2):
                        dve.wait_ge(moe["xft"], NX * (2 * h + gg) + n + 1)
                        dve.tensor_copy(xft[:, QC * n:QC * n + chunk_cols(n)], ps[:, n, 0:chunk_cols(n)])\
                           .then_inc(moe["xftc_v"], 1)
                dve.wait_ge(moe["logitc"], 2 * NK * (h + 1))
                dve.max(m8[:, :], lg[:, :]).then_inc(moe["top"], 1)
                dve.wait_ge(moe["top"], 2 * h + 1)
                dve.tensor_scalar(st[:, 0:1], m8[:, 0:1], -1.0, None, ALU.mult).then_inc(moe["top"], 1)
                mwait(dve.match_replace(mk[:, :], m8[:, :], lg[:, :], NEG))
                mwait(dve.tensor_tensor(mk[:, :], lg[:, :], mk[:, :], ALU.not_equal))
                dve.wait_ge(moe["exp"], h + 1)
                mwait(dve.reciprocal(st[:, 2:3], st[:, 1:2]))
                mwait(dve.scalar_tensor_tensor(mk[:, :], pe_[:, :], st[:, 2:3], mk[:, :], ALU.mult, ALU.mult))
                for n in range(0, NX, 2):
                    dve.wait_ge(moe["mt"], NX * h + n + 1)
                    k = len(chunk_tiles(n))
                    rows = tile_rows(4 * n)
                    dve.tensor_copy(mt[0:rows, 4 * n:4 * n + k, :].rearrange("p t n -> p (t n)"), ps[0:rows, n, 0:128 * k])\
                       .then_inc(moe["mtc_v"], 1)
                dve.wait_ge(moe["pool"], h + 1)
                for b in range(PB):
                    j, gg = b % GB, b // GB
                    last = dve.tensor_copy(pooled[0:C, :, b], ps[C * j:C * j + C, 7, 64 * gg + E * j:64 * gg + E * j + E])
                last.then_inc(moe["poolc"], 1)
                dve.wait_ge(moe["out"], h + 1)
                dve.tensor_copy(eo[:, :].rearrange("p (b e) -> p e b", b=PB),
                                ps[0:C, 1, 0:E * PB].rearrange("p (e b) -> p e b", e=E)).then_inc(moe["outc"], 1)
                dve.wait_ge(moe["outt"], h + 1)
                dve.tensor_tensor(bdo[:, :].rearrange("p (b c) -> p b c", b=PB), bcast(ps[:, 2, 0:C], PB),
                                  cv("blk8").rearrange("p (b o) -> p b o", o=1).broadcast_to([128, PB, C]), ALU.mult)\
                   .then_inc(moe["bdo"], 1)
                for t in range(NT):
                    rows = tile_rows(t)
                    dve.wait_ge(moe["scat"], NT * h + t + 1)
                    v = tok[0:rows, PB * h:PB * (h + 1), t, :]
                    dve.tensor_tensor(v, v, ps[0:rows, 3 + t % 4, 0:PB * C].rearrange("p (b c) -> p b c", b=PB), ALU.add)\
                       .then_inc(moe["add"], 1)

        @block.tensor
        def _(pe):
            def ident(n):
                return cv("ident", n)[:, 0:n]

            pe.wait_ge(s_cst, 16)
            for g in range(G):
                pe.wait_ge(s_xorder, g + 1)
                for n in range(NK):
                    if g:
                        pe.wait_ge(s_xe, NK * (g - 1) + n + 1)
                    for j in range(4):
                        k = 4 * n + j
                        last = pe.transpose(ps[:, n, PI * j:PI * (j + 1)], xin2[:, g % 2, k].rearrange("p b c -> p (b c)"), ident(PI))
                    last.then_inc(s_xt, 1)

            pe.wait_ge(s_vec, VS_REP)
            for i in range(4):
                pe.transpose(ps[:, 4, C * i:C * (i + 1)], wsmall[0:C, i, :, :].rearrange("p j c -> p (j c)"), ident(C))
            pe.transpose(ps[:, 4, 128:128 + E], wsmall[0:E, 4, :, :].rearrange("p j c -> p (j c)"), ident(E))
            pe.transpose(ps[:, 5, 0:128], w1raw[:, :, :].rearrange("p j c -> p (j c)"), ident(128))
            pe.transpose(ps[:, 6, 0:C], w2raw[:, :], ident(C)).then_inc(s_wt, 1)
            pe.wait_ge(s_vec, VS_FOLD)
            for i in range(3):
                pe.matmul(ps[:, 4, i:i + 1], wbd[:, i, :], pv[:, B1N:B1N + 1], start=True, stop=True)
            pe.matmul(ps[:, 5, 0:1], w1t[0:C, :], pv[0:C, B2N:B2N + 1], start=True, stop=True).then_inc(s_wb, 1)
            pe.wait_ge(s_vec, VS_BV)
            pe.matmul(ps[:, 5, 8:9 + C], cv("vmix", C + 1), wvb[:, :], start=True, stop=True)
            pe.matmul(ps[:, 4, 3:4], wp[:, 256:384], bv[:, BV:BV + 1], start=True, stop=False)
            pe.matmul(ps[:, 4, 3:4], cv("center"), pv[:, OB:OB + 1], start=False, stop=True).then_inc(s_wb, 1)
            pe.wait_ge(s_vec, VS_STAGE0)
            pe.wait_ge(s_clear, 5)

            def variance(n, k):
                pe.wait_ge(ln[k]["square"], n + 1)
                pe.matmul(ps[:, ZB, 0:CT], cv("mean"), sq[:, :], start=True, stop=True).then_inc(ln[k]["var"], 1)

            def scores(v, u):
                if not (isinstance(v, int) and v == 0):
                    pe.wait_ge(conv["bias"], v)
                for hf in range(2):
                    w = slice(L * (2 * u + hf), L * (2 * u + hf + 1))
                    for j in range(GB):
                        last = pe.matmul(ps[64 * hf:64 * hf + L, j // 2, NH * L * (j % 2):NH * L * (j % 2 + 1)],
                                         qz[:, j, w], kz[:, :, w], start=True, stop=True)
                last.then_inc(conv["score"], 1)

            def values(v, u, p):
                if not (isinstance(v, int) and v < 2):
                    pe.wait_ge(conv["oc"], v - 1)
                elif v == 1:
                    pe.wait_ge(conv["vcopy"], 1)
                for hf in range(2):
                    w = slice(L * (2 * u + hf), L * (2 * u + hf + 1))
                    for hh in range(2):
                        last = pe.matmul(ps[64 * hh:64 * hh + L, VB_, 128 * hf:128 * hf + 128], xn[:, p, w],
                                         wp[:, 384:512], start=True, stop=True)
                last.then_inc(conv["vprod"], 1)

            def transposes(v, u):
                i = u % 2
                pe.wait_ge(conv["prob"], v + 1)
                for k in range(2):
                    if not (isinstance(v, int) and v == 0):
                        pe.wait_ge(conv[("pcopy_a", "pcopy_b")[k]], v)
                    for n in range(4):
                        m = 4 * k + n
                        last = pe.transpose(ps[:, PT_ + k, 128 * n:128 * n + 113], pr[0:113, i, 128 * m:128 * m + 128],
                                            ident(113))
                    last.then_inc(conv["ptrans"], 1)

            def weighted_values(v, u, more):
                i = u % 2
                pe.wait_ge(conv["pcopy_a"], v + 1)
                pe.wait_ge(conv["pcopy_b"], v + 1)
                pe.wait_ge(conv["vcopy"], v + 1 + more)
                for hf in range(2):
                    for pair in range(2):
                        for j in range(GB):
                            w = 2 * (u % 2) + hf
                            s_ = 256 * hf + 64 * j + C * pair
                            q = 113 * (2 * j + pair) + 64 * hf
                            last = pe.matmul(ps[C * j:C * (j + 1), VB_, 2 * GB * C + L * w:2 * GB * C + L * (w + 1)],
                                             vs[0:113, i, s_:s_ + C], pt[0:113, i, q:q + L], start=(pair == 0),
                                             stop=(pair == 1), skip_group_check=True)
                last.then_inc(conv["av"], 1)

            def out_projection(n):
                pe.wait_ge(conv["oc"], n * NU + NU)
                pe.matmul(ps[:, XB, 0:CT], wp[:, 256:384], oc[:, :], start=True, stop=True).then_inc(ln[1]["center"], 1)

            def hidden(n, j):
                pe.wait_ge(ln[1]["norm"], n + 1)
                if j in (1, 2):
                    pe.wait_ge(conv["gelu"], n * GB + j)
                pe.matmul(ps[:, (XB, XB, XB, YB)[j], 0:CT], w1f[:, j, :], xn2[:, :], start=True, stop=True)\
                  .then_inc(conv["hid"], 1)

            def mlp_out(n):
                for j in range(GB):
                    pe.wait_ge(conv["gelu"], n * GB + j + 1)
                    last = pe.matmul(ps[C * j:C * (j + 1), ZB, 0:CT], w2t[:, :], gh[:, j, :], start=True, stop=True)
                last.then_inc(conv["y"], 1)

            def center_window(n):
                pe.wait_ge(conv["xg"], n + 1)
                pe.matmul(ps[:, YB, 0:CT], cv("center"), xg[:, :], start=True, stop=True).then_inc(ln[0]["center"], 1)

            def center_sum(n):
                pe.wait_ge(conv["t1"], n + 1)
                pe.matmul(ps[:, YB, 0:CT], cv("center"), t1[:, :], start=True, stop=True).then_inc(ln[2]["center"], 1)

            def project(n, p):
                pe.wait_ge(ln[0]["norm"], n + 1)
                pe.matmul(ps[:, YB, 0:CT], wp[:, 0:128], xn[:, p, :], start=True, stop=True).then_inc(conv["qk"], 1)
                pe.matmul(ps[:, ZB, 0:CT], wp[:, 128:256], xn[:, p, :], start=True, stop=True).then_inc(conv["qk"], 1)

            def chunk(it, p, post=True, pre=True, norm=True):
                v, n = it * NU, it - 1
                if post:
                    out_projection(n)
                values(v + 1, 1, p)
                transposes(v, 0)
                if post:
                    if norm:
                        pe.wait_ge(ln[2]["std"], n)
                    variance(n, 1)
                scores(v + 2, 2)
                if pre:
                    if norm:
                        pe.wait_ge(ln[2]["norm"], n)
                    center_window(it + 1)
                weighted_values(v, 0, 1)
                if pre:
                    if post:
                        pe.wait_ge(ln[1]["std"], n + 1)
                    variance(it + 1, 0)
                values(v + 2, 2, p)
                transposes(v + 1, 1)
                if post:
                    hidden(n, 0)
                scores(v + 3, 3)
                weighted_values(v + 1, 1, 1)
                if pre:
                    project(it + 1, 1 - p)
                if post:
                    hidden(n, 1)
                values(v + 3, 3, p)
                transposes(v + 2, 2)
                if post:
                    hidden(n, 2)
                weighted_values(v + 2, 2, 1)
                if pre:
                    pe.wait_ge(conv["qz"], it + 2)
                    pe.wait_ge(conv["kz"], it + 2)
                    scores(v + 4, 0)
                elif norm:
                    pe.wait_ge(ln[2]["norm"], n)
                if post:
                    hidden(n, 3)
                    mlp_out(n)
                if pre:
                    values(v + 4, 0, 1 - p)
                if post:
                    center_sum(n)
                transposes(v + 3, 3)
                if post:
                    variance(n, 2)
                if pre:
                    scores(v + 5, 1)
                weighted_values(v + 3, 3, int(pre))

            center_window(0)
            variance(0, 0)
            project(0, 0)
            pe.wait_ge(conv["qz"], 1)
            pe.wait_ge(conv["kz"], 1)
            scores(0, 0)
            values(0, 0, 0)
            scores(1, 1)
            chunk(0, 0, post=False, norm=False)
            chunk(1, 1, norm=False)
            with pe.Fori(0, G * NC // 2 - 2) as i:
                chunk(i * 2 + 2, 0)
                chunk(i * 2 + 3, 1)
            chunk(G * NC - 2, 0)
            chunk(G * NC - 1, 1, pre=False)
            n = G * NC - 1
            out_projection(n)
            pe.wait_ge(ln[2]["std"], n)
            variance(n, 1)
            for j in range(GB):
                if j == 3:
                    pe.wait_ge(ln[2]["norm"], n)
                hidden(n, j)
            mlp_out(n)
            center_sum(n)
            variance(n, 2)
            pe.wait_ge(ln[2]["norm"], G * NC)

            def produce(b, p, kind, n, j, done):
                bank = JB[j % len(JB)]
                if not (isinstance(done, int) and done <= 0):
                    pe.wait_ge(att["ring"], done)
                if kind == "proj":
                    if n == 0:
                        pe.wait_ge(att["load"], b * 32 + 32)
                    w = wqr if n < NK else wkr
                    pe.matmul(ps[0:96, bank, 0:KN], w[:, :, :].rearrange("p r c -> p (r c)"),
                              xr[:, KN * (n % NK):KN * (n % NK) + KN], start=True, stop=True).then_inc(att["prod"], 1)
                elif kind == "value":
                    for t in range(7 * n, min(7 * n + 7, NT)):
                        rows = tile_rows(t)
                        last = pe.matmul(ps[0:rows, bank, 2 * C * (t % 7):2 * C * (t % 7 + 1)], xr[:, T * t:T * t + rows],
                                         wva[:, :], start=True, stop=True)
                    last.then_inc(att["vprod"], 1)
                else:
                    t, m = n // NK, n % NK
                    rows = tile_rows(t)
                    pe.matmul(ps[0:rows, bank, 0:KN], q2[p][0:96, T * t:T * t + rows], k2[p][0:96, KN * m:KN * m + KN],
                              start=True, stop=True).then_inc(att["score1"], 1)

            def max_row(b, p, c, w, done=0):
                pe.wait_ge(att["maxall"], b * NT + chunk_tiles(c)[-1] + 1)
                if not (isinstance(done, int) and done <= 0):
                    pe.wait_ge(att["exp"], done)
                for t in chunk_tiles(c):
                    rows, i = tile_rows(t), t % 4
                    at_ = 4 * ((NQ * p + c) % 2) + i
                    last = pe.matmul(ps[96:97, w % SB, T * i:T * i + rows], mq[:, at_:at_ + 1], cv("negident")[:, 0:rows],
                                     start=True, stop=True)
                last.then_inc(att["mrow"], 1)

            def second_pass(b, p, x, last_image):
                c, tiles, _ = steps2[x]
                n = chunk_cols(c)
                if x == first_of[c]:
                    pe.wait_ge(att["exp"], b * NUNIT + 2 + row_unit[c] if c else
                               1 if isinstance(b, int) and b == 0 else b * NUNIT + 2 + row_unit[NQ] - NUNIT)
                for w, m, rows, n, mine in units[x]:
                    k = place_of(w, last_image)
                    bank, done = turn(k, 1 if isinstance(b, int) and b == 0 else NUNIT, SB)
                    if not (isinstance(b, int) and 1 + b * NUNIT + done <= 0):
                        pe.wait_ge(att["exp"], 1 + b * NUNIT + done)
                    for t, at_ in mine:
                        rows = tile_rows(t)
                        last = pe.matmul(ps[0:rows, bank, at_ % QC:at_ % QC + chunk_cols(c)],
                                         k2[p][0:97, T * t:T * t + rows], q2[p][0:97, QC * c:QC * c + chunk_cols(c)],
                                         start=True, stop=True)
                        if t == mine[-1][0]:
                            last.then_inc(att["score2"], 1)
                        yield t

            def key_sums(b, p, x, last_image=False):
                c, tiles, _ = steps2[x]
                n = chunk_cols(c)
                pe.wait_ge(att["exp"], 1 + b * NUNIT + place_of(units[x][-1][0], last_image) + 1)
                if x == first_of[c] and not (isinstance(b, int) and b == 0 and c == 0):
                    pe.wait_ge(att["o"], b * NQ + c)
                for t, at_ in tiles:
                    parts = 4 if t == NT - 1 and n == QC else 1
                    w = n // parts
                    for h in range(parts):
                        g = h if parts > 1 else t % 4
                        last = pe.matmul(ps[C * g:C * (g + 1), 6, w * h:w * h + w], vf[p][:, t, :],
                                         pk[:, x % DEPTH, at_ + w * h:at_ + w * h + w],
                                         start=(t < 4), stop=(t >= NT - 4), skip_group_check=True)
                last.then_inc(att["av"], 1)

            def out_values(b, c):
                pe.wait_ge(att["acopy"], b * NQ + c + 1)
                for q in chunk_tiles(c):
                    rows, i = tile_rows(q), q % 4
                    last = pe.matmul(ps[0:rows, 6, (C + 1) * i:(C + 1) * (i + 1)], ua[:, T * i:T * i + rows], wvo[:, :],
                                     start=True, stop=True)
                last.then_inc(att["out"], 1)

            def step_rest(b, p, x, first, last):
                for c, late in chunks_at(out_at, x):
                    if not (late and first):
                        out_values(b - late, c)
                for y in sums_at(x):
                    if y >= 0:
                        key_sums(b, p, y, last)
                    elif not first:
                        key_sums(b - 1, 1 - p, y + NSTEP)

            def image_steps(b, p, first=False, last=False):
                for x in range(NSTEP):
                    scores = second_pass(b, p, x, last)
                    next(scores)
                    for j, ahead, kind, n in jobs_at(x, last):
                        done = turn(j, len(lead) if isinstance(b, int) and b == 0 else NJ, len(JB))[1]
                        produce(b + ahead, (p + ahead) % 2, kind, n, j, b * NJ + len(lead) + done)
                        next(scores, None)
                    for _ in scores:
                        pass
                    if x in turn_at and not (last and turn_at[x] == NQ):
                        c = turn_at[x]
                        bank, done = turn(row_unit[c], 1 if isinstance(b, int) and b == 0 else NUNIT, SB)
                        if c == NQ:
                            max_row(b + 1, 1 - p, 0, bank, 1 + b * NUNIT + done)
                        else:
                            max_row(b, p, c, bank, 1 + b * NUNIT + done)
                    step_rest(b, p, x, first, last)

            pe.wait_ge(s_clear2, 1)
            for j, (kind, n) in enumerate(lead):
                produce(0, 0, kind, n, j, j - len(JB) + 1)
            max_row(0, 0, 0, 0)
            image_steps(0, 0, first=True)
            with pe.Fori(0, B // 2 - 1) as i:
                image_steps(i * 2 + 1, 1)
                image_steps(i * 2 + 2, 0)
            image_steps(B - 1, 1, last=True)
            for x in range(LAG + 2):
                for c, late in chunks_at(out_at, x):
                    if late:
                        out_values(B - 1, c)
                for y in sums_at(x):
                    if y < 0:
                        key_sums(B - 1, 1, y + NSTEP, True)

            pe.wait_ge(att["xf"], B + 1)
            for h in range(B // PB):
                for gg in range(2):
                    g = 2 * h + gg
                    if g == 2:
                        pe.wait_ge(moe["add"], NT)
                    for n in range(NX):
                        if gg:
                            pe.wait_ge(moe["xftc_v"], 4 * g)
                            pe.wait_ge(moe["xftc_a"], 3 * g)
                            pe.wait_ge(moe["logitc"], NK * g)
                        for t in chunk_tiles(n):
                            rows = tile_rows(t)
                            last = pe.transpose(ps[:, n, T * (t % 4):T * (t % 4) + rows], xf[0:rows, t, GB * g:GB * g + GB, :].rearrange("p b c -> p (b c)"),
                                                ident(rows))
                        last.then_inc(moe["xft"], 1)
                    pe.wait_ge(moe["xftc_v"], 4 * (g + 1))
                    pe.wait_ge(moe["xftc_a"], 3 * (g + 1))
                    for n in range(NK):
                        pe.matmul(ps[64 * gg:64 * gg + 64, n, 0:KN], wgate[:, :, :].rearrange("p j e -> p (j e)"),
                                  xft[:, KN * n:KN * n + KN], start=True, stop=True).then_inc(moe["logit"], 1)
                pe.wait_ge(moe["mk"], 4 * (h + 1))
                for n in range(NX):
                    for t in chunk_tiles(n):
                        rows = tile_rows(t)
                        last = pe.transpose(ps[0:rows, n, 128 * (t % 4):128 * (t % 4) + 128], mk[:, T * t:T * t + rows],
                                            ident(128))
                    last.then_inc(moe["mt"], 1)
                pe.wait_ge(moe["mtc_v"], 4 * (h + 1))
                pe.wait_ge(moe["mtc_a"], 3 * (h + 1))
                pe.wait_ge(moe["logitc"], 2 * NK * (h + 1))
                for gg in range(2):
                    g = 2 * h + gg
                    for t in range(NT):
                        rows = tile_rows(t)
                        last = pe.matmul(ps[:, 7, 64 * gg:64 * gg + 64], xf[0:rows, t, GB * g:GB * g + GB, :].rearrange("p b c -> p (b c)"),
                                         mt[0:rows, t, 64 * gg:64 * gg + 64], start=(t == 0), stop=(t == NT - 1))
                last.then_inc(moe["pool"], 1)
                pe.wait_ge(moe["poolc"], h + 1)
                pe.wait_ge(moe["weights"], 48)
                for e in range(E):
                    last = pe.matmul(ps[:, 0, PB * e:PB * (e + 1)], w1e[:, e, :], pooled[:, e, :], start=True, stop=True)
                last.then_inc(moe["hid"], 1)
                pe.wait_ge(moe["gelu"], h + 1)
                for e in range(E):
                    o = ps[0:C, 1, PB * e:PB * (e + 1)]
                    pe.matmul(o, w2e[:, e, :], eh[:, PB * e:PB * (e + 1)], start=True, stop=False)
                    last = pe.matmul(o, w2b[:, e, :], cv("one", 1), start=False, stop=True)
                last.then_inc(moe["out"], 1)
                pe.wait_ge(moe["outc"], h + 1)
                pe.transpose(ps[:, 2, 0:C], eo[:, :], ident(C)).then_inc(moe["outt"], 1)
                pe.wait_ge(moe["bdo"], h + 1)
                for t in range(NT):
                    rows = tile_rows(t)
                    if t >= 4:
                        pe.wait_ge(moe["add"], NT * h + t - 3)
                    pe.matmul(ps[0:rows, 3 + t % 4, 0:PB * C], mk[:, T * t:T * t + rows], bdo[:, :], start=True, stop=True)\
                      .then_inc(moe["scat"], 1)


_INS = ["x", "L0_conv_norm1_g", "L0_conv_norm1_b", "L0_conv_qkv_w", "L0_conv_qkv_b", "L0_conv_out_w", "L0_conv_out_b",
        "L0_conv_pe_table", "L0_conv_norm2_g", "L0_conv_norm2_b", "L0_conv_mlp_w1", "L0_conv_mlp_b1", "L0_conv_mlp_w2",
        "L0_conv_mlp_b2", "L1_attn_Wq", "L1_attn_bq", "L1_attn_Wk", "L1_attn_bk", "L1_attn_Wv", "L1_attn_bv",
        "L1_ffn_gate_w", "L1_ffn_gate_b", "L1_ffn_weight1", "L1_ffn_weight2"]


def kernel(**inputs):
    import concourse.bacc as _bacc
    from concourse.bass_utils import run_bass_kernel_spmd as _run

    nc = _bacc.Bacc("TRN2", target_bir_lowering=False, num_devices=1)
    arrays, args = {}, {}
    for name in _INS:
        v = np.ascontiguousarray(inputs[name])
        arrays[f"in_{name}"] = v
        args[name] = nc.dram_tensor(f"in_{name}", v.shape, mybir.dt.from_np(v.dtype), kind="ExternalInput").ap()
    arrays["constants"] = shape_constants()
    cst = nc.dram_tensor("constants", (128, NCONST), F32, kind="ExternalInput").ap()
    out = nc.dram_tensor("result", (B, H, W, C), F32, kind="ExternalOutput").ap()
    conv_attention_moe(nc, args, cst, out)
    r = _run(nc, [arrays], core_ids=[0])
    return r.results[0]["result"]
```
